# Optimizing a Trainium2 kernel written in Bass

```python
import numpy as np
import jax
import jax.numpy as jnp

def _softmax(x, axis=-1):
    return jax.nn.softmax(x, axis=axis)
def _gelu(x):
    return jax.nn.gelu(x, approximate=True)
def _silu(x):
    return jax.nn.silu(x)
def _sigmoid(x):
    return jax.nn.sigmoid(x)
def _layernorm(x, axis=-1, eps=1e-5):
    m = jnp.mean(x, axis=axis, keepdims=True)
    v = jnp.var(x, axis=axis, keepdims=True)
    return (x - m) / jnp.sqrt(v + eps)
def _scatter_add(tgt, idx, src, axis=0):
    return tgt.at[idx].add(src)
def _segment_sum(src, seg, n):
    return jax.ops.segment_sum(src, seg, n)

kernel_name = 'mk_conv_preact_d2_conv_nchw256_c6212d'

def setup_inputs(seed: int = 0):
    np.random.seed(seed)
    _w = jnp.asarray
    def _rec_inputs():
        import jax
        import jax.numpy as jnp
        _gk = jax.random.key(seed)
        x = 7.22e-05 + 1 * jax.random.normal(jax.random.fold_in(_gk, 1), (8, 256, 64, 64), jnp.float32)
        return x
    x = _rec_inputs()
    def _L0_conv_setup():
        import jax, jax.numpy as jnp
        import numpy as np
        HEADS = 8
        DIM_KEY = 64
        REL_LEN = 7
        BN_EPS = 1e-05

        def _rel_proj(l, rel):
            diff = jnp.arange(l)[None, :] - jnp.arange(l)[:, None]
            valid = (diff >= 0) & (diff < REL_LEN)
            gathered = rel[jnp.clip(diff, 0, REL_LEN - 1)]
            return jnp.where(valid[..., None], gathered, 0.0)
        key = jax.random.key(seed)
        ks = jax.random.split(key, 6)
        b, c, x, y = (8, 256, 64, 64)
        dim_hidden = DIM_KEY * HEADS
        return {'img': jax.random.normal(ks[0], (b, c, x, y), dtype=jnp.float32), 'w_qkv': jax.random.normal(ks[1], (3 * dim_hidden, c), dtype=jnp.float32) * 0.02, 'w_out': jax.random.normal(ks[2], (256, dim_hidden), dtype=jnp.float32) * 0.02, 'b_out': jax.random.normal(ks[3], (256,), dtype=jnp.float32) * 0.02, 'bn_gamma': jnp.ones((DIM_KEY,), dtype=jnp.float32), 'bn_beta': jnp.zeros((DIM_KEY,), dtype=jnp.float32), 'rel_rows': jax.random.normal(ks[4], (REL_LEN, DIM_KEY), dtype=jnp.float32), 'rel_columns': jax.random.normal(ks[5], (REL_LEN, DIM_KEY), dtype=jnp.float32)}
    _L0_conv_all = _L0_conv_setup()
    _L0_conv_in = {k: v for k, v in _L0_conv_all.items() if k in ('w_qkv', 'w_out', 'b_out', 'bn_gamma', 'bn_beta', 'rel_rows', 'rel_columns', )}
    del _L0_conv_all

    def _L1_conv_setup():
        import jax, jax.numpy as jnp
        import numpy as np
        GRID = (256, 256, 32)
        NUM_CLASSES = 21
        MIN_B = np.array([-25.6, -25.6, -2.0], np.float32)
        MAX_B = np.array([25.6, 25.6, 1.2], np.float32)
        VOX = (MAX_B - MIN_B) / np.array(GRID, np.float32)
        FS = 3
        PRIOR = 0.001
        N_PTS = 1000000

        def _forward(current_map, point_cloud, weights):
            min_b = jnp.asarray(MIN_B)
            max_b = jnp.asarray(MAX_B)
            vox = jnp.asarray(VOX)
            maxes = jnp.asarray(np.array(GRID, np.int32) - 1)
            xyz = point_cloud[:, :3]
            labels = point_cloud[:, 3].astype(jnp.int32)
            valid = jnp.all((xyz < max_b) & (xyz >= min_b), axis=1)
            inds = jnp.floor((xyz - min_b) / vox).astype(jnp.int32)
            inds = jnp.clip(inds, 0, maxes)
            labels = jnp.clip(labels, 0, NUM_CLASSES - 1)
            update = jnp.zeros_like(current_map).at[inds[:, 0], inds[:, 1], inds[:, 2], labels].add(valid.astype(current_map.dtype))
            mid = FS // 2
            filt = jax.nn.sigmoid(weights).at[0, 0, mid, mid, mid].set(1.0)
            x = jnp.transpose(update, (3, 0, 1, 2))[:, None]
            y = jax.lax.conv_general_dilated(x, filt, window_strides=(1, 1, 1), padding='SAME', dimension_numbers=('NCDHW', 'OIDHW', 'NCDHW'))
            new_update = jnp.transpose(y[:, 0], (1, 2, 3, 0))
            return current_map + new_update
        key = jax.random.key(seed)
        k1, k2, k3, k4 = jax.random.split(key, 4)
        current_map = PRIOR + 0.1 * jax.random.uniform(k1, (*GRID, NUM_CLASSES), dtype=jnp.float32)
        lo = jnp.asarray(MIN_B) - 1.0
        hi = jnp.asarray(MAX_B) + 1.0
        xyz = lo + (hi - lo) * jax.random.uniform(k2, (N_PTS, 3), dtype=jnp.float32)
        labels = jax.random.randint(k3, (N_PTS, 1), 0, NUM_CLASSES).astype(jnp.float32)
        point_cloud = jnp.concatenate([xyz, labels], axis=1)
        weights = 0.1 * jax.random.normal(k4, (1, 1, FS, FS, FS), dtype=jnp.float32)
        mid = FS // 2
        weights = weights.at[0, 0, mid, mid, mid].set(1.0)
        return {'current_map': current_map, 'point_cloud': point_cloud, 'weights': weights}
    _L1_conv_all = _L1_conv_setup()
    _L1_conv_in = {k: v for k, v in _L1_conv_all.items() if k in ('point_cloud', 'weights', )}
    del _L1_conv_all

    return {
        "x": x,
        "L0_conv_w_qkv": _L0_conv_in["w_qkv"],
        "L0_conv_w_out": _L0_conv_in["w_out"],
        "L0_conv_b_out": _L0_conv_in["b_out"],
        "L0_conv_bn_gamma": _L0_conv_in["bn_gamma"],
        "L0_conv_bn_beta": _L0_conv_in["bn_beta"],
        "L0_conv_rel_rows": _L0_conv_in["rel_rows"],
        "L0_conv_rel_columns": _L0_conv_in["rel_columns"],
        "L1_conv_point_cloud": _L1_conv_in["point_cloud"],
        "L1_conv_weights": _L1_conv_in["weights"],
    }

def reference(x, L0_conv_w_qkv, L0_conv_w_out, L0_conv_b_out, L0_conv_bn_gamma, L0_conv_bn_beta, L0_conv_rel_rows, L0_conv_rel_columns, L1_conv_point_cloud, L1_conv_weights):
    import jax
    import jax.numpy as jnp
    def _L0_conv_ref(img, w_qkv, w_out, b_out, bn_gamma, bn_beta, rel_rows, rel_columns):
        import jax, jax.numpy as jnp
        import numpy as np
        HEADS = 8
        DIM_KEY = 64
        REL_LEN = 7
        BN_EPS = 1e-05

        def _rel_proj(l, rel):
            diff = jnp.arange(l)[None, :] - jnp.arange(l)[:, None]
            valid = (diff >= 0) & (diff < REL_LEN)
            gathered = rel[jnp.clip(diff, 0, REL_LEN - 1)]
            return jnp.where(valid[..., None], gathered, 0.0)
        b, c, x, y = img.shape
        h, dk = (HEADS, DIM_KEY)
        qkv = jnp.einsum('oc,bcxy->boxy', w_qkv, img)
        q, k, v = jnp.split(qkv, 3, axis=1)
        q, k, v = (t.reshape(b * h, dk, x, y) for t in (q, k, v))
        k = jax.nn.softmax(k, axis=-1)
        context = jnp.einsum('ndxy,nexy->nde', k, v)
        content_out = jnp.einsum('nde,ndxy->nexy', context, q)
        Px = _rel_proj(x, rel_rows)
        Sx = jnp.einsum('ndxy,xid->nixy', q, Px)
        Yh = jnp.einsum('nixy,neiy->nexy', Sx, v)
        mean = Yh.mean(axis=(0, 2, 3), keepdims=True)
        var = Yh.var(axis=(0, 2, 3), keepdims=True)
        Yh = (Yh - mean) * jax.lax.rsqrt(var + BN_EPS)
        Yh = Yh * bn_gamma[None, :, None, None] + bn_beta[None, :, None, None]
        Py = _rel_proj(y, rel_columns)
        Sy = jnp.einsum('ndxy,xid->nixy', q, Py)
        rel_pos_out = jnp.einsum('nixy,neiy->nexy', Sy, Yh)
        content_out = content_out + rel_pos_out
        content_out = content_out.reshape(b, h * dk, x, y)
        return jnp.einsum('oc,bcxy->boxy', w_out, content_out) + b_out[None, :, None, None]

    def _L1_conv_ref(current_map, point_cloud, weights):
        import jax, jax.numpy as jnp
        import numpy as np
        GRID = (256, 256, 32)
        NUM_CLASSES = 21
        MIN_B = np.array([-25.6, -25.6, -2.0], np.float32)
        MAX_B = np.array([25.6, 25.6, 1.2], np.float32)
        VOX = (MAX_B - MIN_B) / np.array(GRID, np.float32)
        FS = 3
        PRIOR = 0.001
        N_PTS = 1000000

        def _forward(current_map, point_cloud, weights):
            min_b = jnp.asarray(MIN_B)
            max_b = jnp.asarray(MAX_B)
            vox = jnp.asarray(VOX)
            maxes = jnp.asarray(np.array(GRID, np.int32) - 1)
            xyz = point_cloud[:, :3]
            labels = point_cloud[:, 3].astype(jnp.int32)
            valid = jnp.all((xyz < max_b) & (xyz >= min_b), axis=1)
            inds = jnp.floor((xyz - min_b) / vox).astype(jnp.int32)
            inds = jnp.clip(inds, 0, maxes)
            labels = jnp.clip(labels, 0, NUM_CLASSES - 1)
            update = jnp.zeros_like(current_map).at[inds[:, 0], inds[:, 1], inds[:, 2], labels].add(valid.astype(current_map.dtype))
            mid = FS // 2
            filt = jax.nn.sigmoid(weights).at[0, 0, mid, mid, mid].set(1.0)
            x = jnp.transpose(update, (3, 0, 1, 2))[:, None]
            y = jax.lax.conv_general_dilated(x, filt, window_strides=(1, 1, 1), padding='SAME', dimension_numbers=('NCDHW', 'OIDHW', 'NCDHW'))
            new_update = jnp.transpose(y[:, 0], (1, 2, 3, 0))
            return current_map + new_update
        return _forward(current_map, point_cloud, weights)

    def _gn(v, G=32, eps=1e-5):
        B_, C_, H_, W_ = v.shape
        g = v.reshape(B_, G, C_ // G, H_, W_)
        m = jnp.mean(g, axis=(2, 3, 4), keepdims=True)
        s = jnp.var(g, axis=(2, 3, 4), keepdims=True)
        return ((g - m) / jnp.sqrt(s + eps)).reshape(v.shape)

    def _ln_c(v, eps=1e-6):
        m = jnp.mean(v, axis=1, keepdims=True)
        s = jnp.var(v, axis=1, keepdims=True)
        return (v - m) / jnp.sqrt(s + eps)

    def _ln_t(v, eps=1e-5):
        m = jnp.mean(v, axis=-1, keepdims=True)
        s = jnp.var(v, axis=-1, keepdims=True)
        return (v - m) / jnp.sqrt(s + eps)

    def _to_tokens(v):
        B_, C_, H_, W_ = v.shape
        return v.reshape(B_, C_, H_ * W_).transpose(0, 2, 1)
    def _from_tokens(t, like):
        B_, C_, H_, W_ = like.shape
        return t.transpose(0, 2, 1).reshape(B_, C_, H_, W_)

    x = x + _L0_conv_ref(_gn(x), L0_conv_w_qkv, L0_conv_w_out, L0_conv_b_out, L0_conv_bn_gamma, L0_conv_bn_beta, L0_conv_rel_rows, L0_conv_rel_columns)
    x = x + _L1_conv_ref(_gn(x), L1_conv_point_cloud, L1_conv_weights)
    return x


_drawn_inputs = setup_inputs


def setup_inputs(seed=0):
    import zlib

    import numpy as np

    out = dict(_drawn_inputs(seed))
    spreads = {'L0_conv_bn_gamma': (1.0, 0.2), 'L0_conv_bn_beta': (0.0, 0.1)}
    factors = {'L0_conv_b_out': 8.0, 'L1_conv_weights': 101.516}
    for name, (base, spread) in spreads.items():
        noise = np.random.default_rng([zlib.crc32(name.encode()), seed]).standard_normal(out[name].shape)
        drawn = base * np.exp(spread * noise) if base else spread * noise
        out[name] = jnp.asarray(drawn.astype(out[name].dtype))
    for name, factor in factors.items():
        out[name] = (out[name] * factor).astype(out[name].dtype)
    return out
```

```python
import numpy as np
import concourse.bass as bass
from concourse import mybir
from contextlib import ExitStack

IMAGES, CHANNELS, SIDE = 8, 256, 64
HEADS, DK, REL = 8, 64, 7
PIX = SIDE * SIDE
CT = CHANNELS // 128
PAIRS = HEADS // 2
YL = SIDE // 2
NS = 2 * REL * HEADS
EDGE = REL - 1
GROUP = 8
PARTS = 3
TAPS = 2 * REL - 1
SROWS = 2 * PARTS * REL
GENK = SROWS + 2 * PARTS * TAPS
STRIP = 3 * SIDE - 1
BN_EPS, GN_EPS = 1e-5, 1e-5

POINTS = 1000000
PROWS = 125
PCOLS = POINTS // PROWS
NCHUNK = IMAGES * PAIRS
CHUNK = PCOLS // NCHUNK
TOP = 24
NX, NY, NZ, NL = 8, 256, 32, 21
ZL = NZ * NL
BLOCK = 128 * ZL
BLOCKS = NX * 2
SET = 40
OHG = 8
MAGIC = 1.5 * 2.0 ** 23
ZSLOT = NZ + 3
HROW = ZSLOT * NL
ZA = 17


def constants():
    c = {}
    p = np.arange(128)
    c["group_mean"] = (p[:, None] // GROUP == p[None] // GROUP).astype(np.float32) / GROUP
    c["swap_half"] = (p[:, None] == (p[None] + 64) % 128).astype(np.float32)
    c["both_halves"] = (p[:, None] % 64 == p[None] % 64).astype(np.float32)
    s = np.arange(NS)
    kind, r, head = s // (REL * HEADS), s // HEADS % REL, s % HEADS
    hm = np.zeros((128, PAIRS, NS), np.float32)
    for q in range(PAIRS):
        hm[:, q] = head[None] == 2 * q + p[:, None] // 64
    c["head_mask"] = hm.reshape(128, -1)
    c["head_mask_cols"] = (hm * (kind == 1)).reshape(128, -1).astype(np.float32)
    c["bad_mask"] = ((kind[:, None] == 1) & (r[:, None] + SIDE - EDGE + np.arange(EDGE)[None] >= SIDE)).astype(np.float32)
    c["good_mask"] = (r[:, None] + SIDE - EDGE + np.arange(EDGE)[None] < SIDE).astype(np.float32)
    d = np.zeros((GENK, 2, STRIP), np.float32)
    for y2 in range(2):
        for part in range(PARTS):
            for kind, (row0, taps) in enumerate(((0, REL), (PARTS * 2 * REL, TAPS))):
                for j in range(taps):
                    d[row0 + (y2 * PARTS + part) * taps + j, kind, SIDE - 1 + SIDE * y2 + j] = 1
    c["strip"] = d.reshape(GENK, 2 * STRIP)
    sh = np.stack([(p[:, None] == p[None] + b - 1) for b in range(3)], 1).astype(np.float32)
    c["shift"] = sh.reshape(128, 3 * 128)
    cr = np.zeros((128, 2, 128), np.float32)
    cr[0, 0, 127] = 1
    cr[127, 1, 0] = 1
    c["cross"] = cr.reshape(128, 256)
    lo = np.arange(BLOCKS) * BLOCK + 1.0
    c["block_lo"] = np.tile(lo[None], (128, 1)).astype(np.float32)
    c["block_hi"] = np.tile(lo[None] + BLOCK, (128, 1)).astype(np.float32)
    c["index"] = np.tile(np.arange(ZL)[None], (128, 1)).astype(np.float32)
    return c


def build(nc, t, out):
    fp32, bf16, fp16, i32 = mybir.dt.float32, mybir.dt.bfloat16, mybir.dt.float16, mybir.dt.int32
    ALU, ACT, AX = mybir.AluOpType, mybir.ActivationFunctionType, mybir.AxisListType
    ds = bass.ds
    VY = np.float32(51.2) / np.float32(256)

    s_dram = nc.dram_tensor("s_scratch", [IMAGES, NS, PIX], fp32, kind="Internal").ap()
    sp_dram = nc.dram_tensor("sp_scratch", [IMAGES, PARTS, REL, HEADS, PIX], bf16, kind="Internal").ap()
    tp_dram = nc.dram_tensor("tp_scratch", [IMAGES, PARTS, TAPS, HEADS, PIX], bf16, kind="Internal").ap()
    bad_dram = nc.dram_tensor("bad_scratch", [IMAGES, NS, SIDE * EDGE], fp32, kind="Internal").ap()
    a_dram = nc.dram_tensor("a_scratch", [IMAGES, 128, CT * CHANNELS], fp32, kind="Internal").ap()
    p_dram = nc.dram_tensor("p_scratch", [IMAGES, PAIRS, 128, PIX], fp32, kind="Internal").ap()
    keys_dram = nc.dram_tensor("keys_scratch", [PROWS, 2 * BLOCKS * SET + PCOLS], fp32, kind="Internal").ap()
    cand_dram = nc.dram_tensor("cand_scratch", [PROWS, NCHUNK * TOP], fp32, kind="Internal").ap()
    pc_dram = t["points"].rearrange("(p k) c -> p (k c)", p=PROWS)
    x_dram = t["x"].rearrange("b (t p) h w -> b p t (h w)", p=128)
    out_dram = out.rearrange("b (t p) h w -> b p t (h w)", p=128)

    top = ExitStack()
    with top:
        def sb(stack, name, shape, dt=fp32):
            return stack.enter_context(nc.sbuf_tensor(name, shape, dt))

        front = top.enter_context(ExitStack())
        setup = top.enter_context(ExitStack())

        def sem(name):
            return top.enter_context(nc.semaphore(name))

        group_mean = sb(top, "group_mean", [128, 128])
        both_halves = sb(top, "both_halves", [128, 128])
        wout = sb(top, "wout", [128, PAIRS, CHANNELS])
        g_t = sb(top, "g_t", [128, CT, NS])
        g_n = sb(top, "g_n", [NS, CHANNELS])
        affine = sb(top, "affine", [128, IMAGES, CT, 2])
        ustat = sb(top, "ustat", [128, NCHUNK, 2])
        block_lo = sb(top, "block_lo", [128, BLOCKS])
        block_hi = sb(top, "block_hi", [128, BLOCKS])
        gamma = sb(top, "gamma", [128, 1])
        beta = sb(top, "beta", [128, 1])
        b_out = sb(top, "b_out", [128, CT])

        swap_half = sb(front, "swap_half", [128, 128])
        wq = sb(front, "wq", [128, PAIRS, CHANNELS])
        head_mask = sb(setup, "head_mask", [128, PAIRS, NS])
        relbd = sb(setup, "relbd", [128, PAIRS, NS])
        reld = sb(setup, "reld", [128, 2 * REL])

        PJ = top.enter_context(nc.psum_tensor("PJ", [128, 2, 512], fp32))
        GN = top.enter_context(nc.psum_tensor("GN", [128, 2, 512], fp32))
        ST = top.enter_context(nc.psum_tensor("ST", [128, 2, 512], fp32))
        CX = top.enter_context(nc.psum_tensor("CX", [128, 512], fp32))
        MS = top.enter_context(nc.psum_tensor("MS", [128, 512], fp32))

        setup_in = sem("setup_in")
        relbd_ready = sem("relbd_ready")
        g_ready = sem("g_ready")
        g_copied = sem("g_copied")
        with nc.Block() as block:
            @block.sync
            def _(sp):
                n = 0
                for dst, src in (
                        (group_mean[:], t["group_mean"]), (swap_half[:], t["swap_half"]),
                        (both_halves[:], t["both_halves"]),
                        (wq[:], t["w_q"].rearrange("(q p) c -> p q c", p=128)),
                        (wout[:], t["w_out_t"].rearrange("(q p) c -> p q c", p=128)),
                        (head_mask[:].rearrange("p q s -> p (q s)"), t["head_mask"]),
                        (reld[0:64, :], t["rel_t"]), (reld[64:128, :], t["rel_t"]),
                        (block_lo[:], t["block_lo"]), (block_hi[:], t["block_hi"]),
                        (gamma[0:64, :], t["gamma"]), (gamma[64:128, :], t["gamma"]),
                        (beta[0:64, :], t["beta"]), (beta[64:128, :], t["beta"]),
                        (b_out[:], t["b_out"])):
                    sp.dma_start(dst, src).then_inc(setup_in, 16)
                    n += 16
                assert n == 15 * 16

            @block.vector
            def _(dve):
                dve.wait_ge(setup_in, 15 * 16)
                for q in range(PAIRS):
                    nc.vector.tensor_tensor(
                        relbd[:, q, :].rearrange("p (k n) -> p k n", n=HEADS),
                        head_mask[:, q, :].rearrange("p (k n) -> p k n", n=HEADS),
                        reld[:].unsqueeze(2).to_broadcast([128, 2 * REL, HEADS]), ALU.mult).then_inc(relbd_ready, 1)
                dve.wait_ge(g_ready, 3)
                nc.vector.tensor_copy(g_n[:], CX[0:NS, 0:CHANNELS]).then_inc(g_copied, 1)
                nc.vector.tensor_copy(g_t[:, 0, :], MS[:, 0:NS]).then_inc(g_copied, 1)
                nc.vector.tensor_copy(g_t[:, 1, :], ST[:, 0, 0:NS]).then_inc(g_copied, 1)
                dve.wait_ge(g_copied, 3)

            @block.tensor
            def _(pe):
                pe.wait_ge(setup_in, 15 * 16)
                pe.wait_ge(relbd_ready, PAIRS)
                for dst, lhs, rhs in ((CX[0:NS, 0:CHANNELS], lambda q: relbd[:, q, :], lambda q: wq[:, q, :]),
                                      (MS[:, 0:NS], lambda q: wq[:, q, 0:128], lambda q: relbd[:, q, :]),
                                      (ST[:, 0, 0:NS], lambda q: wq[:, q, 128:256], lambda q: relbd[:, q, :])):
                    for q in range(PAIRS):
                        last = nc.tensor.matmul(dst, lhs(q), rhs(q), start=(q == 0), stop=(q == PAIRS - 1))
                    last.then_inc(g_ready, 1)

        setup.close()
        pass1(nc, t, locals())
        front.close()
        histogram_and_pass2(nc, t, locals())


def pass1(nc, t, e):
    fp32, bf16 = mybir.dt.float32, mybir.dt.bfloat16
    ALU, ACT, AX = mybir.AluOpType, mybir.ActivationFunctionType, mybir.AxisListType
    ds = bass.ds
    sb, sem = e["sb"], e["sem"]
    PJ, GN, ST, CX, MS = e["PJ"], e["GN"], e["ST"], e["CX"], e["MS"]
    wq, wout, g_t, affine, ustat = (e[k] for k in ("wq", "wout", "g_t", "affine", "ustat"))
    group_mean, swap_half, both_halves = e["group_mean"], e["swap_half"], e["both_halves"]
    s_dram, sp_dram, tp_dram, bad_dram, a_dram, p_dram, keys_dram = (
        e[k] for k in ("s_dram", "sp_dram", "tp_dram", "bad_dram", "a_dram", "p_dram", "keys_dram"))
    pc_dram, x_dram, cand_dram = e["pc_dram"], e["x_dram"], e["cand_dram"]
    VY = e["VY"]
    HY = YL // 2
    NST = 8
    SLOTS = 4

    with ExitStack() as own:
        xr = sb(own, "xr", [128, CT, PIX])
        xn = sb(own, "xn", [128, CT, PIX])
        kv = sb(own, "kv", [128, YL, 256])
        band = [sb(own, "band0", [128, HY, 2, 2, SIDE]), sb(own, "band1", [128, HY, 2, 2, SIDE])]
        ptile = sb(own, "ptile", [128, SLOTS, 512])
        srow = sb(own, "srow", [GENK, 2, 2, YL, SIDE], bf16)
        wkv = sb(own, "wkv", [128, CT, PAIRS, 256])
        strip = sb(own, "strip", [GENK, 2, STRIP], bf16)
        bad_mask = sb(own, "bad_mask", [NS, EDGE])
        good_mask = sb(own, "good_mask", [NS, EDGE])
        tt = sb(own, "tt", [128, TAPS, 4, SIDE])
        sbad = sb(own, "sbad", [NS, SIDE, EDGE])
        bnst = sb(own, "bnst", [128, CT, 8, 6])
        ybn = sb(own, "ybn", [128, 16, 6])
        mvy = sb(own, "mvy", [128, 2])
        mv = sb(own, "mv", [128, CT, 2])
        tmp2 = sb(own, "tmp2", [128, CT])
        tmp3 = sb(own, "tmp3", [128, CT])
        mxq = sb(own, "mxq", [128, 4, 128])
        mx = sb(own, "mx", [128, 128])
        mxx = sb(own, "mxx", [128, 128])
        rz = sb(own, "rz", [128, 128])
        ctxbd = sb(own, "ctxbd", [128, 128])
        fmat = sb(own, "fmat", [128, CHANNELS])
        amat = sb(own, "amat", [128, CT * CHANNELS])
        pc = sb(own, "pc", [PROWS, CHUNK, 4])
        ptb = sb(own, "pt", [128, 6, CHUNK])
        pt = ptb[0:PROWS]
        top24 = sb(own, "top24", [PROWS, TOP])

        flat = xr[:].rearrange("p c f -> p (c f)")
        QW = 4 * SIDE
        stile = flat[0:NS, 0:PIX].rearrange("p (a l x) -> p a l x", a=2, x=SIDE)
        sy = flat[:, 2 * PIX - 2 * REL * QW:].rearrange("p (k l x) -> p k l x", l=4, x=SIDE)
        RS = PARTS * REL * QW // 2
        s_parts = flat[:, 0:RS].bitcast(bf16).rearrange("p (a f) -> p a f", a=PARTS)
        s_rest = flat[:, RS:RS + REL * QW]
        TW = TAPS * QW // 2
        t_at = [2 * PIX - 2 * REL * QW, 2 * PIX - 2 * REL * QW + TW, RS]
        t_parts = [flat[:, o:o + TW].bitcast(bf16) for o in t_at]
        prod = [ptb[:].rearrange("p k c -> p (k c)")[:, 0:REL * QW // 2].rearrange("p (k l x) -> p k l x", l=2, x=SIDE),
                ptile[:].rearrange("p k c -> p (k c)")[:, 0:REL * QW // 2].rearrange("p (k l x) -> p k l x", l=2, x=SIDE)]

        counted = ("x_in bn_done mvp_ready gstat_mm var_ready std_ready xn_ready s_mm s_act s_dve s_out bad_out "
                   "s_cast s_sub t_sum_dve t_sum_pool t_cast sp_out tp_out s_back0 s_back1 t_back0 t_back1 pj_mm kv_evac gen_mm gen_act gen_dve "
                   "y_mm y_stat p_mm p_act p_dve p_out0 p_out1 p_out2 p_out3 "
                   "max_ready swap_mm shift_ready sub_done exp_done zsum_ready zsum_mm rz_ready norm_done ctx_mm ctx_copied "
                   "f_mm f_copied a_mm a_copied a_out pts_in key_ready key_out top_ready top_out unit_read dve_step pool_step").split()
        S = {n: sem(n) for n in counted + ["w_in", "sy_in", "zeroed", "strip_ready", "apart", "pool_apart", "credited"]}
        starts_at_one = [S[n] for n in counted]
        G = type("Sems", (), S)
        p_out = [G.p_out0, G.p_out1, G.p_out2, G.p_out3]
        s_back, t_back = [G.s_back0, G.s_back1], [G.t_back0, G.t_back1]

        def per(img, each, n):
            return img * each + n + 1

        with nc.Block() as block:
            @block.sync
            def _(sp):
                for s in starts_at_one:
                    sp.sem_inc(s, 1)
                sp.sem_inc(G.credited, 1)
                sp.wait_ge(G.credited, 1)

        ORDER = {False: ("s0", "s1", "y0", "t0", "y1", "t1", "p0", "p1"),
                 True: ("s0", "s1", "y0", "y1", "t0", "t1", "p0", "p1")}
        JOB = ("s0", "s1", "t0", "t1")
        GNR = [GN[:, 0, :], GN[:, 1, :], PJ[:, 0, :]]
        STR = [ST[:, 0, :], ST[:, 1, :], PJ[:, 1, :]]
        MAX_CUT = (0, 12, 22, 30, 32)
        CAST_AT = (0, 2, 4)
        SUM_AT = (0, 2, 4, 6)
        ZSUM_AT = 9
        DVE_STEPS = 197

        def free_band(eng, img, q, job):
            if job[0] == "s":
                eng.wait_ge(G.p_mm, per(img, 64, 16 * q))
            else:
                eng.wait_ge(G.y_mm, per(img, 64, 16 * q + 8 * int(job[1]) + 8))

        with nc.Block() as block:
            @block.sync
            def _(sp):
                sp.dma_start(wkv[:], t["w_kv_t"].rearrange("(t p) q f -> p t q f", p=128)).then_inc(G.w_in, 16)
                sp.dma_start(band[0][0:GENK].rearrange("p l n a x -> p (l n a x)")[:, 0:2 * STRIP], t["strip"]).then_inc(G.w_in, 16)
                sp.dma_start(bad_mask[:], t["bad_mask"]).then_inc(G.w_in, 16)
                sp.dma_start(good_mask[:], t["good_mask"]).then_inc(G.w_in, 16)
                sp.wait_ge(G.zeroed, 3)

                def load_image(img):
                    for c in range(CT):
                        sp.dma_start(xr[:, c, :], x_dram[ds(img, 1), :, c, :].rearrange("b p f -> (b p) f")).then_inc(G.x_in, 16)

                def load_rows(img, q, kind, half):
                    dram, rows, row0 = ((sp_dram, PARTS * REL, 0), (tp_dram, PARTS * TAPS, SROWS))[kind]
                    for y2 in range(2):
                        at = y2 * (PIX // 2) + half * (PIX // 4)
                        src = dram[ds(img, 1), :, :, 2 * q:2 * q + 2, at:at + PIX // 4].rearrange("b a k n f -> (b a k) n f")
                        sp.dma_start(srow[row0 + rows * y2:row0 + rows * (y2 + 1), :, y2, HY * half:HY * (half + 1), :]
                                     .rearrange("p n l x -> p n (l x)"), src).then_inc((s_back, t_back)[kind][half], 16)

                def s_out(img):
                    for h in range(2):
                        sp.wait_ge(G.s_act, per(img, NST, 4 * h + 4))
                        sp.wait_ge(G.s_dve, per(img, NST, 4 * h + 4))
                        sp.dma_start(s_dram[ds(img, 1), :, :].rearrange("b s (a l f) -> (b s) a l f", a=2, l=2)[:, :, h, :],
                                     stile[:, :, HY * h:HY * (h + 1), :].rearrange("p a l x -> p a (l x)")).then_inc(G.s_out, 16)
                    sp.dma_start(bad_dram[ds(img, 1), :, :].rearrange("b s f -> (b s) f"),
                                 sbad[:].rearrange("p y x -> p (y x)")).then_inc(G.bad_out, 16)

                def keys_out(img, c):
                    sp.wait_ge(G.key_ready, per(img, PAIRS, c + 1))
                    sp.dma_start(keys_dram[:, ds((img * PAIRS + c) * CHUNK + BLOCKS * SET, CHUNK)],
                                 pt[:, 5, :]).then_inc(G.key_out, 16)
                    sp.wait_ge(G.top_ready, per(img, PAIRS, c + 1))
                    sp.dma_start(cand_dram[:, ds((img * PAIRS + c) * TOP, TOP)], top24[:]).then_inc(G.top_out, 16)

                def points_in(img, c):
                    sp.wait_ge(G.unit_read, per(img, PAIRS, c))
                    sp.dma_start(pc[:].rearrange("p k c -> p (k c)"),
                                 pc_dram[:, ds((img * PAIRS + c) * (4 * CHUNK), 4 * CHUNK)]).then_inc(G.pts_in, 16)

                def image(img, last):
                    for a in range(PARTS):
                        sp.wait_ge(G.s_cast, per(img, PARTS, a + 1))
                        sp.dma_start(sp_dram[ds(img, 1), a, :, :, :].rearrange("b k n (c f) -> (b n c) k f", c=16),
                                     s_parts[:, a, :].rearrange("p (k f) -> p k f", k=REL)).then_inc(G.sp_out, 16)
                    sp.wait_ge(G.sp_out, per(img, 48, 48))
                    sp.wait_ge(G.gen_mm, per(img, 128, 0))
                    for h in range(2):
                        load_rows(img, 0, 0, h)
                    for a in range(PARTS):
                        sp.wait_ge(G.t_cast, per(img, PARTS, a + 1))
                        sp.dma_start(tp_dram[ds(img, 1), a, :, :, :].rearrange("b k n (c f) -> (b n c) k f", c=16),
                                     t_parts[a].rearrange("p (k f) -> p k f", k=TAPS)).then_inc(G.tp_out, 16)
                    sp.wait_ge(G.tp_out, per(img, 48, 48))
                    for h in range(2):
                        load_rows(img, 0, 1, h)
                    if not last:
                        load_image(img + 1)
                    for q in range(PAIRS):
                        if q == 0:
                            points_in(img, 0)
                        if q == 2:
                            points_in(img, 3)
                            keys_out(img, 2)
                        for h in range(2):
                            if q + 1 < PAIRS:
                                sp.wait_ge(G.gen_mm, per(img, 128, 32 * q + 8 * (JOB.index("t0") + h + 1)))
                                load_rows(img, q + 1, 0, h)
                                load_rows(img, q + 1, 1, h)
                        if q == PAIRS - 1 and not last:
                            s_out(img + 1)
                        for k in range(8):
                            m = 8 * q + k
                            sp.wait_ge(G.p_act, per(img, 64, 2 * m + 2))
                            sp.wait_ge(G.p_dve, per(img, 64, 2 * m + 2))
                            sp.dma_start(p_dram[ds(img, 1), q, :, 512 * k:512 * (k + 1)].rearrange("b p f -> (b p) f"),
                                         ptile[:, m % SLOTS, :]).then_inc(p_out[m % SLOTS], 16)
                        if q < 2:
                            points_in(img, q + 1)
                        if q < 3:
                            keys_out(img, (0, 1, 3)[q])
                    sp.wait_ge(G.a_copied, per(img, PAIRS, PAIRS))
                    sp.dma_start(a_dram[ds(img, 1), :, :].rearrange("b p f -> (b p) f"), amat[:]).then_inc(G.a_out, 16)

                load_image(0)
                s_out(0)
                with sp.Fori(0, IMAGES - 1) as img:
                    image(img, False)
                image(IMAGES - 1, True)
                for done, each in ((G.a_out, 16), (G.bad_out, 16), (G.key_out, 16 * PAIRS), (G.top_out, 16 * PAIRS),
                                   *((p, 8 * 16) for p in p_out)):
                    sp.wait_ge(done, per(IMAGES, each, 0))

            @block.gpsimd
            def _(pool):
                steps = [0]
                TSTEPS = 12

                def link(ins, img):
                    steps[0] += 1
                    ins.then_inc(G.pool_step, 1)
                    pool.wait_ge(G.pool_step, per(img, TSTEPS, steps[0]))

                nc.gpsimd.memset(srow[:, 0, :, :, :], 0.0).then_inc(G.zeroed, 1)
                nc.gpsimd.memset(srow[:, 1, :, :, :], 0.0).then_inc(G.zeroed, 1)
                nc.gpsimd.memset(ctxbd[:], 0.0).then_inc(G.zeroed, 1)

                def s_back_in(idx):
                    pool.wait_ge(G.s_out, per(idx, 32, 32))
                    for kind in range(2):
                        src = s_dram[ds(idx, 1), kind * REL * HEADS:(kind + 1) * REL * HEADS, :]
                        pool.dma_start(sy[:, REL * kind:REL * (kind + 1), :, :].rearrange("p k l x -> p k (l x)"),
                                       src.rearrange("b (k n) (c f) -> (b n c) k f", n=HEADS, c=16)).then_inc(G.sy_in, 16)

                def image(img, last):
                    steps[0] = 0
                    own_tt = tt[:, :, 2:4, :]
                    pool.wait_ge(G.sy_in, img * 32 + 32)
                    pool.wait_ge(G.tp_out, per(img, 48, 0))
                    pool.wait_ge(G.p_out0, per(img, 128, 0))
                    pool.wait_ge(G.p_out1, per(img, 128, 0))
                    pool.sem_inc(G.pool_apart, 1)
                    nc.gpsimd.memset(own_tt[:, REL:], 0.0)
                    link(nc.gpsimd.tensor_tensor(own_tt[:, 0:REL], sy[:, 0:REL, 2:4, :],
                                                 sy[:, REL, 2:4, :].unsqueeze(1).to_broadcast([128, REL, 2, SIDE]), ALU.mult), img)
                    for r2 in range(1, REL):
                        w = SIDE - r2
                        link(nc.gpsimd.tensor_tensor(prod[1][:, :, :, 0:w], sy[:, 0:REL, 2:4, r2:],
                                                     sy[:, REL + r2, 2:4, 0:w].unsqueeze(1).to_broadcast([128, REL, 2, w]), ALU.mult), img)
                        add = nc.gpsimd.tensor_tensor(own_tt[:, r2:r2 + REL, :, 0:w], own_tt[:, r2:r2 + REL, :, 0:w],
                                                      prod[1][:, :, :, 0:w], ALU.add)
                        if r2 < REL - 1:
                            link(add, img)
                        else:
                            add.then_inc(G.t_sum_pool, 1)
                    assert steps[0] == TSTEPS
                    for a in range(2):
                        pool.wait_ge(G.t_sum_pool, per(img, 3, a + 1))
                        pool.wait_ge(G.t_cast, per(img, PARTS, a + 1))
                        nc.gpsimd.tensor_tensor(own_tt, own_tt, t_parts[a].rearrange("p (k l x) -> p k l x", l=4, x=SIDE)[:, :, 2:4, :],
                                                ALU.subtract).then_inc(G.t_sum_pool, 1)
                    for q in range(PAIRS):
                        pool.wait_ge(G.shift_ready, per(img, PAIRS, q + 1))
                        for b in range(4):
                            k4 = kv[:, 8 * b:8 * b + 8, 0:128]
                            nc.gpsimd.tensor_tensor(k4, k4, mxx[:].unsqueeze(1).to_broadcast([128, 8, 128]),
                                                    ALU.subtract).then_inc(G.sub_done, 1)
                        if q == PAIRS - 1 and not last:
                            s_back_in(img + 1)
                        pool.wait_ge(G.rz_ready, per(img, PAIRS, q + 1))
                        for b in range(4):
                            k4 = kv[:, 8 * b:8 * b + 8, 0:128]
                            nc.gpsimd.tensor_tensor(k4, k4, rz[:].unsqueeze(1).to_broadcast([128, 8, 128]),
                                                    ALU.mult).then_inc(G.norm_done, 1)

                s_back_in(0)
                with pool.Fori(0, IMAGES - 1) as img:
                    image(img, False)
                image(IMAGES - 1, True)

            @block.scalar
            def _(act):
                act.wait_ge(G.w_in, 64)
                nc.scalar.activation(strip[:].rearrange("p k x -> p (k x)"),
                                     band[0][0:GENK].rearrange("p l n a x -> p (l n a x)")[:, 0:2 * STRIP], ACT.Copy).then_inc(G.strip_ready, 1)

                def root(idx):
                    act.wait_ge(G.var_ready, per(idx, 1, 1))
                    nc.scalar.activation(tmp3[:], tmp2[:], ACT.Sqrt).then_inc(G.std_ready, 1)

                def normalise(idx):
                    act.wait_ge(G.bn_done, per(idx, 1, 1))
                    nc.scalar.activation(xn[:, 1, :].rearrange("p (y x) -> p y x", x=SIDE),
                                         xr[:, 1, :].rearrange("p (x y) -> p y x", y=SIDE), ACT.Identity,
                                         bias=mv[:, 1, 1:2], scale=mv[:, 1, 0:1]).then_inc(G.xn_ready, 1)

                def gen_tiles(img, q, job):
                    free_band(act, img, q, job)
                    for k in range(1, 8, 2):
                        g = 8 * JOB.index(job) + k
                        act.wait_ge(G.gen_mm, per(img, 128, 32 * q + g + 1))
                        nc.scalar.activation(
                            band[int(job[1])][:, :, :, :, 8 * k:8 * k + 8].rearrange("p l n a x -> p (n a) l x"),
                            GNR[g % 3].rearrange("p (x m l) -> p m l x", x=8, l=HY), ACT.Copy).then_inc(G.gen_act, 1)

                def s_part(img, a):
                    if a == 0:
                        act.wait_ge(G.sy_in, img * 32 + 32)
                        src = sy[:, 0:REL, :, :].rearrange("p k l x -> p (k l x)")
                    else:
                        act.wait_ge(G.s_sub, per(img, 2, a))
                        src = s_rest
                    nc.scalar.activation(s_parts[:, a, :], src, ACT.Copy).then_inc(G.s_cast, 1)

                def t_part(img, a):
                    act.wait_ge(G.t_sum_dve, per(img, 3, a + 1))
                    act.wait_ge(G.t_sum_pool, per(img, 3, a + 1))
                    nc.scalar.activation(t_parts[a], tt[:].rearrange("p k l x -> p (k l x)"), ACT.Copy).then_inc(G.t_cast, 1)

                def exps(img, q, bs):
                    for b in bs:
                        act.wait_ge(G.sub_done, per(img, 16, 4 * q + b + 1))
                        nc.scalar.activation(kv[:, 8 * b:8 * b + 8, 0:128], kv[:, 8 * b:8 * b + 8, 0:128],
                                             ACT.Exp).then_inc(G.exp_done, 1)

                def s_tiles(img):
                    for k in range(NST):
                        act.wait_ge(G.s_mm, per(img, NST, k + 1))
                        nc.scalar.activation(stile[:, :, 4 * k:4 * k + 4, :].rearrange("p a l x -> p l a x"),
                                             ST[0:NS, k % 2, :].rearrange("p (l a x) -> p l a x", l=4, a=2),
                                             ACT.Copy).then_inc(G.s_act, 1)

                def image(img, last):
                    for q in range(PAIRS):
                        act.wait_ge(G.ctx_mm, per(img, PAIRS, q))
                        for k in range(16):
                            act.wait_ge(G.pj_mm, per(img, 64, 16 * q + k + 1))
                            nc.scalar.activation(kv[:, 2 * k:2 * k + 2, :].rearrange("p l f -> p (l f)"),
                                                 PJ[:, k % 2, :], ACT.Copy).then_inc(G.kv_evac, 1)
                            if q == 0 and k in CAST_AT:
                                s_part(img, CAST_AT.index(k))
                            if q == PAIRS - 1 and k == 13 and not last:
                                root(img + 1)
                        done = 0
                        for job in ORDER[q == 0]:
                            if job in JOB:
                                gen_tiles(img, q, job)
                                if q == 0 and job in ("s0", "s1"):
                                    t_part(img, int(job[1]))
                                if q == PAIRS - 1 and job == "s1" and not last:
                                    act.wait_ge(G.pj_mm, per(img, 64, 64))
                                    normalise(img + 1)
                            elif job[0] == "y":
                                if q == 0 and job == "y0":
                                    t_part(img, 2)
                                exps(img, q, (2 * int(job[1]), 2 * int(job[1]) + 1))
                                if q == PAIRS - 1 and job == "y1" and not last:
                                    s_tiles(img + 1)
                            else:
                                for k in range(8):
                                    n = 8 * int(job[1]) + k
                                    m = 8 * q + n // 2
                                    act.wait_ge(G.p_mm, per(img, 64, 16 * q + n + 1))
                                    act.wait_ge(p_out[m % SLOTS], per(img, 128, 16 * (m // SLOTS)))
                                    nc.scalar.activation(ptile[0:64, m % SLOTS, 256 * (n % 2):256 * (n % 2) + 256],
                                                         STR[(16 + n) % 3][0:64, 0:256], ACT.Copy).then_inc(G.p_act, 1)

                root(0)
                normalise(0)
                s_tiles(0)
                with act.Fori(0, IMAGES - 1) as img:
                    image(img, False)
                image(IMAGES - 1, True)

            @block.tensor
            def _(pe):
                pe.wait_ge(G.w_in, 64)
                pe.wait_ge(G.strip_ready, 1)
                pe.wait_ge(G.zeroed, 3)

                def moments(idx):
                    pe.wait_ge(G.mvp_ready, per(idx, 1, 1))
                    nc.tensor.matmul(MS[:, 0:2 * CT], group_mean[:], mv[:].rearrange("p t k -> p (t k)"),
                                     start=True, stop=True).then_inc(G.gstat_mm, 1)

                def gen(img, q, job):
                    half, rank = int(job[1]), JOB.index(job)
                    kind = 0 if job[0] == "s" else 1
                    K = SROWS if kind == 0 else GENK
                    pe.wait_ge(s_back[half], per(img, 32 * PAIRS, 32 * (q + 1)))
                    if kind == 1:
                        pe.wait_ge(t_back[half], per(img, 32 * PAIRS, 32 * (q + 1)))
                    for k in range(8):
                        g = 8 * rank + k
                        if g >= 3:
                            pe.wait_ge(G.gen_act if (g - 3) % 2 else G.gen_dve, per(img, 64, 16 * q + (g - 3) // 2 + 1))
                        elif g == 2:
                            pe.wait_ge(G.kv_evac, per(img, 64, 16 * q + 16))
                        for j in range(8):
                            x = 8 * k + j
                            last = nc.tensor.matmul(
                                GNR[g % 3][:, 64 * j:64 * j + 64],
                                strip[0:K, kind, SIDE - 1 - x:3 * SIDE - 1 - x],
                                srow[0:K, :, :, HY * half:HY * (half + 1), x].rearrange("p n a l -> p (n a) l"), start=True, stop=True)
                        last.then_inc(G.gen_mm, 1)

                def band_stands(img, q, job):
                    pe.wait_ge(G.gen_act, per(img, 64, 16 * q + 4 * JOB.index(job) + 4))
                    pe.wait_ge(G.gen_dve, per(img, 64, 16 * q + 4 * JOB.index(job) + 4))

                def stage(u, half, k):
                    for j in range(2):
                        yl = 2 * k + j
                        last = nc.tensor.matmul(
                            STR[u % 3].rearrange("p (n l f) -> p l n f", n=2, l=2)[:, j],
                            kv[:, HY * half + yl, 128:256],
                            band[half][:, yl, :, :, :].rearrange("p n a x -> p (n a x)"), start=True, stop=True)
                    return last

                def flush_f(img, q):
                    pe.wait_ge(G.ctx_copied, per(img, 2 * PAIRS, 2 * q + 2))
                    nc.tensor.matmul(MS[:, 256:512], ctxbd[:], wout[:, q, :], start=True, stop=True).then_inc(G.f_mm, 1)

                def flush_a(img, q):
                    pe.wait_ge(G.f_copied, per(img, PAIRS, q + 1))
                    for c in range(CT):
                        last = nc.tensor.matmul(CX[:, 256 * c:256 * c + 256], wq[:, q, 128 * c:128 * c + 128],
                                                fmat[:], start=True, stop=True)
                    last.then_inc(G.a_mm, 1)

                def s_tiles(idx):
                    pe.wait_ge(G.xn_ready, per(idx, CT, CT))
                    for k in range(NST):
                        if k >= 2:
                            pe.wait_ge(G.s_act, per(idx, NST, k - 1))
                        for c in range(CT):
                            last = nc.tensor.matmul(ST[0:NS, k % 2, :], g_t[:, c, :], xn[:, c, 512 * k:512 * k + 512],
                                                    start=(c == 0), stop=(c == CT - 1))
                        last.then_inc(G.s_mm, 1)

                def image(img, last_image):
                    for q in range(PAIRS):
                        for k in range(16):
                            if k == 0:
                                for left in (G.gen_act, G.gen_dve, G.p_act, G.p_dve):
                                    pe.wait_ge(left, per(img, 64, 16 * q))
                            elif k >= 2:
                                pe.wait_ge(G.kv_evac, per(img, 64, 16 * q + k - 1))
                            for j in range(2):
                                yl = 2 * k + j
                                for c in range(CT):
                                    last = nc.tensor.matmul(PJ[:, k % 2, 256 * j:256 * j + 256],
                                                            xn[:, c, 128 * yl:128 * yl + 128], wkv[:, c, q, :],
                                                            start=(c == 0), stop=(c == CT - 1))
                            last.then_inc(G.pj_mm, 1)
                            if q > 0 and k == 3:
                                flush_f(img, q - 1)
                            if q > 0 and k == 7:
                                flush_a(img, q - 1)
                            if q == PAIRS - 1 and k == 11 and not last_image:
                                moments(img + 1)
                        for job in ORDER[q == 0]:
                            half = int(job[1])
                            if job in JOB:
                                gen(img, q, job)
                                if job == "s0":
                                    pe.wait_ge(G.max_ready, per(img, PAIRS, q + 1))
                                    nc.tensor.matmul(MS[:, 0:128], swap_half[:], mx[:], start=True, stop=True).then_inc(G.swap_mm, 1)
                            elif job[0] == "y":
                                band_stands(img, q, "s%d" % half)
                                if half == 0:
                                    pe.wait_ge(G.kv_evac, per(img, 64, 16 * q + 16))
                                for k in range(8):
                                    n = 8 * half + k
                                    if n >= 3:
                                        pe.wait_ge(G.y_stat, per(img, 64, 16 * q + n - 2))
                                    elif q == 0:
                                        pe.wait_ge(G.s_act, per(img, NST, NST))
                                    stage(n, half, k).then_inc(G.y_mm, 1)
                                if q == PAIRS - 1 and half == 1 and not last_image:
                                    pe.wait_ge(G.y_stat, per(img, 64, 64))
                                    s_tiles(img + 1)
                            else:
                                band_stands(img, q, "t%d" % half)
                                for k in range(8):
                                    n = 8 * half + k
                                    if n >= 3:
                                        pe.wait_ge(G.p_act, per(img, 64, 16 * q + n - 2))
                                        pe.wait_ge(G.p_dve, per(img, 64, 16 * q + n - 2))
                                    else:
                                        pe.wait_ge(G.y_stat, per(img, 64, 16 * q + 14 + n))
                                        if q == PAIRS - 1 and n == 0 and not last_image:
                                            pe.wait_ge(G.s_act, per(img + 1, NST, NST))
                                    stage(16 + n, half, k).then_inc(G.p_mm, 1)
                                    if n == ZSUM_AT:
                                        pe.wait_ge(G.zsum_ready, per(img, PAIRS, q + 1))
                                        nc.tensor.matmul(MS[:, 128:256], both_halves[:], mx[:], start=True, stop=True).then_inc(G.zsum_mm, 1)
                        for yl in range(YL):
                            if yl % 8 == 0:
                                pe.wait_ge(G.norm_done, per(img, 16, 4 * q + yl // 8 + 1))
                                if yl == 0:
                                    pe.wait_ge(G.a_copied, per(img, PAIRS, q))
                            last = nc.tensor.matmul(CX[:, 0:128], kv[:, yl, 128:256], kv[:, yl, 0:128],
                                                    start=(yl == 0), stop=(yl == YL - 1))
                        last.then_inc(G.ctx_mm, 1)
                    flush_f(img, PAIRS - 1)
                    flush_a(img, PAIRS - 1)

                moments(0)
                s_tiles(0)
                with pe.Fori(0, IMAGES - 1) as img:
                    image(img, False)
                image(IMAGES - 1, True)

            @block.vector
            def _(dve):
                steps = [0]
                now = [0]
                first = [0]

                def link(ins):
                    steps[0] += 1
                    ins.then_inc(G.dve_step, 1)
                    dve.wait_ge(G.dve_step, per(now[0], DVE_STEPS, first[0] + steps[0]))

                def apart():
                    dve.sem_inc(G.apart, 1)

                def gen_tiles(img, q, job):
                    free_band(dve, img, q, job)
                    for k in range(0, 8, 2):
                        g = 8 * JOB.index(job) + k
                        dve.wait_ge(G.gen_mm, per(img, 128, 32 * q + g + 1))
                        nc.vector.tensor_copy(
                            band[int(job[1])][:, :, :, :, 8 * k:8 * k + 8].rearrange("p l n a x -> p (n a) l x"),
                            GNR[g % 3].rearrange("p (x m l) -> p m l x", x=8, l=HY)).then_inc(G.gen_dve, 1)

                def stats(idx):
                    dve.wait_ge(G.x_in, per(idx, 32, 32))
                    for c in range(CT):
                        for k in range(8):
                            apart()
                            last = nc.vector.bn_stats(bnst[:, c, k, :], xr[:, c, 512 * k:512 * k + 512])
                    link(last)
                    apart()
                    nc.vector.bn_aggr(mv[:, 0, :], bnst[:, 0, :, :].rearrange("p k s -> p (k s)"))
                    link(nc.vector.bn_aggr(mv[:, 1, :], bnst[:, 1, :, :].rearrange("p k s -> p (k s)")))
                    link(nc.vector.tensor_tensor(tmp2[:], mv[:, :, 0], mv[:, :, 0], ALU.mult))
                    link(nc.vector.tensor_tensor(mv[:, :, 1], mv[:, :, 1], tmp2[:], ALU.add))
                    nc.vector.sem_inc(G.mvp_ready, 1)

                def variance(idx):
                    dve.wait_ge(G.gstat_mm, per(idx, 1, 1))
                    link(nc.vector.tensor_copy(mv[:].rearrange("p t k -> p (t k)"), MS[:, 0:2 * CT]))
                    link(nc.vector.tensor_tensor(tmp2[:], mv[:, :, 0], mv[:, :, 0], ALU.mult))
                    link(nc.vector.tensor_tensor(tmp2[:], mv[:, :, 1], tmp2[:], ALU.subtract))
                    link(nc.vector.tensor_scalar(tmp2[:], tmp2[:], 0.0, GN_EPS, ALU.max, ALU.add))
                    nc.vector.sem_inc(G.var_ready, 1)

                def scale_bias(idx):
                    dve.wait_ge(G.std_ready, per(idx, 1, 1))
                    link(nc.vector.reciprocal(tmp3[:], tmp3[:]))
                    link(nc.vector.tensor_tensor(tmp2[:], mv[:, :, 0], tmp3[:], ALU.mult))
                    nc.vector.tensor_scalar(mv[:, :, 1], tmp2[:], -1.0, None, ALU.mult)
                    link(nc.vector.tensor_copy(mv[:, :, 0], tmp3[:]))
                    link(nc.vector.tensor_copy(affine[:, ds(idx, 1), :, :].rearrange("p b t k -> p (b t k)"),
                                               mv[:].rearrange("p t k -> p (t k)")))
                    nc.vector.sem_inc(G.bn_done, 1)

                def normalise():
                    nc.vector.tensor_scalar(xn[:, 0, :].rearrange("p (y x) -> p y x", x=SIDE),
                                            xr[:, 0, :].rearrange("p (x y) -> p y x", y=SIDE),
                                            mv[:, 0, 0:1], mv[:, 0, 1:2], ALU.mult, ALU.add).then_inc(G.xn_ready, 1)

                def s_edges(img):
                    dve.wait_ge(G.bad_out, per(img, 16, 0))
                    for k in range(NST):
                        dve.wait_ge(G.s_act, per(img, NST, k + 1))
                        edge = stile[:, :, 4 * k:4 * k + 4, SIDE - EDGE:].rearrange("p a l x -> p l a x")
                        link(nc.vector.tensor_tensor(
                            sbad[:, 8 * k:8 * k + 8, :].rearrange("p (l a) x -> p l a x", a=2), edge,
                            bad_mask[:].unsqueeze(1).unsqueeze(1).to_broadcast([NS, 4, 2, EDGE]), ALU.mult))
                        nc.vector.tensor_tensor(
                            edge, edge,
                            good_mask[:].unsqueeze(1).unsqueeze(1).to_broadcast([NS, 4, 2, EDGE]), ALU.mult).then_inc(G.s_dve, 1)

                def t_product(r2):
                    w = SIDE - r2
                    if r2 == 0:
                        nc.vector.memset(tt[:, REL:, 0:2, :], 0.0)
                        link(nc.vector.tensor_tensor(tt[:, 0:REL, 0:2, :], sy[:, 0:REL, 0:2, :],
                                                     sy[:, REL, 0:2, :].unsqueeze(1).to_broadcast([128, REL, 2, SIDE]), ALU.mult))
                        return
                    link(nc.vector.tensor_tensor(prod[0][:, :, :, 0:w], sy[:, 0:REL, 0:2, r2:],
                                                 sy[:, REL + r2, 0:2, 0:w].unsqueeze(1).to_broadcast([128, REL, 2, w]), ALU.mult))
                    sum_ = tt[:, r2:r2 + REL, 0:2, 0:w]
                    link(nc.vector.tensor_tensor(sum_, sum_, prod[0][:, :, :, 0:w], ALU.add))

                def t_rest(img, a):
                    dve.wait_ge(G.t_cast, per(img, PARTS, a + 1))
                    nc.vector.tensor_tensor(tt[:, :, 0:2, :], tt[:, :, 0:2, :],
                                            t_parts[a].rearrange("p (k l x) -> p k l x", l=4, x=SIDE)[:, :, 0:2, :],
                                            ALU.subtract).then_inc(G.t_sum_dve, 1)

                def s_minus(img, a):
                    dve.wait_ge(G.s_cast, per(img, PARTS, a + 1))
                    if a == 1:
                        dve.wait_ge(G.s_sub, per(img, 2, 1))
                    src = sy[:, 0:REL, :, :].rearrange("p k l x -> p (k l x)") if a == 0 else s_rest
                    nc.vector.tensor_tensor(s_rest, src, s_parts[:, a, :], ALU.subtract).then_inc(G.s_sub, 1)

                def maxima(img, q, b):
                    dve.wait_ge(G.kv_evac, per(img, 64, 16 * q + MAX_CUT[b + 1] // 2))
                    return nc.vector.tensor_reduce(mxq[:, b, :], kv[:, MAX_CUT[b]:MAX_CUT[b + 1], 0:128].rearrange("p l c -> p c l"),
                                                   AX.X, ALU.max)

                def take_f(img, q):
                    dve.wait_ge(G.f_mm, per(img, PAIRS, q + 1))
                    nc.vector.tensor_copy(fmat[:], MS[:, 256:512]).then_inc(G.f_copied, 1)

                def take_a(img, q):
                    dve.wait_ge(G.a_mm, per(img, PAIRS, q + 1))
                    if q == 0:
                        dve.wait_ge(G.a_out, per(img, 16, 0))
                        nc.vector.tensor_copy(amat[:], CX[:]).then_inc(G.a_copied, 1)
                    else:
                        dve.wait_ge(G.a_copied, per(img, PAIRS, q))
                        nc.vector.tensor_tensor(amat[:], amat[:], CX[:], ALU.add).then_inc(G.a_copied, 1)

                def points_x(img, q):
                    dve.wait_ge(G.pts_in, per(img, 16 * PAIRS, 16 * (q + 1)))
                    dve.wait_ge(G.key_out, per(img, 16 * PAIRS, 16 * q))
                    link(nc.vector.tensor_scalar(pt[:, 0, :], pc[:, :, 0], -25.6, 5.0, ALU.subtract, ALU.mult))
                    link(nc.vector.tensor_scalar(pt[:, 1, :], pt[:, 0, :], MAGIC, MAGIC, ALU.add, ALU.subtract))
                    link(nc.vector.tensor_tensor(pt[:, 2, :], pt[:, 1, :], pt[:, 0, :], ALU.is_gt))
                    link(nc.vector.tensor_tensor(pt[:, 1, :], pt[:, 1, :], pt[:, 2, :], ALU.subtract))
                    link(nc.vector.tensor_scalar(pt[:, 5, :], pt[:, 1, :], float(2 * BLOCK), 1.0, ALU.mult, ALU.add))

                def points_axis(img, q, axis, low, high, inv, size, vox, cells):
                    vh = float(np.round(float(vox) * 2 ** 14) / 2 ** 14)
                    vl = float(np.float32(float(vox) - vh - float(vox) * 2.0 ** -24 * 0.75))
                    v = pc[:, :, axis]
                    nc.vector.tensor_scalar(pt[:, 1, :], v, low, None, ALU.subtract)
                    link(nc.vector.tensor_scalar(pt[:, 0, :], v, low, inv, ALU.subtract, ALU.mult))
                    link(nc.vector.tensor_scalar(pt[:, 2, :], pt[:, 0, :], MAGIC, MAGIC, ALU.add, ALU.subtract))
                    link(nc.vector.scalar_tensor_tensor(pt[:, 0, :], pt[:, 2, :], -vh, pt[:, 1, :], ALU.mult, ALU.add))
                    link(nc.vector.scalar_tensor_tensor(pt[:, 1, :], pt[:, 2, :], vl, pt[:, 0, :], ALU.mult, ALU.is_gt))
                    link(nc.vector.tensor_tensor(pt[:, 2, :], pt[:, 2, :], pt[:, 1, :], ALU.subtract))
                    link(nc.vector.tensor_scalar(pt[:, 2, :], pt[:, 2, :], float(size - 1), float(cells), ALU.min, ALU.mult))
                    link(nc.vector.tensor_tensor(pt[:, 5, :], pt[:, 5, :], pt[:, 2, :], ALU.add))
                    link(nc.vector.scalar_tensor_tensor(pt[:, 3, :], v, low, pt[:, 4, :], ALU.is_ge, ALU.mult))
                    link(nc.vector.scalar_tensor_tensor(pt[:, 4, :], v, high, pt[:, 3, :], ALU.is_lt, ALU.mult))

                def points_label(img, q):
                    link(nc.vector.tensor_scalar(pt[:, 0, :], pc[:, :, 3], 0.0, float(NL - 1), ALU.max, ALU.min))
                    link(nc.vector.tensor_scalar(pt[:, 1, :], pt[:, 0, :], MAGIC, MAGIC, ALU.add, ALU.subtract))
                    link(nc.vector.tensor_tensor(pt[:, 2, :], pt[:, 1, :], pt[:, 0, :], ALU.is_gt))
                    link(nc.vector.tensor_tensor(pt[:, 1, :], pt[:, 1, :], pt[:, 2, :], ALU.subtract))
                    link(nc.vector.tensor_tensor(pt[:, 5, :], pt[:, 5, :], pt[:, 1, :], ALU.add))
                    link(nc.vector.memset(pt[:, 4, :], 1.0))

                def points_top(img, q):
                    nc.vector.sem_inc(G.unit_read, 1)
                    link(nc.vector.tensor_tensor(pt[:, 5, :], pt[:, 5, :], pt[:, 4, :], ALU.mult))
                    link(nc.vector.scalar_tensor_tensor(pt[:, 0, :], pt[:, 5, :], float(NX * 2 * BLOCK), pt[:, 5, :],
                                                        ALU.is_le, ALU.mult))
                    link(nc.vector.tensor_scalar(pt[:, 5, :], pt[:, 0, :], 0.0, None, ALU.max))
                    nc.vector.sem_inc(G.key_ready, 1)
                    src = pt[:, 5, :]
                    dve.wait_ge(G.top_out, per(img, 16 * PAIRS, 16 * q))
                    for k in range(3):
                        apart()
                        link(nc.vector.max(top24[:, 8 * k:8 * k + 8], src))
                        if k < 2:
                            apart()
                            link(nc.vector.match_replace(pt[:, k, :], top24[:, 8 * k:8 * k + 8], src, 0.0))
                            src = pt[:, k, :]
                    nc.vector.sem_inc(G.top_ready, 1)

                def image(img, last):
                    now[0] = img
                    steps[0] = 0
                    for q in range(PAIRS):
                        if q == 0:
                            dve.wait_ge(G.sy_in, img * 32 + 32)
                            dve.wait_ge(G.tp_out, per(img, 48, 0))
                            apart()
                            t_product(0)
                            s_minus(img, 0)
                            t_product(1)
                            t_product(2)
                            s_minus(img, 1)
                            for r2 in range(3, REL):
                                t_product(r2)
                            nc.vector.sem_inc(G.t_sum_dve, 1)
                        for b in range(4):
                            last_max = maxima(img, q, b)
                            if q == PAIRS - 1 and not last:
                                if b == 0:
                                    stats(img + 1)
                                if b == 1:
                                    variance(img + 1)
                                if b == 2:
                                    scale_bias(img + 1)
                        link(last_max)
                        nc.vector.tensor_reduce(mx[:], mxq[:].rearrange("p b c -> p c b"), AX.X, ALU.max).then_inc(G.max_ready, 1)
                        for job in ORDER[q == 0]:
                            if job in JOB:
                                gen_tiles(img, q, job)
                                if job == "s0":
                                    dve.wait_ge(G.swap_mm, per(img, PAIRS, q + 1))
                                    nc.vector.tensor_tensor(mxx[:], mx[:], MS[:, 0:128], ALU.max).then_inc(G.shift_ready, 1)
                                if q == 0 and job in ("s0", "s1"):
                                    t_rest(img, int(job[1]))
                                if q == PAIRS - 1 and job == "s1" and not last:
                                    dve.wait_ge(G.pj_mm, per(img, 64, 64))
                                    normalise()
                            elif job[0] == "y":
                                for k in range(8):
                                    n = 8 * int(job[1]) + k
                                    dve.wait_ge(G.y_mm, per(img, 64, 16 * q + n + 1))
                                    for h in range(2):
                                        apart()
                                        st = nc.vector.bn_stats(ybn[64 * h:64 * h + 64, n, :],
                                                                STR[n % 3][64 * h:64 * h + 64, 256 * h:256 * h + 256])
                                    st.then_inc(G.y_stat, 1)
                                if q == PAIRS - 1 and job == "y1" and not last:
                                    s_edges(img + 1)
                            else:
                                for k in range(8):
                                    n = 8 * int(job[1]) + k
                                    m = 8 * q + n // 2
                                    dve.wait_ge(G.p_mm, per(img, 64, 16 * q + n + 1))
                                    dve.wait_ge(p_out[m % SLOTS], per(img, 128, 16 * (m // SLOTS)))
                                    nc.vector.tensor_copy(ptile[64:128, m % SLOTS, 256 * (n % 2):256 * (n % 2) + 256],
                                                          STR[(16 + n) % 3][64:128, 256:512]).then_inc(G.p_dve, 1)
                                    if n in SUM_AT:
                                        b = SUM_AT.index(n)
                                        dve.wait_ge(G.exp_done, per(img, 16, 4 * q + b + 1))
                                        part = nc.vector.tensor_reduce(
                                            mxq[:, b, :], kv[:, 8 * b:8 * b + 8, 0:128].rearrange("p l c -> p c l"), AX.X, ALU.add)
                                        if b == 3:
                                            link(part)
                                            nc.vector.tensor_reduce(mx[:], mxq[:].rearrange("p b c -> p c b"), AX.X, ALU.add)\
                                                .then_inc(G.zsum_ready, 1)
                                    if n == ZSUM_AT + 1:
                                        dve.wait_ge(G.zsum_mm, per(img, PAIRS, q + 1))
                                        nc.vector.reciprocal(rz[:], MS[:, 128:256]).then_inc(G.rz_ready, 1)
                        dve.wait_ge(G.y_stat, per(img, 64, 16 * q + 16))
                        apart()
                        link(nc.vector.bn_aggr(mvy[:], ybn[:].rearrange("p k s -> p (k s)")))
                        link(nc.vector.tensor_copy(ustat[:, ds(img * PAIRS + q, 1), :].rearrange("p u k -> p (u k)"), mvy[:]))
                        for piece in WINDOW[q]:
                            piece(img, q)

                def take_ctx(img, q):
                    dve.wait_ge(G.ctx_mm, per(img, PAIRS, q + 1))
                    for h in range(2):
                        nc.vector.tensor_copy(ctxbd[64 * h:64 * h + 64, 64 * h:64 * h + 64],
                                              CX[64 * h:64 * h + 64, 64 * h:64 * h + 64]).then_inc(G.ctx_copied, 1)

                def px(c):
                    return lambda img, q: (points_x(img, c), points_label(img, c))

                def py(c):
                    return lambda img, q: points_axis(img, c, 1, -25.6, 25.6, 5.0, NY, VY, ZL)

                def pz(c):
                    return lambda img, q: points_axis(img, c, 2, -2.0, float(np.float32(1.2)), 10.0, NZ, np.float32(0.1), NL)

                def top(c):
                    return lambda img, q: points_top(img, c)

                WINDOW = ((px(0), py(0), take_ctx, pz(0), top(0), take_f, px(1), take_a, py(1)),
                          (pz(1), top(1), take_ctx, px(2), py(2), take_f, pz(2), take_a, top(2)),
                          (px(3), py(3), take_ctx, pz(3), top(3), take_f, take_a),
                          (take_ctx, take_f, take_a))

                dve.wait_ge(G.w_in, 64)
                dve.wait_ge(G.zeroed, 3)
                stats(0)
                variance(0)
                scale_bias(0)
                normalise()
                s_edges(0)
                first[0] = steps[0]
                with dve.Fori(0, IMAGES - 1) as img:
                    image(img, False)
                    assert steps[0] == DVE_STEPS
                image(IMAGES - 1, True)


def histogram_and_pass2(nc, t, e):
    fp32, bf16, fp16, i32 = mybir.dt.float32, mybir.dt.bfloat16, mybir.dt.float16, mybir.dt.int32
    ALU, ACT, AX = mybir.AluOpType, mybir.ActivationFunctionType, mybir.AxisListType
    ds = bass.ds
    sb, sem = e["sb"], e["sem"]
    PJ, GN, ST, CX, MS = e["PJ"], e["GN"], e["ST"], e["CX"], e["MS"]
    block_lo, block_hi, cand_dram, keys_dram = e["block_lo"], e["block_hi"], e["cand_dram"], e["keys_dram"]
    SLOTS = NX + 2
    with ExitStack() as own:
        hist = sb(own, "hist", [128, SLOTS * 2 * HROW])

        with ExitStack() as tmp:
            cand = sb(tmp, "cand", [PROWS, NCHUNK, TOP])
            work = sb(tmp, "work", [PROWS, 2, NCHUNK * TOP])
            best = sb(tmp, "best", [PROWS, SET])
            sets = sb(tmp, "sets", [PROWS, BLOCKS, SET])
            over = sb(tmp, "over", [PROWS, 4])
            overb = sb(tmp, "overb", [PROWS, BLOCKS])
            ones = sb(tmp, "ones", [PROWS, 1])
            full = sb(tmp, "full", [1, 1])
            control = sb(tmp, "control", [1, 4], i32)
            kset = sb(tmp, "kset", [PROWS, 2, SET])
            rel = sb(tmp, "rel", [PROWS, SET])
            tq = sb(tmp, "tq", [PROWS, SET])
            yrow = sb(tmp, "yrow", [PROWS, 2, SET])
            zlab = sb(tmp, "zlab", [PROWS, 2, SET])
            index = sb(tmp, "index", [PROWS, ZL])
            index16 = sb(tmp, "index16", [PROWS, ZL], fp16)
            hoty = sb(tmp, "hoty", [PROWS, 2, OHG, 128], bf16)
            hotz = sb(tmp, "hotz", [PROWS, 2, OHG, ZL], bf16)
            names = ("idx_in apart sort_step flags_ready over_mm control_ready sets_ready sets_out set_in0 set_in1 set_read "
                     "hot_ready hot_used hist_mm hist_added hist_zero decode_step").split()
            G = type("Sems", (), {n: sem("hist_" + n) for n in names})
            SORT = 11
            NG = SET // OHG
            PSUM = [PJ[:].rearrange("p b f -> p (b f)")[:, 0:ZL], GN[:].rearrange("p b f -> p (b f)")[:, 0:ZL]]

            with nc.Block() as block:
                @block.sync
                def _(sp):
                    sp.dma_start(cand[:].rearrange("p n k -> p (n k)"), cand_dram).then_inc(G.idx_in, 16)
                    sp.dma_start(index[:], t["index"][0:PROWS, :]).then_inc(G.idx_in, 16)
                    sp.wait_ge(G.sets_ready, 1)
                    sp.dma_start(keys_dram[:, 0:BLOCKS * SET], sets[:].rearrange("p b k -> p (b k)")).then_inc(G.sets_out, 16)
                    sp.wait_ge(G.sets_out, 16)
                    sp.wait_ge(G.control_ready, 1)
                    rounds = sp.value_load(control[0:1, 0:1], min_val=1, max_val=PCOLS // SET)
                    stride = sp.value_load(control[0:1, 1:2], min_val=0, max_val=SET)
                    base = sp.value_load(control[0:1, 2:3], min_val=0, max_val=BLOCKS * SET)
                    with sp.Fori(0, rounds) as r:
                        with sp.Fori(0, BLOCKS // 2) as half:
                            for j in range(2):
                                sp.wait_ge(G.set_read, r * BLOCKS + half * 2 + j + 1)
                                sp.dma_start(kset[:, j, :], keys_dram[:, ds(base + r * SET + (half * 2 + j) * stride, SET)])\
                                  .then_inc([G.set_in0, G.set_in1][j], 16)

                @block.gpsimd
                def _(pool):
                    nc.gpsimd.memset(hist[:], 0.0).then_inc(G.hist_zero, 1)

                @block.tensor
                def _(pe):
                    pe.sem_inc(G.hot_used, 2)
                    pe.wait_ge(G.flags_ready, 1)
                    nc.tensor.matmul(CX[0:1, 0:1], over[:, 3:4], ones[:], start=True, stop=True).then_inc(G.over_mm, 1)
                    pe.wait_ge(G.control_ready, 1)
                    rounds = pe.value_load(control[0:1, 0:1], min_val=1, max_val=PCOLS // SET)
                    with pe.Fori(0, rounds) as r:
                        with pe.Fori(0, BLOCKS // 2) as half:
                            for j in range(2):
                                pe.wait_ge(G.hist_added, r * BLOCKS + half * 2 + j + 1)
                                for g in range(NG):
                                    i = j * NG + g
                                    pe.wait_ge(G.hot_ready, r * (BLOCKS * NG) + half * (2 * NG) + i + 1)
                                    for k in range(OHG):
                                        first, last = g == 0 and k == 0, g == NG - 1 and k == OHG - 1
                                        nc.tensor.matmul(PSUM[j][:, 0:512], hoty[:, i % 2, k, :], hotz[:, i % 2, k, 0:512],
                                                         start=first, stop=last)
                                        mm = nc.tensor.matmul(PSUM[j][:, 512:ZL], hoty[:, i % 2, k, :], hotz[:, i % 2, k, 512:ZL],
                                                              start=first, stop=last)
                                    if g < NG - 1:
                                        mm.then_inc(G.hot_used, 1)
                                    else:
                                        mm.then_inc(G.hist_mm, 1)

                @block.vector
                def _(dve):
                    steps = [0]

                    def link(ins, base):
                        steps[0] += 1
                        ins.then_inc(G.sort_step, 1)
                        dve.wait_ge(G.sort_step, base + steps[0])

                    dve.sem_inc(G.hist_added, 2)
                    dve.sem_inc(G.set_read, 2)
                    nc.vector.memset(ones[:], 1.0)
                    dve.wait_ge(G.idx_in, 32)
                    with dve.Fori(0, BLOCKS) as b:
                        steps[0] = 0
                        now = b * SORT
                        link(nc.vector.scalar_tensor_tensor(work[:, 0, :], cand[:].rearrange("p n k -> p (n k)"),
                                                            block_hi[0:PROWS, ds(b, 1)],
                                                            cand[:].rearrange("p n k -> p (n k)"), ALU.is_lt, ALU.mult), now)
                        for k in range(SET // 8):
                            dve.sem_inc(G.apart, 1)
                            link(nc.vector.max(best[:, 8 * k:8 * k + 8], work[:, k % 2, :]), now)
                            if k < SET // 8 - 1:
                                dve.sem_inc(G.apart, 1)
                                link(nc.vector.match_replace(work[:, 1 - k % 2, :], best[:, 8 * k:8 * k + 8],
                                                             work[:, k % 2, :], 0.0), now)
                        link(nc.vector.tensor_copy(sets[:, ds(b, 1), :].rearrange("p b k -> p (b k)"), best[:]), now)
                        assert steps[0] == SORT
                    nc.vector.sem_inc(G.sets_ready, 1)
                    steps[0] = 0
                    now = BLOCKS * SORT
                    link(nc.vector.tensor_reduce(over[:, 0:1], cand[:, :, TOP - 1], AX.X, ALU.max), now)
                    link(nc.vector.tensor_scalar(over[:, 1:2], over[:, 0:1], 0.0, None, ALU.is_gt), now)
                    link(nc.vector.tensor_tensor(overb[:], sets[:, :, SET - 1], block_lo[0:PROWS, :], ALU.is_ge), now)
                    link(nc.vector.tensor_reduce(over[:, 2:3], overb[:], AX.X, ALU.max), now)
                    nc.vector.tensor_tensor(over[:, 3:4], over[:, 1:2], over[:, 2:3], ALU.max).then_inc(G.flags_ready, 1)
                    dve.wait_ge(G.over_mm, 1)
                    link(nc.vector.tensor_scalar(full[:], CX[0:1, 0:1], 1.0, None, ALU.min), now)
                    nc.vector.tensor_scalar(control[:, 0:1], full[:], float(PCOLS // SET - 1), 1.0, ALU.mult, ALU.add)
                    nc.vector.tensor_scalar(control[:, 1:2], full[:], -float(SET), float(SET), ALU.mult, ALU.add)
                    nc.vector.tensor_scalar(control[:, 2:3], full[:], float(BLOCKS * SET), None, ALU.mult).then_inc(G.control_ready, 1)
                    link(nc.vector.tensor_copy(index16[:], index[:]), now)
                    dve.wait_ge(G.control_ready, 1)
                    dve.wait_ge(G.hist_zero, 1)
                    rounds = dve.value_load(control[0:1, 0:1], min_val=1, max_val=PCOLS // SET)
                    DEC = 4
                    with dve.Fori(0, rounds) as r:
                        with dve.Fori(0, BLOCKS // 2) as half:
                            for j in range(2):
                                it = r * BLOCKS + half * 2 + j
                                b = half * 2 + j
                                dve.wait_ge([G.set_in0, G.set_in1][j], (r * (BLOCKS // 2) + half + 1) * 16)
                                nc.vector.tensor_scalar(rel[:], kset[:, j, :], block_lo[0:PROWS, ds(b, 1)], None,
                                                        ALU.subtract).then_inc(G.decode_step, 1)
                                dve.wait_ge(G.decode_step, it * DEC + 1)
                                nc.vector.tensor_scalar(tq[:], rel[:], (ZL - 1) / 2, 1.0 / ZL, ALU.subtract, ALU.mult)\
                                  .then_inc(G.decode_step, 1)
                                dve.wait_ge(G.decode_step, it * DEC + 2)
                                nc.vector.tensor_scalar(yrow[:, j, :], tq[:], MAGIC, MAGIC, ALU.add, ALU.subtract)\
                                  .then_inc(G.decode_step, 1)
                                dve.wait_ge(G.decode_step, it * DEC + 3)
                                nc.vector.scalar_tensor_tensor(zlab[:, j, :], yrow[:, j, :], -float(ZL), rel[:], ALU.mult, ALU.add)\
                                  .then_inc(G.decode_step, 1)
                                dve.wait_ge(G.decode_step, it * DEC + 4)
                                nc.vector.sem_inc(G.set_read, 1)
                                for g in range(NG):
                                    i = j * NG + g
                                    if g >= 2:
                                        dve.wait_ge(G.hot_used, it * (NG - 1) + g - 1 + 2)
                                    elif g == 1:
                                        dve.wait_ge(G.hist_mm, it)
                                    else:
                                        dve.wait_ge(G.hot_used, it * (NG - 1) + 2)
                                    for k in range(OHG):
                                        c = g * OHG + k
                                        nc.vector.tensor_scalar(hoty[:, i % 2, k, :], index16[:, 0:128], yrow[:, j, c:c + 1], None,
                                                                ALU.is_equal)
                                        hot = nc.vector.tensor_scalar(hotz[:, i % 2, k, :], index16[:], zlab[:, j, c:c + 1], None,
                                                                      ALU.is_equal)
                                    hot.then_inc(G.hot_ready, 1)
                                dve.wait_ge(G.hist_mm, it + 1)
                                row = hist[:, ds((b + 2) * HROW + NL, ZL)]
                                nc.vector.tensor_tensor(row, row, PSUM[j], ALU.add).then_inc(G.hist_added, 1)

        pass2(nc, t, e, own, hist)


def pass2(nc, t, e, own, hist):
    fp32 = mybir.dt.float32
    ALU, ACT, AX = mybir.AluOpType, mybir.ActivationFunctionType, mybir.AxisListType
    ds = bass.ds
    sb, sem = e["sb"], e["sem"]
    PJ, GN, ST, CX, MS = e["PJ"], e["GN"], e["ST"], e["CX"], e["MS"]
    wout, g_t, g_n, affine, ustat, group_mean = (e[k] for k in ("wout", "g_t", "g_n", "affine", "ustat", "group_mean"))
    both_halves = e["both_halves"]
    gamma, beta, b_out = e["gamma"], e["beta"], e["b_out"]
    bad_dram, a_dram, p_dram, x_dram, out_dram = (e[k] for k in ("bad_dram", "a_dram", "p_dram", "x_dram", "out_dram"))

    wouta = sb(own, "wouta", [128, PAIRS, CHANNELS])
    edge_u = sb(own, "edge_u", [NS, CHANNELS])
    edge_neg = sb(own, "edge_neg", [NS, CHANNELS])
    ug = sb(own, "ug", [128, CT * CHANNELS])
    taps = sb(own, "taps", [128, 9, 128])
    cross = sb(own, "cross", [128, 2, 9, 128])

    with ExitStack() as tmp:
        mask_cols = sb(tmp, "mask_cols", [128, PAIRS, NS])
        ccols = sb(tmp, "ccols", [128, PAIRS, NS])
        shift = sb(tmp, "shift", [128, 3, 128])
        crossm = sb(tmp, "crossm", [128, 2, 128])
        filt = sb(tmp, "filt", [128, 27])
        fexp = sb(tmp, "fexp", [128, 27])
        mom = sb(tmp, "mom", [128, 2, NCHUNK])
        moms = sb(tmp, "moms", [128, 2])
        bn = sb(tmp, "bn", [128, 8])
        tacc = sb(tmp, "tacc", [128, 2, 128])
        names = "pre_in mom_ready mom_mm bn_var bn_std c_ready u_mm u_copied ug_mm ug_copied exp_out pre_step".split()
        G = type("Sems", (), {n: sem("pre_" + n) for n in names})
        with nc.Block() as block:
            @block.sync
            def _(sp):
                sp.dma_start(mask_cols[:].rearrange("p q s -> p (q s)"), t["head_mask_cols"]).then_inc(G.pre_in, 16)
                sp.dma_start(shift[:].rearrange("p b f -> p (b f)"), t["shift"]).then_inc(G.pre_in, 16)
                sp.dma_start(crossm[:].rearrange("p b f -> p (b f)"), t["cross"]).then_inc(G.pre_in, 16)
                sp.dma_start(filt[:], t["conv_w"].to_broadcast([128, 27])).then_inc(G.pre_in, 16)

            @block.scalar
            def _(act):
                act.wait_ge(G.pre_in, 64)
                nc.scalar.activation(fexp[:], filt[:], ACT.Exp, scale=-1.0).then_inc(G.exp_out, 1)
                act.wait_ge(G.bn_var, 1)
                nc.scalar.activation(bn[:, 4:5], bn[:, 3:4], ACT.Sqrt).then_inc(G.bn_std, 1)

            @block.tensor
            def _(pe):
                pe.wait_ge(G.mom_ready, 1)
                nc.tensor.matmul(MS[:, 0:2], both_halves[:], moms[:], start=True, stop=True).then_inc(G.mom_mm, 1)
                pe.wait_ge(G.c_ready, 1)
                for q in range(PAIRS):
                    mm = nc.tensor.matmul(CX[0:NS, 0:CHANNELS], ccols[:, q, :], wout[:, q, :], start=(q == 0), stop=(q == PAIRS - 1))
                mm.then_inc(G.u_mm, 1)
                pe.wait_ge(G.u_copied, 2)
                for c in range(CT):
                    mm = nc.tensor.matmul(CX[:, 256 * c:256 * c + 256], g_n[:, 128 * c:128 * c + 128], edge_u[:], start=True, stop=True)
                mm.then_inc(G.ug_mm, 1)

            @block.vector
            def _(dve):
                steps = [0]

                def link(ins):
                    steps[0] += 1
                    ins.then_inc(G.pre_step, 1)
                    dve.wait_ge(G.pre_step, steps[0])

                link(nc.vector.tensor_tensor(mom[:, 1, :], ustat[:, :, 0], ustat[:, :, 0], ALU.mult))
                nc.vector.tensor_copy(mom[:, 0, :], ustat[:, :, 0])
                link(nc.vector.tensor_tensor(mom[:, 1, :], mom[:, 1, :], ustat[:, :, 1], ALU.add))
                nc.vector.tensor_reduce(moms[:], mom[:], AX.X, ALU.add).then_inc(G.mom_ready, 1)
                dve.wait_ge(G.mom_mm, 1)
                link(nc.vector.tensor_scalar(bn[:, 0:2], MS[:, 0:2], 1.0 / (2 * NCHUNK), None, ALU.mult))
                link(nc.vector.tensor_tensor(bn[:, 2:3], bn[:, 0:1], bn[:, 0:1], ALU.mult))
                link(nc.vector.tensor_tensor(bn[:, 2:3], bn[:, 1:2], bn[:, 2:3], ALU.subtract))
                nc.vector.tensor_scalar(bn[:, 3:4], bn[:, 2:3], 0.0, BN_EPS, ALU.max, ALU.add).then_inc(G.bn_var, 1)
                dve.wait_ge(G.bn_std, 1)
                link(nc.vector.reciprocal(bn[:, 5:6], bn[:, 4:5]))
                link(nc.vector.tensor_tensor(bn[:, 5:6], bn[:, 5:6], gamma[:], ALU.mult))
                link(nc.vector.tensor_tensor(bn[:, 6:7], bn[:, 0:1], bn[:, 5:6], ALU.mult))
                link(nc.vector.tensor_tensor(bn[:, 6:7], beta[:], bn[:, 6:7], ALU.subtract))
                nc.vector.tensor_scalar(wouta[:], wout[:], bn[:, 5:6], None, ALU.mult)
                dve.wait_ge(G.pre_in, 64)
                nc.vector.tensor_scalar(ccols[:], mask_cols[:], bn[:, 6:7], None, ALU.mult).then_inc(G.c_ready, 1)
                dve.wait_ge(G.u_mm, 1)
                nc.vector.tensor_copy(edge_u[:], CX[0:NS, 0:CHANNELS]).then_inc(G.u_copied, 1)
                nc.vector.tensor_scalar(edge_neg[:], CX[0:NS, 0:CHANNELS], -1.0, None, ALU.mult).then_inc(G.u_copied, 1)
                dve.wait_ge(G.ug_mm, 1)
                nc.vector.tensor_copy(ug[:], CX[:])
                dve.wait_ge(G.exp_out, 1)
                link(nc.vector.tensor_scalar(fexp[:], fexp[:], 1.0, None, ALU.add))
                link(nc.vector.reciprocal(filt[:], fexp[:]))
                link(nc.vector.memset(filt[:, 13:14], 1.0))
                for a in range(3):
                    for c in range(3):
                        tap = lambda b: filt[:, 9 * a + 3 * b + c:9 * a + 3 * b + c + 1]
                        link(nc.vector.tensor_scalar(tacc[:, 0, :], shift[:, 0, :], tap(0), None, ALU.mult))
                        link(nc.vector.scalar_tensor_tensor(tacc[:, 1, :], shift[:, 1, :], tap(1), tacc[:, 0, :], ALU.mult, ALU.add))
                        link(nc.vector.scalar_tensor_tensor(taps[:, 3 * a + c, :], shift[:, 2, :], tap(2), tacc[:, 1, :], ALU.mult, ALU.add))
                        nc.vector.tensor_scalar(cross[:, 0, 3 * a + c, :], crossm[:, 0, :], tap(2), None, ALU.mult)
                        link(nc.vector.tensor_scalar(cross[:, 1, 3 * a + c, :], crossm[:, 1, :], tap(0), None, ALU.mult))

    xr = [sb(own, "x_even", [128, CT, PIX]), sb(own, "x_odd", [128, CT, PIX])]
    xn = sb(own, "xn2", [128, CT, PIX])
    ptile = sb(own, "ptile2", [128, 2, PAIRS, 512])
    at = sb(own, "at", [128, 2, CT * CHANNELS])
    sbad = sb(own, "sbad2", [NS, 2, SIDE * EDGE])
    bnst = sb(own, "bnst2", [128, CT, 8, 6])
    mv = sb(own, "mv2", [128, CT, 2])
    aff = sb(own, "aff2", [128, CT, 2])
    tmp2 = sb(own, "tmp22", [128, CT])
    std = sb(own, "std2", [128, CT])
    names = ("x_in0 x_in1 a_in0 a_in1 p_in0 p_in1 at_ready xn_ready o_mm o_evac p_used stat_ready stat_mm var_ready std_ready aff_ready apart "
             "scaled conv_mm conv_added stored0 stored1 step").split()
    G = type("Sems", (), {n: sem("out_" + n) for n in names})
    STEPS = 20
    OPS = [PJ[:, 0, :], PJ[:, 1, :], GN[:, 0, :], GN[:, 1, :]]
    CPS = [ST[:, 0, :], ST[:, 1, :], CX[:], MS[:]]
    ZCUT = [(0, ZA), (ZA, NZ + 1 - ZA)]

    with nc.Block() as block:
        @block.sync
        def _(sp):
            def fetch(pair_of_images, j):
                i = pair_of_images
                sp.wait_ge([G.stored0, G.stored1][j], i * 32)
                for c in range(CT):
                    sp.dma_start(xr[j][:, c, :], x_dram[ds(i * 2 + j, 1), :, c, :].rearrange("b p f -> (b p) f"))\
                      .then_inc([G.x_in0, G.x_in1][j], 16)
                sp.dma_start(at[:, j, :], a_dram[ds(i * 2 + j, 1), :, :].rearrange("b p f -> (b p) f"))\
                  .then_inc([G.a_in0, G.a_in1][j], 16)
                sp.dma_start(sbad[:, j, :], bad_dram[ds(i * 2 + j, 1), :, :].rearrange("b s f -> (b s) f"))\
                  .then_inc([G.a_in0, G.a_in1][j], 16)

            def store(i, j):
                sp.wait_ge(G.conv_added, i * 8 + 4 * j + 4)
                for c in range(CT):
                    sp.dma_start(out_dram[ds(i * 2 + j, 1), :, c, :].rearrange("b p f -> (b p) f"), xr[j][:, c, :])\
                      .then_inc([G.stored0, G.stored1][j], 16)

            fetch(0, 0)
            with sp.Fori(0, IMAGES // 2 - 1) as i:
                fetch(i, 1)
                store(i, 0)
                fetch(i + 1, 0)
                store(i, 1)
            fetch(IMAGES // 2 - 1, 1)
            store(IMAGES // 2 - 1, 0)
            store(IMAGES // 2 - 1, 1)
            sp.wait_ge(G.stored0, 16 * IMAGES)
            sp.wait_ge(G.stored1, 16 * IMAGES)

        @block.gpsimd
        def _(pool):
            with pool.Fori(0, IMAGES) as img:
                for k in range(8):
                    if k < 2:
                        pool.wait_ge(G.p_used, img * 8)
                    else:
                        pool.wait_ge(G.p_used, img * 8 + k - 1)
                    pool.dma_start(ptile[:, k % 2, :, :],
                                   p_dram[ds(img, 1), :, :, 512 * k:512 * k + 512].rearrange("b q p f -> (b p) q f"))\
                        .then_inc([G.p_in0, G.p_in1][k % 2], 16)

        @block.scalar
        def _(act):
            with act.Fori(0, IMAGES // 2) as i:
                for j in range(2):
                    act.wait_ge([G.x_in0, G.x_in1][j], i * 32 + 32)
                    act.wait_ge(G.o_mm, i * 32 + 16 * j)
                    sc = affine[:, ds(i * 2 + j, 1), 1, 0:1].rearrange("p b k -> p (b k)")
                    bi = affine[:, ds(i * 2 + j, 1), 1, 1:2].rearrange("p b k -> p (b k)")
                    nc.scalar.activation(xn[:, 1, :].rearrange("p (y x) -> p y x", x=SIDE),
                                         xr[j][:, 1, :].rearrange("p (x y) -> p y x", y=SIDE), ACT.Identity,
                                         bias=bi, scale=sc).then_inc(G.xn_ready, 1)
                    act.wait_ge(G.var_ready, i * 2 + j + 1)
                    nc.scalar.activation(std[:], tmp2[:], ACT.Sqrt).then_inc(G.std_ready, 1)
                    act.wait_ge(G.aff_ready, i * 2 + j + 1)
                    nc.scalar.activation(xr[j][:, 1, :], xr[j][:, 1, :], ACT.Identity,
                                         bias=aff[:, 1, 1:2], scale=aff[:, 1, 0:1]).then_inc(G.scaled, 1)

        @block.tensor
        def _(pe):
            with pe.Fori(0, IMAGES // 2) as i:
                for j in range(2):
                    pe.wait_ge(G.xn_ready, i * 4 + 2 * j + 2)
                    pe.wait_ge(G.at_ready, i * 2 + j + 1)
                    for k in range(8):
                        pe.wait_ge([G.p_in0, G.p_in1][k % 2], i * 128 + 64 * j + 16 * (k // 2) + 16)
                        for o in range(CT):
                            n = 2 * k + o
                            ps = OPS[n % 4]
                            if n < 4:
                                pe.wait_ge(G.o_evac, i * 32 + 16 * j)
                            else:
                                pe.wait_ge(G.o_evac, i * 32 + 16 * j + n - 3)
                            for c in range(CT):
                                nc.tensor.matmul(ps, at[:, j, 256 * c + 128 * o:256 * c + 128 * o + 128],
                                                 xn[:, c, 512 * k:512 * k + 512], start=(c == 0), stop=False)
                            for q in range(PAIRS):
                                nc.tensor.matmul(ps, wouta[:, q, 128 * o:128 * o + 128], ptile[:, k % 2, q, :],
                                                 start=False, stop=False)
                            mm = nc.tensor.matmul(ps.rearrange("p (y x) -> p y x", x=SIDE)[:, :, SIDE - EDGE:],
                                                  edge_neg[:, 128 * o:128 * o + 128],
                                                  sbad[:, j, 8 * EDGE * k:8 * EDGE * (k + 1)].rearrange("p (y x) -> p y x", x=EDGE),
                                                  start=False, stop=True)
                            mm.then_inc(G.o_mm, 1)
                        pe.wait_ge(G.o_mm, i * 32 + 16 * j + 2 * k + 2)
                        pe.sem_inc(G.p_used, 1)
                    for o in range(CT):
                        for z, (z0, zn) in enumerate(ZCUT):
                            n = 2 * o + z
                            pe.wait_ge(G.conv_added, i * 8 + 4 * j)
                            for a in range(3):
                                for c in range(3):
                                    src = lambda half: hist[:, ds((i * 2 + j + a) * (2 * HROW) + half * HROW + (z0 + c) * NL, zn * NL)]
                                    nc.tensor.matmul(CPS[n][:, 0:zn * NL], taps[:, 3 * a + c, :], src(o),
                                                     start=(a == 0 and c == 0), stop=False)
                                    mm = nc.tensor.matmul(CPS[n][:, 0:zn * NL], cross[:, o, 3 * a + c, :], src(1 - o),
                                                          start=False, stop=(a == 2 and c == 2))
                            mm.then_inc(G.conv_mm, 1)
                    pe.wait_ge(G.stat_ready, i * 2 + j + 1)
                    pe.wait_ge(G.o_evac, i * 32 + 16 * j + 16)
                    nc.tensor.matmul(PJ[:, 0, 0:2 * CT], group_mean[:], mv[:].rearrange("p t k -> p (t k)"),
                                     start=True, stop=True).then_inc(G.stat_mm, 1)

        @block.vector
        def _(dve):
            steps = [0]
            with dve.Fori(0, IMAGES // 2) as i:
                def link(ins):
                    steps[0] += 1
                    ins.then_inc(G.step, 1)
                    dve.wait_ge(G.step, i * STEPS + steps[0])

                for j in range(2):
                    dve.wait_ge([G.a_in0, G.a_in1][j], i * 32 + 32)
                    nc.vector.tensor_tensor(at[:, j, :], at[:, j, :], ug[:], ALU.add).then_inc(G.at_ready, 1)
                    dve.wait_ge([G.x_in0, G.x_in1][j], i * 32 + 32)
                    dve.wait_ge(G.o_mm, i * 32 + 16 * j)
                    sc = affine[:, ds(i * 2 + j, 1), 0, 0:1].rearrange("p b k -> p (b k)")
                    bi = affine[:, ds(i * 2 + j, 1), 0, 1:2].rearrange("p b k -> p (b k)")
                    nc.vector.tensor_scalar(xn[:, 0, :].rearrange("p (y x) -> p y x", x=SIDE),
                                            xr[j][:, 0, :].rearrange("p (x y) -> p y x", y=SIDE),
                                            sc, bi, ALU.mult, ALU.add).then_inc(G.xn_ready, 1)
                    dve.wait_ge(G.xn_ready, i * 4 + 2 * j + 2)
                    for k in range(8):
                        for o in range(CT):
                            n = 2 * k + o
                            dve.wait_ge(G.o_mm, i * 32 + 16 * j + n + 1)
                            xv = xr[j][:, o, :].rearrange("p (x y) -> p y x", y=SIDE)[:, 8 * k:8 * k + 8, :]
                            nc.vector.scalar_tensor_tensor(xv, OPS[n % 4].rearrange("p (y x) -> p y x", x=SIDE), b_out[:, o:o + 1],
                                                           xv, ALU.add, ALU.add).then_inc(G.o_evac, 1)
                    dve.wait_ge(G.o_evac, i * 32 + 16 * j + 16)
                    for c in range(CT):
                        for k in range(8):
                            last = nc.vector.bn_stats(bnst[:, c, k, :], xr[j][:, c, 512 * k:512 * k + 512])
                    link(last)
                    dve.sem_inc(G.apart, 1)
                    nc.vector.bn_aggr(mv[:, 0, :], bnst[:, 0, :, :].rearrange("p k s -> p (k s)"))
                    link(nc.vector.bn_aggr(mv[:, 1, :], bnst[:, 1, :, :].rearrange("p k s -> p (k s)")))
                    link(nc.vector.tensor_tensor(tmp2[:], mv[:, :, 0], mv[:, :, 0], ALU.mult))
                    nc.vector.tensor_tensor(mv[:, :, 1], mv[:, :, 1], tmp2[:], ALU.add).then_inc(G.stat_ready, 1)
                    dve.wait_ge(G.stat_mm, i * 2 + j + 1)
                    link(nc.vector.tensor_copy(mv[:].rearrange("p t k -> p (t k)"), PJ[:, 0, 0:2 * CT]))
                    link(nc.vector.tensor_tensor(tmp2[:], mv[:, :, 0], mv[:, :, 0], ALU.mult))
                    link(nc.vector.tensor_tensor(tmp2[:], mv[:, :, 1], tmp2[:], ALU.subtract))
                    nc.vector.tensor_scalar(tmp2[:], tmp2[:], 0.0, GN_EPS, ALU.max, ALU.add).then_inc(G.var_ready, 1)
                    dve.wait_ge(G.std_ready, i * 2 + j + 1)
                    link(nc.vector.reciprocal(std[:], std[:]))
                    link(nc.vector.tensor_tensor(tmp2[:], mv[:, :, 0], std[:], ALU.mult))
                    nc.vector.tensor_scalar(aff[:, :, 0], std[:], 1.0, None, ALU.add)
                    link(nc.vector.tensor_scalar(aff[:, :, 1], tmp2[:], -1.0, None, ALU.mult))
                    nc.vector.sem_inc(G.aff_ready, 1)
                    link(nc.vector.tensor_scalar(xr[j][:, 0, :], xr[j][:, 0, :], aff[:, 0, 0:1], aff[:, 0, 1:2], ALU.mult, ALU.add))
                    for o in range(CT):
                        if o == 1:
                            dve.wait_ge(G.scaled, i * 2 + j + 1)
                        for z, (z0, zn) in enumerate(ZCUT):
                            n = 2 * o + z
                            dve.wait_ge(G.conv_mm, i * 8 + 4 * j + n + 1)
                            xv = xr[j][:, o, :].rearrange("p (z l) -> p z l", l=SIDE)[:, z0:z0 + zn, 0:NL]
                            nc.vector.tensor_tensor(xv, xv, CPS[n][:, 0:zn * NL].rearrange("p (z l) -> p z l", l=NL), ALU.add)\
                                .then_inc(G.conv_added, 1)
                assert steps[0] == STEPS


def kernel(**inputs):
    import concourse.bacc as bacc
    from concourse.bass_utils import run_bass_kernel_spmd

    def lay(name, *shape):
        return np.ascontiguousarray(np.asarray(inputs[name]).reshape(*shape))

    w_qkv = np.asarray(inputs["L0_conv_w_qkv"])
    kt = w_qkv[HEADS * DK:2 * HEADS * DK].T.reshape(CHANNELS, PAIRS, 128)
    vt = w_qkv[2 * HEADS * DK:].T.reshape(CHANNELS, PAIRS, 128)
    arrays = {
        "x": np.asarray(inputs["x"]),
        "points": np.asarray(inputs["L1_conv_point_cloud"]),
        "conv_w": lay("L1_conv_weights", 1, 27),
        "w_q": np.ascontiguousarray(w_qkv[:HEADS * DK]),
        "w_kv_t": np.ascontiguousarray(np.concatenate([kt, vt], axis=2)),
        "w_out_t": np.ascontiguousarray(np.asarray(inputs["L0_conv_w_out"]).T),
        "b_out": np.ascontiguousarray(np.asarray(inputs["L0_conv_b_out"]).reshape(CT, 128).T),
        "rel_t": np.ascontiguousarray(np.concatenate([np.asarray(inputs["L0_conv_rel_rows"]).T,
                                                      np.asarray(inputs["L0_conv_rel_columns"]).T], axis=1)),
        "gamma": lay("L0_conv_bn_gamma", DK, 1),
        "beta": lay("L0_conv_bn_beta", DK, 1),
        **constants(),
    }
    nc = bacc.Bacc("TRN2", target_bir_lowering=False, num_devices=1)
    t = {k: nc.dram_tensor("in_" + k, a.shape, mybir.dt.from_np(a.dtype), kind="ExternalInput").ap() for k, a in arrays.items()}
    out = nc.dram_tensor("out", [IMAGES, CHANNELS, SIDE, SIDE], mybir.dt.float32, kind="ExternalOutput").ap()
    build(nc, t, out)
    r = run_bass_kernel_spmd(nc, [{"in_" + k: a for k, a in arrays.items()}], core_ids=[0])
    return r.results[0]["out"]
```

```python
import numpy as np
import concourse.bass as bass
from concourse import mybir
from contextlib import ExitStack

IMAGES, CHANNELS, SIDE = 8, 256, 64
HEADS, DK, REL = 8, 64, 7
PIX = SIDE * SIDE
CT = CHANNELS // 128
PAIRS = HEADS // 2
YL = SIDE // 2
NS = 2 * REL * HEADS
EDGE = REL - 1
GROUP = 8
PARTS = 3
TAPS = 2 * REL - 1
SROWS = 2 * PARTS * REL
GENK = SROWS + 2 * PARTS * TAPS
STRIP = 3 * SIDE - 1
BN_EPS, GN_EPS = 1e-5, 1e-5

POINTS = 1000000
PROWS = 125
PCOLS = POINTS // PROWS
NCHUNK = IMAGES * PAIRS
CHUNK = PCOLS // NCHUNK
TOP = 24
NX, NY, NZ, NL = 8, 256, 32, 21
ZL = NZ * NL
BLOCK = 128 * ZL
BLOCKS = NX * 2
SET = 32
OHG = 8
MAGIC = 1.5 * 2.0 ** 23
ZSLOT = NZ + 3
HROW = ZSLOT * NL
ZA = 17


def constants():
    c = {}
    p = np.arange(128)
    c["group_mean"] = (p[:, None] // GROUP == p[None] // GROUP).astype(np.float32) / GROUP
    c["swap_half"] = (p[:, None] == (p[None] + 64) % 128).astype(np.float32)
    c["both_halves"] = (p[:, None] % 64 == p[None] % 64).astype(np.float32)
    s = np.arange(NS)
    kind, r, head = s // (REL * HEADS), s // HEADS % REL, s % HEADS
    hm = np.zeros((128, PAIRS, NS), np.float32)
    for q in range(PAIRS):
        hm[:, q] = head[None] == 2 * q + p[:, None] // 64
    c["head_mask"] = hm.reshape(128, -1)
    c["head_mask_cols"] = (hm * (kind == 1)).reshape(128, -1).astype(np.float32)
    c["bad_mask"] = ((kind[:, None] == 1) & (r[:, None] + SIDE - EDGE + np.arange(EDGE)[None] >= SIDE)).astype(np.float32)
    c["good_mask"] = (r[:, None] + SIDE - EDGE + np.arange(EDGE)[None] < SIDE).astype(np.float32)
    d = np.zeros((GENK, 2, STRIP), np.float32)
    for y2 in range(2):
        for part in range(PARTS):
            for kind, (row0, taps) in enumerate(((0, REL), (PARTS * 2 * REL, TAPS))):
                for j in range(taps):
                    d[row0 + (y2 * PARTS + part) * taps + j, kind, SIDE - 1 + SIDE * y2 + j] = 1
    c["strip"] = d.reshape(GENK, 2 * STRIP)
    sh = np.stack([(p[:, None] == p[None] + b - 1) for b in range(3)], 1).astype(np.float32)
    c["shift"] = sh.reshape(128, 3 * 128)
    cr = np.zeros((9, 2, 128), np.float32)
    cr[:, 0, 127] = 1
    cr[:, 1, 0] = 1
    c["cross"] = cr.reshape(9, 256)
    lo = np.arange(BLOCKS) * BLOCK + 1.0
    c["block_lo"] = np.tile(lo[None], (128, 1)).astype(np.float32)
    c["block_hi"] = np.tile(lo[None] + BLOCK, (128, 1)).astype(np.float32)
    c["index"] = np.tile(np.arange(ZL)[None], (128, 1)).astype(np.float32)
    return c


def build(nc, t, out):
    fp32, bf16, fp16, i32 = mybir.dt.float32, mybir.dt.bfloat16, mybir.dt.float16, mybir.dt.int32
    ALU, ACT, AX = mybir.AluOpType, mybir.ActivationFunctionType, mybir.AxisListType
    ds = bass.ds
    VY = np.float32(51.2) / np.float32(256)

    s_dram = nc.dram_tensor("s_scratch", [IMAGES, NS, PIX], fp32, kind="Internal").ap()
    sp_dram = nc.dram_tensor("sp_scratch", [IMAGES, PARTS, REL, HEADS, PIX], bf16, kind="Internal").ap()
    tp_dram = nc.dram_tensor("tp_scratch", [IMAGES, PARTS, TAPS, HEADS, PIX], bf16, kind="Internal").ap()
    bad_dram = nc.dram_tensor("bad_scratch", [IMAGES, NS, SIDE * EDGE], fp32, kind="Internal").ap()
    a_dram = nc.dram_tensor("a_scratch", [IMAGES, 128, CT * CHANNELS], fp32, kind="Internal").ap()
    p_dram = nc.dram_tensor("p_scratch", [IMAGES, PAIRS, 128, PIX], fp32, kind="Internal").ap()
    keys_dram = nc.dram_tensor("keys_scratch", [PROWS, 2 * BLOCKS * SET + PCOLS], fp32, kind="Internal").ap()
    cand_dram = nc.dram_tensor("cand_scratch", [PROWS, NCHUNK * TOP], fp32, kind="Internal").ap()
    edge_dram = nc.dram_tensor("edge_scratch", [NX + 2, 2, HROW], fp32, kind="Internal").ap()
    pc_dram = t["points"].rearrange("(p k) c -> p (k c)", p=PROWS)
    x_dram = t["x"].rearrange("b (t p) h w -> b p t (h w)", p=128)
    out_dram = out.rearrange("b (t p) h w -> b p t (h w)", p=128)

    top = ExitStack()
    with top:
        def sb(stack, name, shape, dt=fp32):
            return stack.enter_context(nc.sbuf_tensor(name, shape, dt))

        front = top.enter_context(ExitStack())
        setup = top.enter_context(ExitStack())

        def sem(name):
            return top.enter_context(nc.semaphore(name))

        group_mean = sb(top, "group_mean", [128, 128])
        both_halves = sb(top, "both_halves", [128, 128])
        wout = sb(top, "wout", [128, PAIRS, CHANNELS])
        g_t = sb(top, "g_t", [128, CT, NS])
        g_n = sb(top, "g_n", [NS, CHANNELS])
        affine = sb(top, "affine", [128, IMAGES, CT, 2])
        ustat = sb(top, "ustat", [128, NCHUNK, 2])
        block_lo = sb(top, "block_lo", [128, BLOCKS])
        block_hi = sb(top, "block_hi", [128, BLOCKS])
        gamma = sb(top, "gamma", [128, 1])
        beta = sb(top, "beta", [128, 1])
        b_out = sb(top, "b_out", [128, CT])

        swap_half = sb(front, "swap_half", [128, 128])
        wq = sb(front, "wq", [128, PAIRS, CHANNELS])
        head_mask = sb(setup, "head_mask", [128, PAIRS, NS])
        relbd = sb(setup, "relbd", [128, PAIRS, NS])
        reld = sb(setup, "reld", [128, 2 * REL])

        PJ = top.enter_context(nc.psum_tensor("PJ", [128, 2, 512], fp32))
        GN = top.enter_context(nc.psum_tensor("GN", [128, 2, 512], fp32))
        ST = top.enter_context(nc.psum_tensor("ST", [128, 2, 512], fp32))
        CX = top.enter_context(nc.psum_tensor("CX", [128, 512], fp32))
        MS = top.enter_context(nc.psum_tensor("MS", [128, 512], fp32))

        setup_in = sem("setup_in")
        relbd_ready = sem("relbd_ready")
        g_ready = sem("g_ready")
        g_copied = sem("g_copied")
        with nc.Block() as block:
            @block.sync
            def _(sp):
                n = 0
                for dst, src in (
                        (group_mean[:], t["group_mean"]), (swap_half[:], t["swap_half"]),
                        (both_halves[:], t["both_halves"]),
                        (wq[:], t["w_q"].rearrange("(q p) c -> p q c", p=128)),
                        (wout[:], t["w_out_t"].rearrange("(q p) c -> p q c", p=128)),
                        (head_mask[:].rearrange("p q s -> p (q s)"), t["head_mask"]),
                        (reld[0:64, :], t["rel_t"]), (reld[64:128, :], t["rel_t"]),
                        (block_lo[:], t["block_lo"]), (block_hi[:], t["block_hi"]),
                        (gamma[0:64, :], t["gamma"]), (gamma[64:128, :], t["gamma"]),
                        (beta[0:64, :], t["beta"]), (beta[64:128, :], t["beta"]),
                        (b_out[:], t["b_out"])):
                    sp.dma_start(dst, src).then_inc(setup_in, 16)
                    n += 16
                assert n == 15 * 16

            @block.vector
            def _(dve):
                dve.wait_ge(setup_in, 15 * 16)
                for q in range(PAIRS):
                    nc.vector.tensor_tensor(
                        relbd[:, q, :].rearrange("p (k n) -> p k n", n=HEADS),
                        head_mask[:, q, :].rearrange("p (k n) -> p k n", n=HEADS),
                        reld[:].unsqueeze(2).to_broadcast([128, 2 * REL, HEADS]), ALU.mult).then_inc(relbd_ready, 1)
                dve.wait_ge(g_ready, 3)
                nc.vector.tensor_copy(g_n[:], CX[0:NS, 0:CHANNELS]).then_inc(g_copied, 1)
                nc.vector.tensor_copy(g_t[:, 0, :], MS[:, 0:NS]).then_inc(g_copied, 1)
                nc.vector.tensor_copy(g_t[:, 1, :], ST[:, 0, 0:NS]).then_inc(g_copied, 1)
                dve.wait_ge(g_copied, 3)

            @block.tensor
            def _(pe):
                pe.wait_ge(setup_in, 15 * 16)
                pe.wait_ge(relbd_ready, PAIRS)
                for dst, lhs, rhs in ((CX[0:NS, 0:CHANNELS], lambda q: relbd[:, q, :], lambda q: wq[:, q, :]),
                                      (MS[:, 0:NS], lambda q: wq[:, q, 0:128], lambda q: relbd[:, q, :]),
                                      (ST[:, 0, 0:NS], lambda q: wq[:, q, 128:256], lambda q: relbd[:, q, :])):
                    for q in range(PAIRS):
                        last = nc.tensor.matmul(dst, lhs(q), rhs(q), start=(q == 0), stop=(q == PAIRS - 1))
                    last.then_inc(g_ready, 1)

        setup.close()
        pass1(nc, t, locals())
        front.close()
        histogram_and_pass2(nc, t, locals())


def pass1(nc, t, e):
    fp32, bf16 = mybir.dt.float32, mybir.dt.bfloat16
    ALU, ACT, AX = mybir.AluOpType, mybir.ActivationFunctionType, mybir.AxisListType
    ds = bass.ds
    sb, sem = e["sb"], e["sem"]
    PJ, GN, ST, CX, MS = e["PJ"], e["GN"], e["ST"], e["CX"], e["MS"]
    wq, wout, g_t, affine, ustat = (e[k] for k in ("wq", "wout", "g_t", "affine", "ustat"))
    group_mean, swap_half, both_halves = e["group_mean"], e["swap_half"], e["both_halves"]
    s_dram, sp_dram, tp_dram, bad_dram, a_dram, p_dram, keys_dram = (
        e[k] for k in ("s_dram", "sp_dram", "tp_dram", "bad_dram", "a_dram", "p_dram", "keys_dram"))
    pc_dram, x_dram, cand_dram = e["pc_dram"], e["x_dram"], e["cand_dram"]
    VY = e["VY"]
    HY = YL // 2
    NST = 8
    SLOTS = 4

    with ExitStack() as own:
        xr = sb(own, "xr", [128, CT, PIX])
        xn = sb(own, "xn", [128, CT, PIX])
        kv = sb(own, "kv", [128, YL, 256])
        band = [sb(own, "band0", [128, HY, 2, 2, SIDE]), sb(own, "band1", [128, HY, 2, 2, SIDE])]
        ptile = sb(own, "ptile", [128, SLOTS, 512])
        srow = sb(own, "srow", [GENK, 2, 2, YL, SIDE], bf16)
        wkv = sb(own, "wkv", [128, CT, PAIRS, 256])
        strip = sb(own, "strip", [GENK, 2, STRIP], bf16)
        bad_mask = sb(own, "bad_mask", [NS, EDGE])
        good_mask = sb(own, "good_mask", [NS, EDGE])
        tt = sb(own, "tt", [128, TAPS, 4, SIDE])
        sbad = sb(own, "sbad", [NS, SIDE, EDGE])
        bnst = sb(own, "bnst", [128, CT, 8, 6])
        ybn = sb(own, "ybn", [128, 16, 6])
        mvy = sb(own, "mvy", [128, 2])
        mv = sb(own, "mv", [128, CT, 2])
        tmp2 = sb(own, "tmp2", [128, CT])
        tmp3 = sb(own, "tmp3", [128, CT])
        mxq = sb(own, "mxq", [128, 4, 128])
        mx = sb(own, "mx", [128, 128])
        mxx = sb(own, "mxx", [128, 128])
        rz = sb(own, "rz", [128, 128])
        ctxbd = sb(own, "ctxbd", [128, 128])
        fmat = sb(own, "fmat", [128, CHANNELS])
        amat = sb(own, "amat", [128, CT * CHANNELS])
        pc = sb(own, "pc", [PROWS, CHUNK, 4])
        ptb = sb(own, "pt", [128, 6, CHUNK])
        pt = ptb[0:PROWS]
        top24 = sb(own, "top24", [PROWS, TOP])

        flat = xr[:].rearrange("p c f -> p (c f)")
        QW = 4 * SIDE
        stile = flat[0:NS, 0:PIX].rearrange("p (a l x) -> p a l x", a=2, x=SIDE)
        sy = flat[:, 2 * PIX - 2 * REL * QW:].rearrange("p (k l x) -> p k l x", l=4, x=SIDE)
        RS = PARTS * REL * QW // 2
        s_parts = flat[:, 0:RS].bitcast(bf16).rearrange("p (a f) -> p a f", a=PARTS)
        s_rest = flat[:, RS:RS + REL * QW]
        TW = TAPS * QW // 2
        t_at = [2 * PIX - 2 * REL * QW, 2 * PIX - 2 * REL * QW + TW, RS]
        t_parts = [flat[:, o:o + TW].bitcast(bf16) for o in t_at]
        t_view = lambda a, h: t_parts[a].rearrange("p (k l x) -> p k l x", l=4, x=SIDE)[:, :, 2 * h:2 * h + 2, :]
        prod = [ptb[:].rearrange("p k c -> p (k c)")[:, 0:REL * QW // 2].rearrange("p (k l x) -> p k l x", l=2, x=SIDE),
                ptile[:].rearrange("p k c -> p (k c)")[:, 0:REL * QW // 2].rearrange("p (k l x) -> p k l x", l=2, x=SIDE)]

        counted = ("x_in bn_done mvp_ready gstat_mm var_ready std_ready xn_ready s_mm s_act s_dve s_out bad_out "
                   "s_cast s_sub t_sum_dve t_sum_pool t_cast0 t_cast1 sp_out tp_out s_back0 s_back1 t_back0 t_back1 pj_mm kv_evac gen_mm gen_act gen_dve "
                   "y_mm y_stat p_mm p_head0 p_head1 p_out0 p_out1 p_out2 p_out3 "
                   "max_ready swap_mm shift_ready sub_done exp_done zsum_ready zsum_mm rz_ready norm_done ctx_mm ctx_copied "
                   "f_mm f_copied a_mm a_copied a_out pts_in key_ready key_out top_ready top_out unit_read dve_step pool_step").split()
        S = {n: sem(n) for n in counted + ["w_in", "sy_in", "zeroed", "strip_ready", "apart", "pool_apart", "credited"]}
        starts_at_one = [S[n] for n in counted]
        G = type("Sems", (), S)
        p_out = [G.p_out0, G.p_out1, G.p_out2, G.p_out3]
        s_back, t_back = [G.s_back0, G.s_back1], [G.t_back0, G.t_back1]

        def per(img, each, n):
            return img * each + n + 1

        with nc.Block() as block:
            @block.sync
            def _(sp):
                for s in starts_at_one:
                    sp.sem_inc(s, 1)
                sp.sem_inc(G.credited, 1)
                sp.wait_ge(G.credited, 1)

        ORDER = {False: ("s0", "s1", "y0", "t0", "y1", "t1", "p0", "p1"),
                 True: ("s0", "s1", "y0", "y1", "t0", "t1", "p0", "p1")}
        JOB = ("s0", "s1", "t0", "t1")
        GNR = [GN[:, 0, :], GN[:, 1, :], PJ[:, 0, :]]
        STR = [ST[:, 0, :], ST[:, 1, :], PJ[:, 1, :]]
        MAX_CUT = (0, 12, 22, 30, 32)
        CAST_AT = (0, 2, 4)
        T_AT = {13: (0, 0), 14: (0, 1), 15: (1, 0)}
        SUM_AT = (0, 2, 4, 6)
        ZSUM_AT = 9
        BOTH_AT = (0, 2, 4, 6, 8, 10)
        DVE_STEPS = 197

        OWNER = "AADADADD" + "DA" * 12

        def owned(g):
            return OWNER[:g + 1].count(OWNER[g])

        def free_band(eng, img, q, job):
            if job[0] == "s":
                eng.wait_ge(G.p_mm, per(img, 64, 16 * q))
            else:
                eng.wait_ge(G.y_mm, per(img, 64, 16 * q + 8 * int(job[1]) + 8))

        with nc.Block() as block:
            @block.sync
            def _(sp):
                sp.dma_start(wkv[:], t["w_kv_t"].rearrange("(t p) q f -> p t q f", p=128)).then_inc(G.w_in, 16)
                sp.dma_start(band[0][0:GENK].rearrange("p l n a x -> p (l n a x)")[:, 0:2 * STRIP], t["strip"]).then_inc(G.w_in, 16)
                sp.dma_start(bad_mask[:], t["bad_mask"]).then_inc(G.w_in, 16)
                sp.dma_start(good_mask[:], t["good_mask"]).then_inc(G.w_in, 16)
                sp.wait_ge(G.zeroed, 3)

                def load_image(img):
                    for c in range(CT):
                        sp.dma_start(xr[:, c, :], x_dram[ds(img, 1), :, c, :].rearrange("b p f -> (b p) f")).then_inc(G.x_in, 16)

                def load_rows(img, q, kind, half):
                    dram, rows, row0 = ((sp_dram, PARTS * REL, 0), (tp_dram, PARTS * TAPS, SROWS))[kind]
                    for y2 in range(2):
                        at = y2 * (PIX // 2) + half * (PIX // 4)
                        src = dram[ds(img, 1), :, :, 2 * q:2 * q + 2, at:at + PIX // 4].rearrange("b a k n f -> (b a k) n f")
                        sp.dma_start(srow[row0 + rows * y2:row0 + rows * (y2 + 1), :, y2, HY * half:HY * (half + 1), :]
                                     .rearrange("p n l x -> p n (l x)"), src).then_inc((s_back, t_back)[kind][half], 16)

                def s_out(img):
                    for h in range(2):
                        sp.wait_ge(G.s_act, per(img, NST, 4 * h + 4))
                        sp.wait_ge(G.s_dve, per(img, NST, 4 * h + 4))
                        sp.dma_start(s_dram[ds(img, 1), :, :].rearrange("b s (a l f) -> (b s) a l f", a=2, l=2)[:, :, h, :],
                                     stile[:, :, HY * h:HY * (h + 1), :].rearrange("p a l x -> p a (l x)")).then_inc(G.s_out, 16)
                    sp.dma_start(bad_dram[ds(img, 1), :, :].rearrange("b s f -> (b s) f"),
                                 sbad[:].rearrange("p y x -> p (y x)")).then_inc(G.bad_out, 16)

                def keys_out(img, c):
                    sp.wait_ge(G.key_ready, per(img, PAIRS, c + 1))
                    sp.dma_start(keys_dram[:, ds((img * PAIRS + c) * CHUNK + BLOCKS * SET, CHUNK)],
                                 pt[:, 5, :]).then_inc(G.key_out, 16)
                    sp.wait_ge(G.top_ready, per(img, PAIRS, c + 1))
                    sp.dma_start(cand_dram[:, ds((img * PAIRS + c) * TOP, TOP)], top24[:]).then_inc(G.top_out, 16)

                def points_in(img, c):
                    sp.wait_ge(G.unit_read, per(img, PAIRS, c))
                    sp.dma_start(pc[:].rearrange("p k c -> p (k c)"),
                                 pc_dram[:, ds((img * PAIRS + c) * (4 * CHUNK), 4 * CHUNK)]).then_inc(G.pts_in, 16)

                def image(img, last):
                    for a in range(PARTS):
                        sp.wait_ge(G.s_cast, per(img, PARTS, a + 1))
                        sp.dma_start(sp_dram[ds(img, 1), a, :, :, :].rearrange("b k n (c f) -> (b n c) k f", c=16),
                                     s_parts[:, a, :].rearrange("p (k f) -> p k f", k=REL)).then_inc(G.sp_out, 16)
                    sp.wait_ge(G.sp_out, per(img, 48, 48))
                    sp.wait_ge(G.gen_mm, per(img, 128, 0))
                    for h in range(2):
                        load_rows(img, 0, 0, h)
                    for a in range(PARTS):
                        sp.wait_ge(G.t_cast0, per(img, PARTS, a + 1))
                        sp.wait_ge(G.t_cast1, per(img, PARTS, a + 1))
                        sp.dma_start(tp_dram[ds(img, 1), a, :, :, :].rearrange("b k n (c f) -> (b n c) k f", c=16),
                                     t_parts[a].rearrange("p (k f) -> p k f", k=TAPS)).then_inc(G.tp_out, 16)
                    sp.wait_ge(G.tp_out, per(img, 48, 48))
                    for h in range(2):
                        load_rows(img, 0, 1, h)
                    if not last:
                        load_image(img + 1)
                    for q in range(PAIRS):
                        if q == 0:
                            points_in(img, 0)
                        if q == 2:
                            points_in(img, 3)
                            keys_out(img, 2)
                        for h in range(2):
                            if q + 1 < PAIRS:
                                sp.wait_ge(G.gen_mm, per(img, 128, 32 * q + 8 * (JOB.index("t0") + h + 1)))
                                load_rows(img, q + 1, 0, h)
                                load_rows(img, q + 1, 1, h)
                        if q == PAIRS - 1 and not last:
                            s_out(img + 1)
                        for k in range(8):
                            m = 8 * q + k
                            sp.wait_ge(G.p_head0, per(img, 64, 2 * m + 2))
                            sp.wait_ge(G.p_head1, per(img, 64, 2 * m + 2))
                            sp.dma_start(p_dram[ds(img, 1), q, :, 512 * k:512 * (k + 1)].rearrange("b p f -> (b p) f"),
                                         ptile[:, m % SLOTS, :]).then_inc(p_out[m % SLOTS], 16)
                        if q < 2:
                            points_in(img, q + 1)
                        if q < 3:
                            keys_out(img, (0, 1, 3)[q])
                    sp.wait_ge(G.a_copied, per(img, PAIRS, PAIRS))
                    sp.dma_start(a_dram[ds(img, 1), :, :].rearrange("b p f -> (b p) f"), amat[:]).then_inc(G.a_out, 16)

                load_image(0)
                s_out(0)
                with sp.Fori(0, IMAGES - 1) as img:
                    image(img, False)
                image(IMAGES - 1, True)
                for done, each in ((G.a_out, 16), (G.bad_out, 16), (G.key_out, 16 * PAIRS), (G.top_out, 16 * PAIRS),
                                   *((p, 8 * 16) for p in p_out)):
                    sp.wait_ge(done, per(IMAGES, each, 0))

            @block.gpsimd
            def _(pool):
                steps = [0]
                TSTEPS = 12

                def link(ins, img):
                    steps[0] += 1
                    ins.then_inc(G.pool_step, 1)
                    pool.wait_ge(G.pool_step, per(img, TSTEPS, steps[0]))

                nc.gpsimd.memset(srow[:, 0, :, :, :], 0.0).then_inc(G.zeroed, 1)
                nc.gpsimd.memset(srow[:, 1, :, :, :], 0.0).then_inc(G.zeroed, 1)
                nc.gpsimd.memset(ctxbd[:], 0.0).then_inc(G.zeroed, 1)

                def s_back_in(idx):
                    pool.wait_ge(G.s_out, per(idx, 32, 32))
                    for kind in range(2):
                        src = s_dram[ds(idx, 1), kind * REL * HEADS:(kind + 1) * REL * HEADS, :]
                        pool.dma_start(sy[:, REL * kind:REL * (kind + 1), :, :].rearrange("p k l x -> p k (l x)"),
                                       src.rearrange("b (k n) (c f) -> (b n c) k f", n=HEADS, c=16)).then_inc(G.sy_in, 16)

                def image(img, last):
                    steps[0] = 0
                    own_tt = tt[:, :, 2:4, :]
                    pool.wait_ge(G.sy_in, img * 32 + 32)
                    pool.wait_ge(G.tp_out, per(img, 48, 0))
                    pool.wait_ge(G.p_out0, per(img, 128, 0))
                    pool.wait_ge(G.p_out1, per(img, 128, 0))
                    pool.sem_inc(G.pool_apart, 1)
                    nc.gpsimd.memset(own_tt[:, REL:], 0.0)
                    link(nc.gpsimd.tensor_tensor(own_tt[:, 0:REL], sy[:, 0:REL, 2:4, :],
                                                 sy[:, REL, 2:4, :].unsqueeze(1).to_broadcast([128, REL, 2, SIDE]), ALU.mult), img)
                    for r2 in range(1, REL):
                        w = SIDE - r2
                        link(nc.gpsimd.tensor_tensor(prod[1][:, :, :, 0:w], sy[:, 0:REL, 2:4, r2:],
                                                     sy[:, REL + r2, 2:4, 0:w].unsqueeze(1).to_broadcast([128, REL, 2, w]), ALU.mult), img)
                        add = nc.gpsimd.tensor_tensor(own_tt[:, r2:r2 + REL, :, 0:w], own_tt[:, r2:r2 + REL, :, 0:w],
                                                      prod[1][:, :, :, 0:w], ALU.add)
                        if r2 < REL - 1:
                            link(add, img)
                        else:
                            add.then_inc(G.t_sum_pool, 1)
                    assert steps[0] == TSTEPS
                    for a in range(2):
                        pool.wait_ge(G.t_sum_pool, per(img, 3, a + 1))
                        pool.wait_ge(G.t_cast1, per(img, PARTS, a + 1))
                        nc.gpsimd.tensor_tensor(own_tt, own_tt, t_view(a, 1),
                                                ALU.subtract).then_inc(G.t_sum_pool, 1)
                    for q in range(PAIRS):
                        pool.wait_ge(G.shift_ready, per(img, PAIRS, q + 1))
                        for b in range(4):
                            k4 = kv[:, 8 * b:8 * b + 8, 0:128]
                            nc.gpsimd.tensor_tensor(k4, k4, mxx[:].unsqueeze(1).to_broadcast([128, 8, 128]),
                                                    ALU.subtract).then_inc(G.sub_done, 1)
                        if q == PAIRS - 1 and not last:
                            s_back_in(img + 1)
                        pool.wait_ge(G.rz_ready, per(img, PAIRS, q + 1))
                        for b in range(4):
                            k4 = kv[:, 8 * b:8 * b + 8, 0:128]
                            nc.gpsimd.tensor_tensor(k4, k4, rz[:].unsqueeze(1).to_broadcast([128, 8, 128]),
                                                    ALU.mult).then_inc(G.norm_done, 1)

                s_back_in(0)
                with pool.Fori(0, IMAGES - 1) as img:
                    image(img, False)
                image(IMAGES - 1, True)

            @block.scalar
            def _(act):
                act.wait_ge(G.w_in, 64)
                nc.scalar.activation(strip[:].rearrange("p k x -> p (k x)"),
                                     band[0][0:GENK].rearrange("p l n a x -> p (l n a x)")[:, 0:2 * STRIP], ACT.Copy).then_inc(G.strip_ready, 1)

                def root(idx):
                    act.wait_ge(G.var_ready, per(idx, 1, 1))
                    nc.scalar.activation(tmp3[:], tmp2[:], ACT.Sqrt).then_inc(G.std_ready, 1)

                def normalise(idx):
                    act.wait_ge(G.bn_done, per(idx, 1, 1))
                    nc.scalar.activation(xn[:, 1, :].rearrange("p (y x) -> p y x", x=SIDE),
                                         xr[:, 1, :].rearrange("p (x y) -> p y x", y=SIDE), ACT.Identity,
                                         bias=mv[:, 1, 1:2], scale=mv[:, 1, 0:1]).then_inc(G.xn_ready, 1)

                def gen_tiles(img, q, job):
                    free_band(act, img, q, job)
                    for k in range(8):
                        g = 8 * JOB.index(job) + k
                        if OWNER[g] != "A":
                            continue
                        act.wait_ge(G.gen_mm, per(img, 128, 32 * q + g + 1))
                        nc.scalar.activation(
                            band[int(job[1])][:, :, :, :, 8 * k:8 * k + 8].rearrange("p l n a x -> p (n a) l x"),
                            GNR[g % 3].rearrange("p (x m l) -> p m l x", x=8, l=HY), ACT.Copy).then_inc(G.gen_act, 1)

                def s_part(img, a):
                    if a == 0:
                        act.wait_ge(G.sy_in, img * 32 + 32)
                        src = sy[:, 0:REL, :, :].rearrange("p k l x -> p (k l x)")
                    else:
                        act.wait_ge(G.s_sub, per(img, 2, a))
                        src = s_rest
                    nc.scalar.activation(s_parts[:, a, :], src, ACT.Copy).then_inc(G.s_cast, 1)

                def t_part(img, a, h):
                    act.wait_ge([G.t_sum_dve, G.t_sum_pool][h], per(img, 3, a + 1))
                    if a == 0:
                        act.wait_ge([G.t_sum_dve, G.t_sum_pool][1 - h], per(img, 3, 1))
                    nc.scalar.activation(t_view(a, h), tt[:, :, 2 * h:2 * h + 2, :], ACT.Copy).then_inc([G.t_cast0, G.t_cast1][h], 1)

                def exps(img, q, bs):
                    for b in bs:
                        act.wait_ge(G.sub_done, per(img, 16, 4 * q + b + 1))
                        nc.scalar.activation(kv[:, 8 * b:8 * b + 8, 0:128], kv[:, 8 * b:8 * b + 8, 0:128],
                                             ACT.Exp).then_inc(G.exp_done, 1)

                def s_tiles(img):
                    for k in range(NST):
                        act.wait_ge(G.s_mm, per(img, NST, k + 1))
                        nc.scalar.activation(stile[:, :, 4 * k:4 * k + 4, :].rearrange("p a l x -> p l a x"),
                                             ST[0:NS, k % 2, :].rearrange("p (l a x) -> p l a x", l=4, a=2),
                                             ACT.Copy).then_inc(G.s_act, 1)

                def image(img, last):
                    for q in range(PAIRS):
                        act.wait_ge(G.ctx_mm, per(img, PAIRS, q))
                        for k in range(16):
                            act.wait_ge(G.pj_mm, per(img, 64, 16 * q + k + 1))
                            nc.scalar.activation(kv[:, 2 * k:2 * k + 2, :].rearrange("p l f -> p (l f)"),
                                                 PJ[:, k % 2, :], ACT.Copy).then_inc(G.kv_evac, 1)
                            if q == 0 and k in CAST_AT:
                                s_part(img, CAST_AT.index(k))
                            if q == 0 and k in T_AT:
                                t_part(img, *T_AT[k])
                            if q == PAIRS - 1 and k == 14 and not last:
                                root(img + 1)
                        done = 0
                        for job in ORDER[q == 0]:
                            if job in JOB:
                                gen_tiles(img, q, job)
                                if q == 0 and job == "s0":
                                    t_part(img, 1, 1)
                                if q == 0 and job == "s1":
                                    t_part(img, 2, 0)
                                    t_part(img, 2, 1)
                                if q == PAIRS - 1 and job == "s1" and not last:
                                    act.wait_ge(G.pj_mm, per(img, 64, 64))
                                    normalise(img + 1)
                            elif job[0] == "y":
                                exps(img, q, (2 * int(job[1]), 2 * int(job[1]) + 1))
                                if q == PAIRS - 1 and job == "y1" and not last:
                                    s_tiles(img + 1)
                            else:
                                for k in range(8):
                                    n = 8 * int(job[1]) + k
                                    m = 8 * q + n // 2
                                    act.wait_ge(G.p_mm, per(img, 64, 16 * q + n + 1))
                                    if n in BOTH_AT and n > 0:
                                        act.wait_ge(G.p_head1, per(img, 64, 16 * q + n))
                                    act.wait_ge(p_out[m % SLOTS], per(img, 128, 16 * (m // SLOTS)))
                                    nc.scalar.activation(ptile[0:64, m % SLOTS, 256 * (n % 2):256 * (n % 2) + 256],
                                                         STR[(16 + n) % 3][0:64, 0:256], ACT.Copy).then_inc(G.p_head0, 1)
                                    if n in BOTH_AT:
                                        nc.scalar.activation(ptile[64:128, m % SLOTS, 256 * (n % 2):256 * (n % 2) + 256],
                                                             STR[(16 + n) % 3][64:128, 256:512], ACT.Copy).then_inc(G.p_head1, 1)

                root(0)
                normalise(0)
                s_tiles(0)
                with act.Fori(0, IMAGES - 1) as img:
                    image(img, False)
                image(IMAGES - 1, True)

            @block.tensor
            def _(pe):
                pe.wait_ge(G.w_in, 64)
                pe.wait_ge(G.strip_ready, 1)
                pe.wait_ge(G.zeroed, 3)

                def moments(idx):
                    pe.wait_ge(G.mvp_ready, per(idx, 1, 1))
                    nc.tensor.matmul(MS[:, 0:2 * CT], group_mean[:], mv[:].rearrange("p t k -> p (t k)"),
                                     start=True, stop=True).then_inc(G.gstat_mm, 1)

                def gen(img, q, job):
                    half, rank = int(job[1]), JOB.index(job)
                    kind = 0 if job[0] == "s" else 1
                    K = SROWS if kind == 0 else GENK
                    pe.wait_ge(s_back[half], per(img, 32 * PAIRS, 32 * (q + 1)))
                    if kind == 1:
                        pe.wait_ge(t_back[half], per(img, 32 * PAIRS, 32 * (q + 1)))
                    for k in range(8):
                        g = 8 * rank + k
                        if g >= 3:
                            pe.wait_ge(G.gen_act if OWNER[g - 3] == "A" else G.gen_dve, per(img, 64, 16 * q + owned(g - 3)))
                        elif g == 2:
                            pe.wait_ge(G.kv_evac, per(img, 64, 16 * q + 16))
                        for j in range(8):
                            x = 8 * k + j
                            last = nc.tensor.matmul(
                                GNR[g % 3][:, 64 * j:64 * j + 64],
                                strip[0:K, kind, SIDE - 1 - x:3 * SIDE - 1 - x],
                                srow[0:K, :, :, HY * half:HY * (half + 1), x].rearrange("p n a l -> p (n a) l"), start=True, stop=True)
                        last.then_inc(G.gen_mm, 1)

                def band_stands(img, q, job):
                    pe.wait_ge(G.gen_act, per(img, 64, 16 * q + 4 * JOB.index(job) + 4))
                    pe.wait_ge(G.gen_dve, per(img, 64, 16 * q + 4 * JOB.index(job) + 4))

                def stage(u, half, k):
                    for j in range(2):
                        yl = 2 * k + j
                        last = nc.tensor.matmul(
                            STR[u % 3].rearrange("p (n l f) -> p l n f", n=2, l=2)[:, j],
                            kv[:, HY * half + yl, 128:256],
                            band[half][:, yl, :, :, :].rearrange("p n a x -> p (n a x)"), start=True, stop=True)
                    return last

                def flush_f(img, q):
                    pe.wait_ge(G.ctx_copied, per(img, 2 * PAIRS, 2 * q + 2))
                    nc.tensor.matmul(MS[:, 256:512], ctxbd[:], wout[:, q, :], start=True, stop=True).then_inc(G.f_mm, 1)

                def flush_a(img, q):
                    pe.wait_ge(G.f_copied, per(img, PAIRS, q + 1))
                    for c in range(CT):
                        last = nc.tensor.matmul(CX[:, 256 * c:256 * c + 256], wq[:, q, 128 * c:128 * c + 128],
                                                fmat[:], start=True, stop=True)
                    last.then_inc(G.a_mm, 1)

                def s_tiles(idx):
                    pe.wait_ge(G.xn_ready, per(idx, CT, CT))
                    for k in range(NST):
                        if k >= 2:
                            pe.wait_ge(G.s_act, per(idx, NST, k - 1))
                        for c in range(CT):
                            last = nc.tensor.matmul(ST[0:NS, k % 2, :], g_t[:, c, :], xn[:, c, 512 * k:512 * k + 512],
                                                    start=(c == 0), stop=(c == CT - 1))
                        last.then_inc(G.s_mm, 1)

                def image(img, last_image):
                    for q in range(PAIRS):
                        for k in range(16):
                            if k == 0:
                                for left in (G.gen_act, G.gen_dve, G.p_head0, G.p_head1):
                                    pe.wait_ge(left, per(img, 64, 16 * q))
                            elif k >= 2:
                                pe.wait_ge(G.kv_evac, per(img, 64, 16 * q + k - 1))
                            for j in range(2):
                                yl = 2 * k + j
                                for c in range(CT):
                                    last = nc.tensor.matmul(PJ[:, k % 2, 256 * j:256 * j + 256],
                                                            xn[:, c, 128 * yl:128 * yl + 128], wkv[:, c, q, :],
                                                            start=(c == 0), stop=(c == CT - 1))
                            last.then_inc(G.pj_mm, 1)
                            if q > 0 and k == 3:
                                flush_f(img, q - 1)
                            if q > 0 and k == 7:
                                flush_a(img, q - 1)
                            if q == PAIRS - 1 and k == 12 and not last_image:
                                moments(img + 1)
                        for job in ORDER[q == 0]:
                            half = int(job[1])
                            if job in JOB:
                                gen(img, q, job)
                                if job == "s0":
                                    pe.wait_ge(G.max_ready, per(img, PAIRS, q + 1))
                                    nc.tensor.matmul(MS[:, 0:128], swap_half[:], mx[:], start=True, stop=True).then_inc(G.swap_mm, 1)
                            elif job[0] == "y":
                                band_stands(img, q, "s%d" % half)
                                if half == 0:
                                    pe.wait_ge(G.kv_evac, per(img, 64, 16 * q + 16))
                                for k in range(8):
                                    n = 8 * half + k
                                    if n >= 3:
                                        pe.wait_ge(G.y_stat, per(img, 64, 16 * q + n - 2))
                                    elif q == 0:
                                        pe.wait_ge(G.s_act, per(img, NST, NST))
                                    stage(n, half, k).then_inc(G.y_mm, 1)
                                if q == PAIRS - 1 and half == 1 and not last_image:
                                    pe.wait_ge(G.y_stat, per(img, 64, 64))
                                    s_tiles(img + 1)
                            else:
                                band_stands(img, q, "t%d" % half)
                                for k in range(8):
                                    n = 8 * half + k
                                    if n >= 3:
                                        pe.wait_ge(G.p_head0, per(img, 64, 16 * q + n - 2))
                                        pe.wait_ge(G.p_head1, per(img, 64, 16 * q + n - 2))
                                    else:
                                        pe.wait_ge(G.y_stat, per(img, 64, 16 * q + 14 + n))
                                        if q == PAIRS - 1 and n == 0 and not last_image:
                                            pe.wait_ge(G.s_act, per(img + 1, NST, NST))
                                    stage(16 + n, half, k).then_inc(G.p_mm, 1)
                                    if n == ZSUM_AT:
                                        pe.wait_ge(G.zsum_ready, per(img, PAIRS, q + 1))
                                        nc.tensor.matmul(MS[:, 128:256], both_halves[:], mx[:], start=True, stop=True).then_inc(G.zsum_mm, 1)
                        for yl in range(YL):
                            if yl % 8 == 0:
                                pe.wait_ge(G.norm_done, per(img, 16, 4 * q + yl // 8 + 1))
                                if yl == 0:
                                    pe.wait_ge(G.a_copied, per(img, PAIRS, q))
                            last = nc.tensor.matmul(CX[:, 0:128], kv[:, yl, 128:256], kv[:, yl, 0:128],
                                                    start=(yl == 0), stop=(yl == YL - 1))
                        last.then_inc(G.ctx_mm, 1)
                    flush_f(img, PAIRS - 1)
                    flush_a(img, PAIRS - 1)

                moments(0)
                s_tiles(0)
                with pe.Fori(0, IMAGES - 1) as img:
                    image(img, False)
                image(IMAGES - 1, True)

            @block.vector
            def _(dve):
                steps = [0]
                now = [0]
                first = [0]

                def link(ins):
                    steps[0] += 1
                    ins.then_inc(G.dve_step, 1)
                    dve.wait_ge(G.dve_step, per(now[0], DVE_STEPS, first[0] + steps[0]))

                def apart():
                    dve.sem_inc(G.apart, 1)

                def gen_tiles(img, q, job):
                    free_band(dve, img, q, job)
                    for k in range(8):
                        g = 8 * JOB.index(job) + k
                        if OWNER[g] != "D":
                            continue
                        dve.wait_ge(G.gen_mm, per(img, 128, 32 * q + g + 1))
                        nc.vector.tensor_copy(
                            band[int(job[1])][:, :, :, :, 8 * k:8 * k + 8].rearrange("p l n a x -> p (n a) l x"),
                            GNR[g % 3].rearrange("p (x m l) -> p m l x", x=8, l=HY)).then_inc(G.gen_dve, 1)

                def stats(idx):
                    dve.wait_ge(G.x_in, per(idx, 32, 32))
                    for c in range(CT):
                        for k in range(8):
                            apart()
                            last = nc.vector.bn_stats(bnst[:, c, k, :], xr[:, c, 512 * k:512 * k + 512])
                    link(last)
                    apart()
                    nc.vector.bn_aggr(mv[:, 0, :], bnst[:, 0, :, :].rearrange("p k s -> p (k s)"))
                    link(nc.vector.bn_aggr(mv[:, 1, :], bnst[:, 1, :, :].rearrange("p k s -> p (k s)")))
                    link(nc.vector.tensor_tensor(tmp2[:], mv[:, :, 0], mv[:, :, 0], ALU.mult))
                    link(nc.vector.tensor_tensor(mv[:, :, 1], mv[:, :, 1], tmp2[:], ALU.add))
                    nc.vector.sem_inc(G.mvp_ready, 1)

                def variance(idx):
                    dve.wait_ge(G.gstat_mm, per(idx, 1, 1))
                    link(nc.vector.tensor_copy(mv[:].rearrange("p t k -> p (t k)"), MS[:, 0:2 * CT]))
                    link(nc.vector.tensor_tensor(tmp2[:], mv[:, :, 0], mv[:, :, 0], ALU.mult))
                    link(nc.vector.tensor_tensor(tmp2[:], mv[:, :, 1], tmp2[:], ALU.subtract))
                    link(nc.vector.tensor_scalar(tmp2[:], tmp2[:], 0.0, GN_EPS, ALU.max, ALU.add))
                    nc.vector.sem_inc(G.var_ready, 1)

                def scale_bias(idx):
                    dve.wait_ge(G.std_ready, per(idx, 1, 1))
                    link(nc.vector.reciprocal(tmp3[:], tmp3[:]))
                    link(nc.vector.tensor_tensor(tmp2[:], mv[:, :, 0], tmp3[:], ALU.mult))
                    nc.vector.tensor_scalar(mv[:, :, 1], tmp2[:], -1.0, None, ALU.mult)
                    link(nc.vector.tensor_copy(mv[:, :, 0], tmp3[:]))
                    link(nc.vector.tensor_copy(affine[:, ds(idx, 1), :, :].rearrange("p b t k -> p (b t k)"),
                                               mv[:].rearrange("p t k -> p (t k)")))
                    nc.vector.sem_inc(G.bn_done, 1)

                def normalise():
                    nc.vector.tensor_scalar(xn[:, 0, :].rearrange("p (y x) -> p y x", x=SIDE),
                                            xr[:, 0, :].rearrange("p (x y) -> p y x", y=SIDE),
                                            mv[:, 0, 0:1], mv[:, 0, 1:2], ALU.mult, ALU.add).then_inc(G.xn_ready, 1)

                def s_edges(img):
                    dve.wait_ge(G.bad_out, per(img, 16, 0))
                    for k in range(NST):
                        dve.wait_ge(G.s_act, per(img, NST, k + 1))
                        edge = stile[:, :, 4 * k:4 * k + 4, SIDE - EDGE:].rearrange("p a l x -> p l a x")
                        link(nc.vector.tensor_tensor(
                            sbad[:, 8 * k:8 * k + 8, :].rearrange("p (l a) x -> p l a x", a=2), edge,
                            bad_mask[:].unsqueeze(1).unsqueeze(1).to_broadcast([NS, 4, 2, EDGE]), ALU.mult))
                        nc.vector.tensor_tensor(
                            edge, edge,
                            good_mask[:].unsqueeze(1).unsqueeze(1).to_broadcast([NS, 4, 2, EDGE]), ALU.mult).then_inc(G.s_dve, 1)

                def t_product(r2):
                    w = SIDE - r2
                    if r2 == 0:
                        nc.vector.memset(tt[:, REL:, 0:2, :], 0.0)
                        link(nc.vector.tensor_tensor(tt[:, 0:REL, 0:2, :], sy[:, 0:REL, 0:2, :],
                                                     sy[:, REL, 0:2, :].unsqueeze(1).to_broadcast([128, REL, 2, SIDE]), ALU.mult))
                        return
                    link(nc.vector.tensor_tensor(prod[0][:, :, :, 0:w], sy[:, 0:REL, 0:2, r2:],
                                                 sy[:, REL + r2, 0:2, 0:w].unsqueeze(1).to_broadcast([128, REL, 2, w]), ALU.mult))
                    sum_ = tt[:, r2:r2 + REL, 0:2, 0:w]
                    link(nc.vector.tensor_tensor(sum_, sum_, prod[0][:, :, :, 0:w], ALU.add))

                def t_rest(img, a):
                    dve.wait_ge(G.t_cast0, per(img, PARTS, a + 1))
                    nc.vector.tensor_tensor(tt[:, :, 0:2, :], tt[:, :, 0:2, :], t_view(a, 0),
                                            ALU.subtract).then_inc(G.t_sum_dve, 1)

                def s_minus(img, a):
                    dve.wait_ge(G.s_cast, per(img, PARTS, a + 1))
                    if a == 1:
                        dve.wait_ge(G.s_sub, per(img, 2, 1))
                    src = sy[:, 0:REL, :, :].rearrange("p k l x -> p (k l x)") if a == 0 else s_rest
                    nc.vector.tensor_tensor(s_rest, src, s_parts[:, a, :], ALU.subtract).then_inc(G.s_sub, 1)

                def maxima(img, q, b):
                    dve.wait_ge(G.kv_evac, per(img, 64, 16 * q + MAX_CUT[b + 1] // 2))
                    return nc.vector.tensor_reduce(mxq[:, b, :], kv[:, MAX_CUT[b]:MAX_CUT[b + 1], 0:128].rearrange("p l c -> p c l"),
                                                   AX.X, ALU.max)

                def take_f(img, q):
                    dve.wait_ge(G.f_mm, per(img, PAIRS, q + 1))
                    nc.vector.tensor_copy(fmat[:], MS[:, 256:512]).then_inc(G.f_copied, 1)

                def take_a(img, q):
                    dve.wait_ge(G.a_mm, per(img, PAIRS, q + 1))
                    if q == 0:
                        dve.wait_ge(G.a_out, per(img, 16, 0))
                        nc.vector.tensor_copy(amat[:], CX[:]).then_inc(G.a_copied, 1)
                    else:
                        dve.wait_ge(G.a_copied, per(img, PAIRS, q))
                        nc.vector.tensor_tensor(amat[:], amat[:], CX[:], ALU.add).then_inc(G.a_copied, 1)

                def points_x(img, q):
                    dve.wait_ge(G.pts_in, per(img, 16 * PAIRS, 16 * (q + 1)))
                    dve.wait_ge(G.key_out, per(img, 16 * PAIRS, 16 * q))
                    link(nc.vector.tensor_scalar(pt[:, 0, :], pc[:, :, 0], -25.6, 5.0, ALU.subtract, ALU.mult))
                    link(nc.vector.tensor_scalar(pt[:, 1, :], pt[:, 0, :], MAGIC, MAGIC, ALU.add, ALU.subtract))
                    link(nc.vector.tensor_tensor(pt[:, 2, :], pt[:, 1, :], pt[:, 0, :], ALU.is_gt))
                    link(nc.vector.tensor_tensor(pt[:, 1, :], pt[:, 1, :], pt[:, 2, :], ALU.subtract))
                    link(nc.vector.tensor_scalar(pt[:, 5, :], pt[:, 1, :], float(2 * BLOCK), 1.0, ALU.mult, ALU.add))

                def points_axis(img, q, axis, low, high, inv, size, vox, cells):
                    vh = float(np.round(float(vox) * 2 ** 14) / 2 ** 14)
                    vl = float(np.float32(float(vox) - vh - float(vox) * 2.0 ** -24 * 0.75))
                    v = pc[:, :, axis]
                    nc.vector.tensor_scalar(pt[:, 1, :], v, low, None, ALU.subtract)
                    link(nc.vector.tensor_scalar(pt[:, 0, :], v, low, inv, ALU.subtract, ALU.mult))
                    link(nc.vector.tensor_scalar(pt[:, 2, :], pt[:, 0, :], MAGIC, MAGIC, ALU.add, ALU.subtract))
                    link(nc.vector.scalar_tensor_tensor(pt[:, 0, :], pt[:, 2, :], -vh, pt[:, 1, :], ALU.mult, ALU.add))
                    link(nc.vector.scalar_tensor_tensor(pt[:, 1, :], pt[:, 2, :], vl, pt[:, 0, :], ALU.mult, ALU.is_gt))
                    link(nc.vector.tensor_tensor(pt[:, 2, :], pt[:, 2, :], pt[:, 1, :], ALU.subtract))
                    link(nc.vector.tensor_scalar(pt[:, 2, :], pt[:, 2, :], float(size - 1), float(cells), ALU.min, ALU.mult))
                    link(nc.vector.tensor_tensor(pt[:, 5, :], pt[:, 5, :], pt[:, 2, :], ALU.add))
                    link(nc.vector.scalar_tensor_tensor(pt[:, 3, :], v, low, pt[:, 4, :], ALU.is_ge, ALU.mult))
                    link(nc.vector.scalar_tensor_tensor(pt[:, 4, :], v, high, pt[:, 3, :], ALU.is_lt, ALU.mult))

                def points_label(img, q):
                    link(nc.vector.tensor_scalar(pt[:, 0, :], pc[:, :, 3], 0.0, float(NL - 1), ALU.max, ALU.min))
                    link(nc.vector.tensor_scalar(pt[:, 1, :], pt[:, 0, :], MAGIC, MAGIC, ALU.add, ALU.subtract))
                    link(nc.vector.tensor_tensor(pt[:, 2, :], pt[:, 1, :], pt[:, 0, :], ALU.is_gt))
                    link(nc.vector.tensor_tensor(pt[:, 1, :], pt[:, 1, :], pt[:, 2, :], ALU.subtract))
                    link(nc.vector.tensor_tensor(pt[:, 5, :], pt[:, 5, :], pt[:, 1, :], ALU.add))
                    link(nc.vector.memset(pt[:, 4, :], 1.0))

                def points_top(img, q):
                    nc.vector.sem_inc(G.unit_read, 1)
                    link(nc.vector.tensor_tensor(pt[:, 5, :], pt[:, 5, :], pt[:, 4, :], ALU.mult))
                    link(nc.vector.scalar_tensor_tensor(pt[:, 0, :], pt[:, 5, :], float(NX * 2 * BLOCK), pt[:, 5, :],
                                                        ALU.is_le, ALU.mult))
                    link(nc.vector.tensor_scalar(pt[:, 5, :], pt[:, 0, :], 0.0, None, ALU.max))
                    nc.vector.sem_inc(G.key_ready, 1)
                    src = pt[:, 5, :]
                    dve.wait_ge(G.top_out, per(img, 16 * PAIRS, 16 * q))
                    for k in range(3):
                        apart()
                        link(nc.vector.max(top24[:, 8 * k:8 * k + 8], src))
                        if k < 2:
                            apart()
                            link(nc.vector.match_replace(pt[:, k, :], top24[:, 8 * k:8 * k + 8], src, 0.0))
                            src = pt[:, k, :]
                    nc.vector.sem_inc(G.top_ready, 1)

                def image(img, last):
                    now[0] = img
                    steps[0] = 0
                    for q in range(PAIRS):
                        if q == 0:
                            dve.wait_ge(G.sy_in, img * 32 + 32)
                            dve.wait_ge(G.tp_out, per(img, 48, 0))
                            apart()
                            t_product(0)
                            s_minus(img, 0)
                            t_product(1)
                            t_product(2)
                            s_minus(img, 1)
                            for r2 in range(3, REL):
                                t_product(r2)
                            nc.vector.sem_inc(G.t_sum_dve, 1)
                        for b in range(4):
                            last_max = maxima(img, q, b)
                            if q == 0 and b == 2:
                                t_rest(img, 0)
                            if q == PAIRS - 1 and not last:
                                if b == 0:
                                    variance(img + 1)
                                if b == 2:
                                    scale_bias(img + 1)
                        link(last_max)
                        nc.vector.tensor_reduce(mx[:], mxq[:].rearrange("p b c -> p c b"), AX.X, ALU.max).then_inc(G.max_ready, 1)
                        for job in ORDER[q == 0]:
                            if job in JOB:
                                gen_tiles(img, q, job)
                                if job == "s0":
                                    dve.wait_ge(G.swap_mm, per(img, PAIRS, q + 1))
                                    nc.vector.tensor_tensor(mxx[:], mx[:], MS[:, 0:128], ALU.max).then_inc(G.shift_ready, 1)
                                if q == 0 and job == "s0":
                                    t_rest(img, 1)
                                if q == PAIRS - 1 and job == "s1" and not last:
                                    dve.wait_ge(G.pj_mm, per(img, 64, 64))
                                    normalise()
                            elif job[0] == "y":
                                for k in range(8):
                                    n = 8 * int(job[1]) + k
                                    dve.wait_ge(G.y_mm, per(img, 64, 16 * q + n + 1))
                                    for h in range(2):
                                        apart()
                                        st = nc.vector.bn_stats(ybn[64 * h:64 * h + 64, n, :],
                                                                STR[n % 3][64 * h:64 * h + 64, 256 * h:256 * h + 256])
                                    st.then_inc(G.y_stat, 1)
                                if q == PAIRS - 1 and job == "y1" and not last:
                                    s_edges(img + 1)
                            else:
                                for k in range(8):
                                    n = 8 * int(job[1]) + k
                                    m = 8 * q + n // 2
                                    if n not in BOTH_AT:
                                        dve.wait_ge(G.p_mm, per(img, 64, 16 * q + n + 1))
                                        dve.wait_ge(p_out[m % SLOTS], per(img, 128, 16 * (m // SLOTS)))
                                        dve.wait_ge(G.p_head1, per(img, 64, 16 * q + n))
                                        nc.vector.tensor_copy(ptile[64:128, m % SLOTS, 256 * (n % 2):256 * (n % 2) + 256],
                                                              STR[(16 + n) % 3][64:128, 256:512]).then_inc(G.p_head1, 1)
                                    if n in SUM_AT:
                                        b = SUM_AT.index(n)
                                        dve.wait_ge(G.exp_done, per(img, 16, 4 * q + b + 1))
                                        part = nc.vector.tensor_reduce(
                                            mxq[:, b, :], kv[:, 8 * b:8 * b + 8, 0:128].rearrange("p l c -> p c l"), AX.X, ALU.add)
                                        if b == 3:
                                            link(part)
                                            nc.vector.tensor_reduce(mx[:], mxq[:].rearrange("p b c -> p c b"), AX.X, ALU.add)\
                                                .then_inc(G.zsum_ready, 1)
                                    if n == ZSUM_AT + 1:
                                        dve.wait_ge(G.zsum_mm, per(img, PAIRS, q + 1))
                                        nc.vector.reciprocal(rz[:], MS[:, 128:256]).then_inc(G.rz_ready, 1)
                        dve.wait_ge(G.y_stat, per(img, 64, 16 * q + 16))
                        apart()
                        link(nc.vector.bn_aggr(mvy[:], ybn[:].rearrange("p k s -> p (k s)")))
                        link(nc.vector.tensor_copy(ustat[:, ds(img * PAIRS + q, 1), :].rearrange("p u k -> p (u k)"), mvy[:]))
                        for piece in WINDOW[q]:
                            if piece is not next_stats or not last:
                                piece(img, q)

                def take_ctx(img, q):
                    dve.wait_ge(G.ctx_mm, per(img, PAIRS, q + 1))
                    for h in range(2):
                        nc.vector.tensor_copy(ctxbd[64 * h:64 * h + 64, 64 * h:64 * h + 64],
                                              CX[64 * h:64 * h + 64, 64 * h:64 * h + 64]).then_inc(G.ctx_copied, 1)

                def px(c):
                    return lambda img, q: (points_x(img, c), points_label(img, c))

                def py(c):
                    return lambda img, q: points_axis(img, c, 1, -25.6, 25.6, 5.0, NY, VY, ZL)

                def pz(c):
                    return lambda img, q: points_axis(img, c, 2, -2.0, float(np.float32(1.2)), 10.0, NZ, np.float32(0.1), NL)

                def top(c):
                    return lambda img, q: points_top(img, c)

                def next_stats(img, q):
                    stats(img + 1)

                WINDOW = ((px(0), py(0), take_ctx, pz(0), top(0), take_f, px(1), take_a, py(1)),
                          (pz(1), top(1), take_ctx, px(2), py(2), take_f, pz(2), take_a, top(2)),
                          (px(3), py(3), take_ctx, pz(3), top(3), take_f, next_stats, take_a),
                          (take_ctx, take_f, take_a))

                dve.wait_ge(G.w_in, 64)
                dve.wait_ge(G.zeroed, 3)
                stats(0)
                variance(0)
                scale_bias(0)
                normalise()
                s_edges(0)
                first[0] = steps[0]
                with dve.Fori(0, IMAGES - 1) as img:
                    image(img, False)
                    assert steps[0] == DVE_STEPS
                image(IMAGES - 1, True)


def histogram_and_pass2(nc, t, e):
    fp32, bf16, fp16, i32 = mybir.dt.float32, mybir.dt.bfloat16, mybir.dt.float16, mybir.dt.int32
    ALU, ACT, AX = mybir.AluOpType, mybir.ActivationFunctionType, mybir.AxisListType
    ds = bass.ds
    sb, sem = e["sb"], e["sem"]
    PJ, GN, ST, CX, MS = e["PJ"], e["GN"], e["ST"], e["CX"], e["MS"]
    block_lo, block_hi, cand_dram, keys_dram = e["block_lo"], e["block_hi"], e["cand_dram"], e["keys_dram"]
    SLOTS = NX + 2
    with ExitStack() as own:
        hist = sb(own, "hist", [128, SLOTS * 2 * HROW])

        with ExitStack() as tmp:
            cand = sb(tmp, "cand", [PROWS, NCHUNK, TOP])
            work = sb(tmp, "work", [PROWS, 2, NCHUNK * TOP])
            best = sb(tmp, "best", [PROWS, SET])
            sets = sb(tmp, "sets", [PROWS, BLOCKS, SET])
            over = sb(tmp, "over", [PROWS, 4])
            overb = sb(tmp, "overb", [PROWS, BLOCKS])
            ones = sb(tmp, "ones", [PROWS, 1])
            full = sb(tmp, "full", [1, 1])
            control = sb(tmp, "control", [1, 4], i32)
            kset = sb(tmp, "kset", [PROWS, 2, SET])
            rel = sb(tmp, "rel", [PROWS, SET])
            tq = sb(tmp, "tq", [PROWS, SET])
            yrow = sb(tmp, "yrow", [PROWS, 2, SET])
            zlab = sb(tmp, "zlab", [PROWS, 2, SET])
            index = sb(tmp, "index", [PROWS, ZL])
            index16 = sb(tmp, "index16", [PROWS, ZL], fp16)
            NG = SET // OHG
            ydist = sb(tmp, "ydist", [PROWS, OHG, 128])
            hoty = sb(tmp, "hoty", [PROWS, NG, OHG, 128], bf16)
            hotz = sb(tmp, "hotz", [PROWS, NG, OHG, ZL], bf16)
            names = ("idx_in apart sort_step flags_ready over_mm control_ready sets_ready sets_out set_in0 set_in1 set_read "
                     "hotz_ready hoty_pool hoty_act hoty_abs hot_used hist_mm hist_added hist_zero decode_step pool_apart").split()
            G = type("Sems", (), {n: sem("hist_" + n) for n in names})
            SORT = 1 + 2 * (SET // 8)
            INDEX_STEP = BLOCKS * SORT + 6
            DEC = 4

            def group_free(eng, it, g):
                if g < NG - 1:
                    eng.wait_ge(G.hot_used, it * (NG - 1) + g + 1)
                else:
                    eng.wait_ge(G.hist_mm, it + 1)

            PSUM = [PJ[:].rearrange("p b f -> p (b f)")[:, 0:ZL], GN[:].rearrange("p b f -> p (b f)")[:, 0:ZL]]

            with nc.Block() as block:
                @block.sync
                def _(sp):
                    sp.dma_start(cand[:].rearrange("p n k -> p (n k)"), cand_dram).then_inc(G.idx_in, 16)
                    sp.dma_start(index[:], t["index"][0:PROWS, :]).then_inc(G.idx_in, 16)
                    sp.wait_ge(G.sets_ready, 1)
                    sp.dma_start(keys_dram[:, 0:BLOCKS * SET], sets[:].rearrange("p b k -> p (b k)")).then_inc(G.sets_out, 16)
                    sp.wait_ge(G.sets_out, 16)
                    sp.wait_ge(G.control_ready, 1)
                    rounds = sp.value_load(control[0:1, 0:1], min_val=1, max_val=PCOLS // SET)
                    stride = sp.value_load(control[0:1, 1:2], min_val=0, max_val=SET)
                    base = sp.value_load(control[0:1, 2:3], min_val=0, max_val=BLOCKS * SET)
                    with sp.Fori(0, rounds) as r:
                        with sp.Fori(0, BLOCKS // 2) as half:
                            for j in range(2):
                                sp.wait_ge(G.set_read, r * BLOCKS + half * 2 + j + 1)
                                sp.dma_start(kset[:, j, :], keys_dram[:, ds(base + r * SET + (half * 2 + j) * stride, SET)])\
                                  .then_inc([G.set_in0, G.set_in1][j], 16)

                @block.gpsimd
                def _(pool):
                    nc.gpsimd.memset(hist[:], 0.0).then_inc(G.hist_zero, 1)
                    pool.wait_ge(G.control_ready, 1)
                    pool.wait_ge(G.sort_step, INDEX_STEP)
                    rounds = pool.value_load(control[0:1, 0:1], min_val=1, max_val=PCOLS // SET)
                    with pool.Fori(0, rounds) as r:
                        with pool.Fori(0, BLOCKS // 2) as half:
                            for j in range(2):
                                it = r * BLOCKS + half * 2 + j
                                pool.wait_ge(G.decode_step, it * DEC + 3)
                                for g in range(0, NG, 2):
                                    group_free(pool, it, g)
                                    pool.sem_inc(G.pool_apart, 1)
                                    for k in range(OHG):
                                        c = g * OHG + k
                                        hot = nc.gpsimd.tensor_scalar(hoty[:, g, k, :], index16[:, 0:128], yrow[:, j, c:c + 1], None,
                                                                      ALU.is_equal)
                                    hot.then_inc(G.hoty_pool, 1)

                @block.scalar
                def _(act):
                    act.sem_inc(G.hoty_act, 1)
                    act.wait_ge(G.control_ready, 1)
                    act.wait_ge(G.sort_step, INDEX_STEP)
                    rounds = act.value_load(control[0:1, 0:1], min_val=1, max_val=PCOLS // SET)
                    with act.Fori(0, rounds) as r:
                        with act.Fori(0, BLOCKS // 2) as half:
                            for j in range(2):
                                it = r * BLOCKS + half * 2 + j
                                act.wait_ge(G.decode_step, it * DEC + 3)
                                for g in range(1, NG, 2):
                                    n = it * (NG // 2) + g // 2
                                    act.wait_ge(G.hoty_act, n + 1)
                                    for k in range(OHG):
                                        c = g * OHG + k
                                        dist = nc.scalar.activation(ydist[:, k, :], index[:, 0:128], ACT.Abs,
                                                                    bias=yrow[:, j, c:c + 1], scale=-1.0)
                                    dist.then_inc(G.hoty_abs, 1)
                                    act.wait_ge(G.hoty_abs, n + 1)
                                    group_free(act, it, g)
                                    nc.scalar.activation(hoty[:, g, :, :].rearrange("p k y -> p (k y)"),
                                                         ydist[:].rearrange("p k y -> p (k y)"), ACT.Relu,
                                                         bias=ones[:], scale=-1.0).then_inc(G.hoty_act, 1)

                @block.tensor
                def _(pe):
                    pe.sem_inc(G.hot_used, NG - 1)
                    pe.sem_inc(G.hist_mm, 1)
                    pe.wait_ge(G.flags_ready, 1)
                    nc.tensor.matmul(CX[0:1, 0:1], over[:, 3:4], ones[:], start=True, stop=True).then_inc(G.over_mm, 1)
                    pe.wait_ge(G.control_ready, 1)
                    rounds = pe.value_load(control[0:1, 0:1], min_val=1, max_val=PCOLS // SET)
                    with pe.Fori(0, rounds) as r:
                        with pe.Fori(0, BLOCKS // 2) as half:
                            for j in range(2):
                                pe.wait_ge(G.hist_added, r * BLOCKS + half * 2 + j + 1)
                                for g in range(NG):
                                    i = j * NG + g
                                    pe.wait_ge(G.hotz_ready, r * (BLOCKS * NG) + half * (2 * NG) + i + 1)
                                    n = (r * BLOCKS + half * 2 + j) * (NG // 2) + g // 2
                                    if g % 2:
                                        pe.wait_ge(G.hoty_act, n + 2)
                                    else:
                                        pe.wait_ge(G.hoty_pool, n + 1)
                                    for k in range(OHG):
                                        first, last = g == 0 and k == 0, g == NG - 1 and k == OHG - 1
                                        nc.tensor.matmul(PSUM[j][:, 0:512], hoty[:, g, k, :], hotz[:, g, k, 0:512],
                                                         start=first, stop=last)
                                        mm = nc.tensor.matmul(PSUM[j][:, 512:ZL], hoty[:, g, k, :], hotz[:, g, k, 512:ZL],
                                                              start=first, stop=last)
                                    if g < NG - 1:
                                        mm.then_inc(G.hot_used, 1)
                                    else:
                                        mm.then_inc(G.hist_mm, 1)

                @block.vector
                def _(dve):
                    steps = [0]

                    def link(ins, base):
                        steps[0] += 1
                        ins.then_inc(G.sort_step, 1)
                        dve.wait_ge(G.sort_step, base + steps[0])

                    dve.sem_inc(G.hist_added, 2)
                    dve.sem_inc(G.set_read, 2)
                    nc.vector.memset(ones[:], 1.0)
                    dve.wait_ge(G.idx_in, 32)
                    with dve.Fori(0, BLOCKS) as b:
                        steps[0] = 0
                        now = b * SORT
                        link(nc.vector.scalar_tensor_tensor(work[:, 0, :], cand[:].rearrange("p n k -> p (n k)"),
                                                            block_hi[0:PROWS, ds(b, 1)],
                                                            cand[:].rearrange("p n k -> p (n k)"), ALU.is_lt, ALU.mult), now)
                        for k in range(SET // 8):
                            dve.sem_inc(G.apart, 1)
                            link(nc.vector.max(best[:, 8 * k:8 * k + 8], work[:, k % 2, :]), now)
                            if k < SET // 8 - 1:
                                dve.sem_inc(G.apart, 1)
                                link(nc.vector.match_replace(work[:, 1 - k % 2, :], best[:, 8 * k:8 * k + 8],
                                                             work[:, k % 2, :], 0.0), now)
                        link(nc.vector.tensor_copy(sets[:, ds(b, 1), :].rearrange("p b k -> p (b k)"), best[:]), now)
                        assert steps[0] == SORT
                    nc.vector.sem_inc(G.sets_ready, 1)
                    steps[0] = 0
                    now = BLOCKS * SORT
                    link(nc.vector.tensor_reduce(over[:, 0:1], cand[:, :, TOP - 1], AX.X, ALU.max), now)
                    link(nc.vector.tensor_scalar(over[:, 1:2], over[:, 0:1], 0.0, None, ALU.is_gt), now)
                    link(nc.vector.tensor_tensor(overb[:], sets[:, :, SET - 1], block_lo[0:PROWS, :], ALU.is_ge), now)
                    link(nc.vector.tensor_reduce(over[:, 2:3], overb[:], AX.X, ALU.max), now)
                    nc.vector.tensor_tensor(over[:, 3:4], over[:, 1:2], over[:, 2:3], ALU.max).then_inc(G.flags_ready, 1)
                    dve.wait_ge(G.over_mm, 1)
                    link(nc.vector.tensor_scalar(full[:], CX[0:1, 0:1], 1.0, None, ALU.min), now)
                    nc.vector.tensor_scalar(control[:, 0:1], full[:], float(PCOLS // SET - 1), 1.0, ALU.mult, ALU.add)
                    nc.vector.tensor_scalar(control[:, 1:2], full[:], -float(SET), float(SET), ALU.mult, ALU.add)
                    nc.vector.tensor_scalar(control[:, 2:3], full[:], float(BLOCKS * SET), None, ALU.mult).then_inc(G.control_ready, 1)
                    link(nc.vector.tensor_copy(index16[:], index[:]), now)
                    dve.wait_ge(G.control_ready, 1)
                    dve.wait_ge(G.hist_zero, 1)
                    rounds = dve.value_load(control[0:1, 0:1], min_val=1, max_val=PCOLS // SET)
                    def decode(r, half, j):
                        it = r * BLOCKS + half * 2 + j
                        b = half * 2 + j
                        dve.wait_ge([G.set_in0, G.set_in1][j], (r * (BLOCKS // 2) + half + 1) * 16)
                        nc.vector.tensor_scalar(rel[:], kset[:, j, :], block_lo[0:PROWS, ds(b, 1)], None,
                                                ALU.subtract).then_inc(G.decode_step, 1)
                        dve.wait_ge(G.decode_step, it * DEC + 1)
                        nc.vector.tensor_scalar(tq[:], rel[:], (ZL - 1) / 2, 1.0 / ZL, ALU.subtract, ALU.mult)\
                          .then_inc(G.decode_step, 1)
                        dve.wait_ge(G.decode_step, it * DEC + 2)
                        nc.vector.tensor_scalar(yrow[:, j, :], tq[:], MAGIC, MAGIC, ALU.add, ALU.subtract)\
                          .then_inc(G.decode_step, 1)
                        dve.wait_ge(G.decode_step, it * DEC + 3)
                        nc.vector.scalar_tensor_tensor(zlab[:, j, :], yrow[:, j, :], -float(ZL), rel[:], ALU.mult, ALU.add)\
                          .then_inc(G.decode_step, 1)
                        dve.wait_ge(G.decode_step, it * DEC + 4)
                        nc.vector.sem_inc(G.set_read, 1)

                    def one_hots(r, half, j, groups):
                        it = r * BLOCKS + half * 2 + j
                        for g in groups:
                            group_free(dve, it, g)
                            for k in range(OHG):
                                c = g * OHG + k
                                hot = nc.vector.tensor_scalar(hotz[:, g, k, :], index16[:], zlab[:, j, c:c + 1], None,
                                                              ALU.is_equal)
                            hot.then_inc(G.hotz_ready, 1)

                    def add(r, half, j):
                        it = r * BLOCKS + half * 2 + j
                        b = half * 2 + j
                        dve.wait_ge(G.hist_mm, it + 2)
                        row = hist[:, ds((b + 2) * HROW + NL, ZL)]
                        nc.vector.tensor_tensor(row, row, PSUM[j], ALU.add).then_inc(G.hist_added, 1)

                    with dve.Fori(0, rounds) as r:
                        with dve.Fori(0, BLOCKS // 2) as half:
                            decode(r, half, 0)
                            decode(r, half, 1)
                            one_hots(r, half, 0, range(NG))
                            one_hots(r, half, 1, range(NG // 2))
                            add(r, half, 0)
                            one_hots(r, half, 1, range(NG // 2, NG))
                            add(r, half, 1)

        pass2(nc, t, e, own, hist)


def pass2(nc, t, e, own, hist):
    fp32 = mybir.dt.float32
    ALU, ACT, AX = mybir.AluOpType, mybir.ActivationFunctionType, mybir.AxisListType
    ds = bass.ds
    sb, sem = e["sb"], e["sem"]
    PJ, GN, ST, CX, MS = e["PJ"], e["GN"], e["ST"], e["CX"], e["MS"]
    wout, g_t, g_n, affine, ustat, group_mean = (e[k] for k in ("wout", "g_t", "g_n", "affine", "ustat", "group_mean"))
    both_halves = e["both_halves"]
    gamma, beta, b_out = e["gamma"], e["beta"], e["b_out"]
    bad_dram, a_dram, p_dram, x_dram, out_dram, edge_dram = (
        e[k] for k in ("bad_dram", "a_dram", "p_dram", "x_dram", "out_dram", "edge_dram"))

    wouta = sb(own, "wouta", [128, PAIRS, CHANNELS])
    edge_u = sb(own, "edge_u", [NS, CHANNELS])
    edge_neg = sb(own, "edge_neg", [NS, CHANNELS])
    ug = sb(own, "ug", [128, CT * CHANNELS])
    taps = sb(own, "taps", [128, 9, 128])
    cross = sb(own, "cross", [9, 2, 128])

    with ExitStack() as tmp:
        mask_cols = sb(tmp, "mask_cols", [128, PAIRS, NS])
        ccols = sb(tmp, "ccols", [128, PAIRS, NS])
        shift = sb(tmp, "shift", [128, 3, 128])
        crossm = sb(tmp, "crossm", [9, 2, 128])
        wedge = sb(tmp, "wedge", [9, 2])
        filt = sb(tmp, "filt", [128, 27])
        fexp = sb(tmp, "fexp", [128, 27])
        mom = sb(tmp, "mom", [128, 2, NCHUNK])
        moms = sb(tmp, "moms", [128, 2])
        bn = sb(tmp, "bn", [128, 8])
        tacc = sb(tmp, "tacc", [128, 2, 128])
        names = "pre_in mom_ready mom_mm bn_var bn_std c_ready u_mm u_copied ug_mm ug_copied exp_out pre_step edge_out".split()
        G = type("Sems", (), {n: sem("pre_" + n) for n in names})
        with nc.Block() as block:
            @block.sync
            def _(sp):
                sp.dma_start(mask_cols[:].rearrange("p q s -> p (q s)"), t["head_mask_cols"]).then_inc(G.pre_in, 16)
                sp.dma_start(shift[:].rearrange("p b f -> p (b f)"), t["shift"]).then_inc(G.pre_in, 16)
                sp.dma_start(crossm[:].rearrange("p b f -> p (b f)"), t["cross"]).then_inc(G.pre_in, 16)
                sp.dma_start(filt[:], t["conv_w"].to_broadcast([128, 27])).then_inc(G.pre_in, 16)
                sp.dma_start(wedge[:], t["conv_edge"]).then_inc(G.pre_in, 16)
                slots = hist[:].rearrange("p (s h f) -> p s h f", h=2, f=HROW)
                for o, row in enumerate((0, 127)):
                    sp.dma_start(edge_dram[:, o, :].unsqueeze(0), slots[row:row + 1, :, 1 - o, :]).then_inc(G.edge_out, 16)
                sp.wait_ge(G.edge_out, 32)

            @block.scalar
            def _(act):
                act.wait_ge(G.pre_in, 80)
                nc.scalar.activation(fexp[:], filt[:], ACT.Exp, scale=-1.0).then_inc(G.exp_out, 1)
                nc.scalar.activation(wedge[:], wedge[:], ACT.Exp, scale=-1.0).then_inc(G.exp_out, 1)
                act.wait_ge(G.bn_var, 1)
                nc.scalar.activation(bn[:, 4:5], bn[:, 3:4], ACT.Sqrt).then_inc(G.bn_std, 1)

            @block.tensor
            def _(pe):
                pe.wait_ge(G.mom_ready, 1)
                nc.tensor.matmul(MS[:, 0:2], both_halves[:], moms[:], start=True, stop=True).then_inc(G.mom_mm, 1)
                pe.wait_ge(G.c_ready, 1)
                for q in range(PAIRS):
                    mm = nc.tensor.matmul(CX[0:NS, 0:CHANNELS], ccols[:, q, :], wout[:, q, :], start=(q == 0), stop=(q == PAIRS - 1))
                mm.then_inc(G.u_mm, 1)
                pe.wait_ge(G.u_copied, 2)
                for c in range(CT):
                    mm = nc.tensor.matmul(CX[:, 256 * c:256 * c + 256], g_n[:, 128 * c:128 * c + 128], edge_u[:], start=True, stop=True)
                mm.then_inc(G.ug_mm, 1)

            @block.vector
            def _(dve):
                steps = [0]

                def link(ins):
                    steps[0] += 1
                    ins.then_inc(G.pre_step, 1)
                    dve.wait_ge(G.pre_step, steps[0])

                link(nc.vector.tensor_tensor(mom[:, 1, :], ustat[:, :, 0], ustat[:, :, 0], ALU.mult))
                nc.vector.tensor_copy(mom[:, 0, :], ustat[:, :, 0])
                link(nc.vector.tensor_tensor(mom[:, 1, :], mom[:, 1, :], ustat[:, :, 1], ALU.add))
                nc.vector.tensor_reduce(moms[:], mom[:], AX.X, ALU.add).then_inc(G.mom_ready, 1)
                dve.wait_ge(G.mom_mm, 1)
                link(nc.vector.tensor_scalar(bn[:, 0:2], MS[:, 0:2], 1.0 / (2 * NCHUNK), None, ALU.mult))
                link(nc.vector.tensor_tensor(bn[:, 2:3], bn[:, 0:1], bn[:, 0:1], ALU.mult))
                link(nc.vector.tensor_tensor(bn[:, 2:3], bn[:, 1:2], bn[:, 2:3], ALU.subtract))
                nc.vector.tensor_scalar(bn[:, 3:4], bn[:, 2:3], 0.0, BN_EPS, ALU.max, ALU.add).then_inc(G.bn_var, 1)
                dve.wait_ge(G.bn_std, 1)
                link(nc.vector.reciprocal(bn[:, 5:6], bn[:, 4:5]))
                link(nc.vector.tensor_tensor(bn[:, 5:6], bn[:, 5:6], gamma[:], ALU.mult))
                link(nc.vector.tensor_tensor(bn[:, 6:7], bn[:, 0:1], bn[:, 5:6], ALU.mult))
                link(nc.vector.tensor_tensor(bn[:, 6:7], beta[:], bn[:, 6:7], ALU.subtract))
                nc.vector.tensor_scalar(wouta[:], wout[:], bn[:, 5:6], None, ALU.mult)
                dve.wait_ge(G.pre_in, 80)
                nc.vector.tensor_scalar(ccols[:], mask_cols[:], bn[:, 6:7], None, ALU.mult).then_inc(G.c_ready, 1)
                dve.wait_ge(G.u_mm, 1)
                nc.vector.tensor_copy(edge_u[:], CX[0:NS, 0:CHANNELS]).then_inc(G.u_copied, 1)
                nc.vector.tensor_scalar(edge_neg[:], CX[0:NS, 0:CHANNELS], -1.0, None, ALU.mult).then_inc(G.u_copied, 1)
                dve.wait_ge(G.ug_mm, 1)
                nc.vector.tensor_copy(ug[:], CX[:])
                dve.wait_ge(G.exp_out, 2)
                link(nc.vector.tensor_scalar(wedge[:], wedge[:], 1.0, None, ALU.add))
                link(nc.vector.reciprocal(wedge[:], wedge[:]))
                for o in range(2):
                    nc.vector.tensor_scalar(cross[:, o, :], crossm[:, o, :], wedge[:, o:o + 1], None, ALU.mult)
                link(nc.vector.tensor_scalar(fexp[:], fexp[:], 1.0, None, ALU.add))
                link(nc.vector.reciprocal(filt[:], fexp[:]))
                link(nc.vector.memset(filt[:, 13:14], 1.0))
                for a in range(3):
                    for c in range(3):
                        tap = lambda b: filt[:, 9 * a + 3 * b + c:9 * a + 3 * b + c + 1]
                        link(nc.vector.tensor_scalar(tacc[:, 0, :], shift[:, 0, :], tap(0), None, ALU.mult))
                        link(nc.vector.scalar_tensor_tensor(tacc[:, 1, :], shift[:, 1, :], tap(1), tacc[:, 0, :], ALU.mult, ALU.add))
                        link(nc.vector.scalar_tensor_tensor(taps[:, 3 * a + c, :], shift[:, 2, :], tap(2), tacc[:, 1, :], ALU.mult, ALU.add))

    xr = [sb(own, "x_even", [128, CT, PIX]), sb(own, "x_odd", [128, CT, PIX])]
    xn = sb(own, "xn2", [128, CT, PIX])
    ptile = sb(own, "ptile2", [128, 2, PAIRS, 512])
    at = sb(own, "at", [128, 2, CT * CHANNELS])
    sbad = sb(own, "sbad2", [NS, 2, SIDE * EDGE])
    bnst = sb(own, "bnst2", [128, CT, 8, 6])
    mv = sb(own, "mv2", [128, CT, 2])
    aff = sb(own, "aff2", [128, CT, 2])
    tmp2 = sb(own, "tmp22", [128, CT])
    std = sb(own, "std2", [128, CT])
    hedge = sb(own, "hedge", [9, 2, (NZ + 1) * NL])
    names = ("x_in0 x_in1 a_in0 a_in1 p_in0 p_in1 at_ready xn_ready o_mm o_evac p_used stat_ready stat_mm var_ready std_ready aff_ready apart "
             "scaled conv_mm conv_added stored0 stored1 step stat_read edge_in credited").split()
    G = type("Sems", (), {n: sem("out_" + n) for n in names})
    STEPS = 20
    OPS = [PJ[:, 0, :], PJ[:, 1, :], GN[:, 0, :], GN[:, 1, :]]
    CPS = [ST[:, 0, :], ST[:, 1, :], CX[:], MS[:]]
    ZCUT = [(0, ZA), (ZA, NZ + 1 - ZA)]

    def past(n):
        return n + 1

    with nc.Block() as block:
        @block.sync
        def _(sp):
            for s in (G.o_evac, G.conv_added, G.p_used, G.stored0, G.stored1, G.stat_read, G.credited):
                sp.sem_inc(s, 1)
            sp.wait_ge(G.credited, 1)

    with nc.Block() as block:
        @block.sync
        def _(sp):
            def fetch(pair_of_images, j):
                i = pair_of_images
                sp.wait_ge([G.stored0, G.stored1][j], past(i * 32))
                for c in range(CT):
                    sp.dma_start(xr[j][:, c, :], x_dram[ds(i * 2 + j, 1), :, c, :].rearrange("b p f -> (b p) f"))\
                      .then_inc([G.x_in0, G.x_in1][j], 16)
                sp.dma_start(at[:, j, :], a_dram[ds(i * 2 + j, 1), :, :].rearrange("b p f -> (b p) f"))\
                  .then_inc([G.a_in0, G.a_in1][j], 16)
                sp.dma_start(sbad[:, j, :], bad_dram[ds(i * 2 + j, 1), :, :].rearrange("b s f -> (b s) f"))\
                  .then_inc([G.a_in0, G.a_in1][j], 16)

            def store(i, j):
                sp.wait_ge(G.conv_added, past(i * 8 + 4 * j + 4))
                for c in range(CT):
                    sp.dma_start(out_dram[ds(i * 2 + j, 1), :, c, :].rearrange("b p f -> (b p) f"), xr[j][:, c, :])\
                      .then_inc([G.stored0, G.stored1][j], 16)

            def edges(i, j):
                for c in range(3):
                    sp.dma_start(hedge[3 * c:3 * c + 3, :, :], edge_dram[ds(i * 2 + j, 3), :, c * NL:(c + NZ + 1) * NL])\
                      .then_inc(G.edge_in, 16)

            fetch(0, 0)
            edges(0, 0)
            with sp.Fori(0, IMAGES // 2 - 1) as i:
                fetch(i, 1)
                store(i, 0)
                edges(i, 1)
                fetch(i + 1, 0)
                store(i, 1)
                edges(i + 1, 0)
            fetch(IMAGES // 2 - 1, 1)
            store(IMAGES // 2 - 1, 0)
            edges(IMAGES // 2 - 1, 1)
            store(IMAGES // 2 - 1, 1)
            sp.wait_ge(G.stored0, past(16 * IMAGES))
            sp.wait_ge(G.stored1, past(16 * IMAGES))

        @block.gpsimd
        def _(pool):
            with pool.Fori(0, IMAGES) as img:
                for k in range(8):
                    if k < 2:
                        pool.wait_ge(G.p_used, past(img * 8))
                    else:
                        pool.wait_ge(G.p_used, past(img * 8 + k - 1))
                    pool.dma_start(ptile[:, k % 2, :, :],
                                   p_dram[ds(img, 1), :, :, 512 * k:512 * k + 512].rearrange("b q p f -> (b p) q f"))\
                        .then_inc([G.p_in0, G.p_in1][k % 2], 16)

        @block.scalar
        def _(act):
            def normalise(i, j):
                act.wait_ge([G.x_in0, G.x_in1][j], i * 32 + 32)
                sc = affine[:, ds(i * 2 + j, 1), 1, 0:1].rearrange("p b k -> p (b k)")
                bi = affine[:, ds(i * 2 + j, 1), 1, 1:2].rearrange("p b k -> p (b k)")
                nc.scalar.activation(xn[:, 1, :].rearrange("p (y x) -> p y x", x=SIDE),
                                     xr[j][:, 1, :].rearrange("p (x y) -> p y x", y=SIDE), ACT.Identity,
                                     bias=bi, scale=sc).then_inc(G.xn_ready, 1)

            def pair(i, last):
                for j in range(2):
                    if not (last and j == 1):
                        act.wait_ge(G.o_mm, i * 32 + 16 * j + 16)
                        normalise(i + j, 1 - j)
                    act.wait_ge(G.var_ready, i * 2 + j + 1)
                    nc.scalar.activation(std[:], tmp2[:], ACT.Sqrt).then_inc(G.std_ready, 1)
                    act.wait_ge(G.aff_ready, i * 2 + j + 1)
                    nc.scalar.activation(xr[j][:, 1, :], xr[j][:, 1, :], ACT.Identity,
                                         bias=aff[:, 1, 1:2], scale=aff[:, 1, 0:1]).then_inc(G.scaled, 1)

            normalise(0, 0)
            with act.Fori(0, IMAGES // 2 - 1) as i:
                pair(i, False)
            pair(IMAGES // 2 - 1, True)

        @block.tensor
        def _(pe):
            with pe.Fori(0, IMAGES // 2) as i:
                for j in range(2):
                    pe.wait_ge(G.xn_ready, i * 4 + 2 * j + 2)
                    pe.wait_ge(G.at_ready, i * 2 + j + 1)
                    pe.wait_ge(G.stat_read, past(i * 2 + j))
                    for k in range(8):
                        pe.wait_ge([G.p_in0, G.p_in1][k % 2], i * 128 + 64 * j + 16 * (k // 2) + 16)
                        for o in range(CT):
                            n = 2 * k + o
                            ps = OPS[n % 4]
                            if n < 4:
                                pe.wait_ge(G.o_evac, past(i * 32 + 16 * j))
                            else:
                                pe.wait_ge(G.o_evac, past(i * 32 + 16 * j + n - 3))
                            for c in range(CT):
                                nc.tensor.matmul(ps, at[:, j, 256 * c + 128 * o:256 * c + 128 * o + 128],
                                                 xn[:, c, 512 * k:512 * k + 512], start=(c == 0), stop=False)
                            for q in range(PAIRS):
                                nc.tensor.matmul(ps, wouta[:, q, 128 * o:128 * o + 128], ptile[:, k % 2, q, :],
                                                 start=False, stop=False)
                            mm = nc.tensor.matmul(ps.rearrange("p (y x) -> p y x", x=SIDE)[:, :, SIDE - EDGE:],
                                                  edge_neg[:, 128 * o:128 * o + 128],
                                                  sbad[:, j, 8 * EDGE * k:8 * EDGE * (k + 1)].rearrange("p (y x) -> p y x", x=EDGE),
                                                  start=False, stop=True)
                            mm.then_inc(G.o_mm, 1)
                        pe.wait_ge(G.o_mm, i * 32 + 16 * j + 2 * k + 2)
                        pe.sem_inc(G.p_used, 1)
                    for o in range(CT):
                        for z, (z0, zn) in enumerate(ZCUT):
                            n = 2 * o + z
                            pe.wait_ge(G.conv_added, past(i * 8 + 4 * j))
                            for a in range(3):
                                for c in range(3):
                                    nc.tensor.matmul(CPS[n][:, 0:zn * NL], taps[:, 3 * a + c, :],
                                                     hist[:, ds((i * 2 + j + a) * (2 * HROW) + o * HROW + (z0 + c) * NL, zn * NL)],
                                                     start=(a == 0 and c == 0), stop=False)
                            pe.wait_ge(G.edge_in, i * 96 + 48 * j + 48)
                            nc.tensor.matmul(CPS[n][:, 0:zn * NL], cross[:, o, :], hedge[:, o, z0 * NL:(z0 + zn) * NL],
                                             start=False, stop=True).then_inc(G.conv_mm, 1)
                            if n == 2:
                                pe.wait_ge(G.stat_ready, i * 2 + j + 1)
                                pe.wait_ge(G.o_evac, past(i * 32 + 16 * j + 16))
                                nc.tensor.matmul(PJ[:, 0, 0:2 * CT], group_mean[:], mv[:].rearrange("p t k -> p (t k)"),
                                                 start=True, stop=True).then_inc(G.stat_mm, 1)

        @block.vector
        def _(dve):
            steps = [0]

            def normalise(i, j):
                dve.wait_ge([G.a_in0, G.a_in1][j], i * 32 + 32)
                nc.vector.tensor_tensor(at[:, j, :], at[:, j, :], ug[:], ALU.add).then_inc(G.at_ready, 1)
                dve.wait_ge([G.x_in0, G.x_in1][j], i * 32 + 32)
                sc = affine[:, ds(i * 2 + j, 1), 0, 0:1].rearrange("p b k -> p (b k)")
                bi = affine[:, ds(i * 2 + j, 1), 0, 1:2].rearrange("p b k -> p (b k)")
                nc.vector.tensor_scalar(xn[:, 0, :].rearrange("p (y x) -> p y x", x=SIDE),
                                        xr[j][:, 0, :].rearrange("p (x y) -> p y x", y=SIDE),
                                        sc, bi, ALU.mult, ALU.add).then_inc(G.xn_ready, 1)

            def pair(i, last):
                steps[0] = 0

                def link(ins):
                    steps[0] += 1
                    ins.then_inc(G.step, 1)
                    dve.wait_ge(G.step, i * STEPS + steps[0])

                for j in range(2):
                    dve.wait_ge(G.xn_ready, i * 4 + 2 * j + 2)
                    for k in range(8):
                        for o in range(CT):
                            n = 2 * k + o
                            dve.wait_ge(G.o_mm, i * 32 + 16 * j + n + 1)
                            xv = xr[j][:, o, :].rearrange("p (x y) -> p y x", y=SIDE)[:, 8 * k:8 * k + 8, :]
                            nc.vector.scalar_tensor_tensor(xv, OPS[n % 4].rearrange("p (y x) -> p y x", x=SIDE), b_out[:, o:o + 1],
                                                           xv, ALU.add, ALU.add).then_inc(G.o_evac, 1)
                    if not (last and j == 1):
                        dve.wait_ge(G.o_mm, i * 32 + 16 * j + 16)
                        normalise(i + j, 1 - j)
                    dve.wait_ge(G.o_evac, past(i * 32 + 16 * j + 16))
                    for c in range(CT):
                        for k in range(8):
                            ins = nc.vector.bn_stats(bnst[:, c, k, :], xr[j][:, c, 512 * k:512 * k + 512])
                    link(ins)
                    dve.sem_inc(G.apart, 1)
                    nc.vector.bn_aggr(mv[:, 0, :], bnst[:, 0, :, :].rearrange("p k s -> p (k s)"))
                    link(nc.vector.bn_aggr(mv[:, 1, :], bnst[:, 1, :, :].rearrange("p k s -> p (k s)")))
                    link(nc.vector.tensor_tensor(tmp2[:], mv[:, :, 0], mv[:, :, 0], ALU.mult))
                    nc.vector.tensor_tensor(mv[:, :, 1], mv[:, :, 1], tmp2[:], ALU.add).then_inc(G.stat_ready, 1)
                    dve.wait_ge(G.stat_mm, i * 2 + j + 1)
                    link(nc.vector.tensor_copy(mv[:].rearrange("p t k -> p (t k)"), PJ[:, 0, 0:2 * CT]))
                    nc.vector.sem_inc(G.stat_read, 1)
                    link(nc.vector.tensor_tensor(tmp2[:], mv[:, :, 0], mv[:, :, 0], ALU.mult))
                    link(nc.vector.tensor_tensor(tmp2[:], mv[:, :, 1], tmp2[:], ALU.subtract))
                    nc.vector.tensor_scalar(tmp2[:], tmp2[:], 0.0, GN_EPS, ALU.max, ALU.add).then_inc(G.var_ready, 1)
                    dve.wait_ge(G.std_ready, i * 2 + j + 1)
                    link(nc.vector.reciprocal(std[:], std[:]))
                    link(nc.vector.tensor_tensor(tmp2[:], mv[:, :, 0], std[:], ALU.mult))
                    nc.vector.tensor_scalar(aff[:, :, 0], std[:], 1.0, None, ALU.add)
                    link(nc.vector.tensor_scalar(aff[:, :, 1], tmp2[:], -1.0, None, ALU.mult))
                    nc.vector.sem_inc(G.aff_ready, 1)
                    link(nc.vector.tensor_scalar(xr[j][:, 0, :], xr[j][:, 0, :], aff[:, 0, 0:1], aff[:, 0, 1:2], ALU.mult, ALU.add))
                    for o in range(CT):
                        if o == 1:
                            dve.wait_ge(G.scaled, i * 2 + j + 1)
                        for z, (z0, zn) in enumerate(ZCUT):
                            n = 2 * o + z
                            dve.wait_ge(G.conv_mm, i * 8 + 4 * j + n + 1)
                            xv = xr[j][:, o, :].rearrange("p (z l) -> p z l", l=SIDE)[:, z0:z0 + zn, 0:NL]
                            nc.vector.tensor_tensor(xv, xv, CPS[n][:, 0:zn * NL].rearrange("p (z l) -> p z l", l=NL), ALU.add)\
                                .then_inc(G.conv_added, 1)
                assert steps[0] == STEPS

            normalise(0, 0)
            with dve.Fori(0, IMAGES // 2 - 1) as i:
                pair(i, False)
            pair(IMAGES // 2 - 1, True)


def kernel(**inputs):
    import concourse.bacc as bacc
    from concourse.bass_utils import run_bass_kernel_spmd

    def lay(name, *shape):
        return np.ascontiguousarray(np.asarray(inputs[name]).reshape(*shape))

    w_qkv = np.asarray(inputs["L0_conv_w_qkv"])
    kt = w_qkv[HEADS * DK:2 * HEADS * DK].T.reshape(CHANNELS, PAIRS, 128)
    vt = w_qkv[2 * HEADS * DK:].T.reshape(CHANNELS, PAIRS, 128)
    arrays = {
        "x": np.asarray(inputs["x"]),
        "points": np.asarray(inputs["L1_conv_point_cloud"]),
        "conv_w": lay("L1_conv_weights", 1, 27),
        "conv_edge": np.ascontiguousarray(np.asarray(inputs["L1_conv_weights"]).reshape(3, 3, 3)[:, [2, 0], :].transpose(2, 0, 1).reshape(9, 2)),
        "w_q": np.ascontiguousarray(w_qkv[:HEADS * DK]),
        "w_kv_t": np.ascontiguousarray(np.concatenate([kt, vt], axis=2)),
        "w_out_t": np.ascontiguousarray(np.asarray(inputs["L0_conv_w_out"]).T),
        "b_out": np.ascontiguousarray(np.asarray(inputs["L0_conv_b_out"]).reshape(CT, 128).T),
        "rel_t": np.ascontiguousarray(np.concatenate([np.asarray(inputs["L0_conv_rel_rows"]).T,
                                                      np.asarray(inputs["L0_conv_rel_columns"]).T], axis=1)),
        "gamma": lay("L0_conv_bn_gamma", DK, 1),
        "beta": lay("L0_conv_bn_beta", DK, 1),
        **constants(),
    }
    nc = bacc.Bacc("TRN2", target_bir_lowering=False, num_devices=1)
    t = {k: nc.dram_tensor("in_" + k, a.shape, mybir.dt.from_np(a.dtype), kind="ExternalInput").ap() for k, a in arrays.items()}
    out = nc.dram_tensor("out", [IMAGES, CHANNELS, SIDE, SIDE], mybir.dt.float32, kind="ExternalOutput").ap()
    build(nc, t, out)
    r = run_bass_kernel_spmd(nc, [{"in_" + k: a for k, a in arrays.items()}], core_ids=[0])
    return r.results[0]["out"]
```

```python
import numpy as np
import concourse.bass as bass
from concourse import mybir
from contextlib import ExitStack

IMAGES, CHANNELS, SIDE = 8, 256, 64
HEADS, DK, REL = 8, 64, 7
PIX = SIDE * SIDE
CT = CHANNELS // 128
PAIRS = HEADS // 2
YL = SIDE // 2
NS = 2 * REL * HEADS
EDGE = REL - 1
GROUP = 8
PARTS = 3
TAPS = 2 * REL - 1
SROWS = 2 * PARTS * REL
GENK = SROWS + 2 * PARTS * TAPS
STRIP = 3 * SIDE - 1
BN_EPS, GN_EPS = 1e-5, 1e-5

POINTS = 1000000
PROWS = 125
PCOLS = POINTS // PROWS
NCHUNK = IMAGES * PAIRS
CHUNK = PCOLS // NCHUNK
TOP = 24
NX, NY, NZ, NL = 8, 256, 32, 21
ZL = NZ * NL
BLOCK = 128 * ZL
BLOCKS = NX * 2
SET = 32
GROUPS, GTOP = 4, 72
OHG = 8
MAGIC = 1.5 * 2.0 ** 23
ZSLOT = NZ + 3
HROW = ZSLOT * NL
ZA = 17


def constants():
    c = {}
    p = np.arange(128)
    c["group_mean"] = (p[:, None] // GROUP == p[None] // GROUP).astype(np.float32) / GROUP
    c["swap_half"] = (p[:, None] == (p[None] + 64) % 128).astype(np.float32)
    c["both_halves"] = (p[:, None] % 64 == p[None] % 64).astype(np.float32)
    s = np.arange(NS)
    kind, r, head = s // (REL * HEADS), s // HEADS % REL, s % HEADS
    hm = np.zeros((128, PAIRS, NS), np.float32)
    for q in range(PAIRS):
        hm[:, q] = head[None] == 2 * q + p[:, None] // 64
    c["head_mask"] = hm.reshape(128, -1)
    c["head_mask_cols"] = (hm * (kind == 1)).reshape(128, -1).astype(np.float32)
    c["bad_mask"] = ((kind[:, None] == 1) & (r[:, None] + SIDE - EDGE + np.arange(EDGE)[None] >= SIDE)).astype(np.float32)
    c["good_mask"] = (r[:, None] + SIDE - EDGE + np.arange(EDGE)[None] < SIDE).astype(np.float32)
    d = np.zeros((GENK, 2, STRIP), np.float32)
    for y2 in range(2):
        for part in range(PARTS):
            for kind, (row0, taps) in enumerate(((0, REL), (PARTS * 2 * REL, TAPS))):
                for j in range(taps):
                    d[row0 + (y2 * PARTS + part) * taps + j, kind, SIDE - 1 + SIDE * y2 + j] = 1
    c["strip"] = d.reshape(GENK, 2 * STRIP)
    sh = np.stack([(p[:, None] == p[None] + b - 1) for b in range(3)], 1).astype(np.float32)
    c["shift"] = sh.reshape(128, 3 * 128)
    cr = np.zeros((9, 2, 128), np.float32)
    cr[:, 0, 127] = 1
    cr[:, 1, 0] = 1
    c["cross"] = cr.reshape(9, 256)
    lo = np.arange(BLOCKS) * BLOCK + 1.0
    c["block_lo"] = np.tile(np.concatenate([lo, lo[:2]])[None], (128, 1)).astype(np.float32)
    c["block_hi"] = np.tile(lo[None] + BLOCK, (128, 1)).astype(np.float32)
    c["index"] = np.tile(np.arange(ZL)[None], (128, 1)).astype(np.float32)
    return c


def build(nc, t, out):
    fp32, bf16, fp16, i32 = mybir.dt.float32, mybir.dt.bfloat16, mybir.dt.float16, mybir.dt.int32
    ALU, ACT, AX = mybir.AluOpType, mybir.ActivationFunctionType, mybir.AxisListType
    ds = bass.ds
    VY = np.float32(51.2) / np.float32(256)

    s_dram = nc.dram_tensor("s_scratch", [IMAGES, NS, PIX], fp32, kind="Internal").ap()
    sp_dram = nc.dram_tensor("sp_scratch", [IMAGES, PARTS, REL, HEADS, PIX], bf16, kind="Internal").ap()
    tp_dram = nc.dram_tensor("tp_scratch", [IMAGES, PARTS, TAPS, HEADS, PIX], bf16, kind="Internal").ap()
    bad_dram = nc.dram_tensor("bad_scratch", [IMAGES, NS, SIDE * EDGE], fp32, kind="Internal").ap()
    a_dram = nc.dram_tensor("a_scratch", [IMAGES, 128, CT * CHANNELS], fp32, kind="Internal").ap()
    p_dram = nc.dram_tensor("p_scratch", [IMAGES, PAIRS, 128, PIX], fp32, kind="Internal").ap()
    keys_dram = nc.dram_tensor("keys_scratch", [PROWS, 2 * BLOCKS * SET + PCOLS], fp32, kind="Internal").ap()
    cand_dram = nc.dram_tensor("cand_scratch", [PROWS, NCHUNK * TOP], fp32, kind="Internal").ap()
    edge_dram = nc.dram_tensor("edge_scratch", [NX + 2, 2, HROW], fp32, kind="Internal").ap()
    pc_dram = t["points"].rearrange("(p k) c -> p (k c)", p=PROWS)
    x_dram = t["x"].rearrange("b (t p) h w -> b p t (h w)", p=128)
    out_dram = out.rearrange("b (t p) h w -> b p t (h w)", p=128)

    top = ExitStack()
    with top:
        def sb(stack, name, shape, dt=fp32):
            return stack.enter_context(nc.sbuf_tensor(name, shape, dt))

        front = top.enter_context(ExitStack())
        setup = top.enter_context(ExitStack())

        def sem(name):
            return top.enter_context(nc.semaphore(name))

        group_mean = sb(top, "group_mean", [128, 128])
        both_halves = sb(top, "both_halves", [128, 128])
        wout = sb(top, "wout", [128, PAIRS, CHANNELS])
        g_t = sb(top, "g_t", [128, CT, NS])
        g_n = sb(top, "g_n", [NS, CHANNELS])
        affine = sb(top, "affine", [128, IMAGES, CT, 2])
        ustat = sb(top, "ustat", [128, NCHUNK, 2])
        block_lo = sb(top, "block_lo", [128, BLOCKS + 2])
        block_hi = sb(top, "block_hi", [128, BLOCKS])
        gamma = sb(top, "gamma", [128, 1])
        beta = sb(top, "beta", [128, 1])
        b_out = sb(top, "b_out", [128, CT])

        xr = sb(front, "xr", [128, CT, PIX])
        swap_half = sb(front, "swap_half", [128, 128])
        wq = sb(front, "wq", [128, PAIRS, CHANNELS])
        head_mask = sb(setup, "head_mask", [128, PAIRS, NS])
        relbd = sb(setup, "relbd", [128, PAIRS, NS])
        reld = sb(setup, "reld", [128, 2 * REL])

        PJ = top.enter_context(nc.psum_tensor("PJ", [128, 2, 512], fp32))
        GN = top.enter_context(nc.psum_tensor("GN", [128, 2, 512], fp32))
        ST = top.enter_context(nc.psum_tensor("ST", [128, 2, 512], fp32))
        CX = top.enter_context(nc.psum_tensor("CX", [128, 512], fp32))
        MS = top.enter_context(nc.psum_tensor("MS", [128, 512], fp32))

        setup_in = sem("setup_in")
        x_in = sem("x_in")
        relbd_ready = sem("relbd_ready")
        g_ready = sem("g_ready")
        g_copied = sem("g_copied")
        with nc.Block() as block:
            @block.sync
            def _(sp):
                n = 0
                for dst, src in (
                        (group_mean[:], t["group_mean"]), (swap_half[:], t["swap_half"]),
                        (both_halves[:], t["both_halves"]),
                        (wq[:], t["w_q"].rearrange("(q p) c -> p q c", p=128)),
                        (wout[:], t["w_out_t"].rearrange("(q p) c -> p q c", p=128)),
                        (head_mask[:].rearrange("p q s -> p (q s)"), t["head_mask"]),
                        (reld[0:64, :], t["rel_t"]), (reld[64:128, :], t["rel_t"]),
                        (block_lo[:], t["block_lo"]), (block_hi[:], t["block_hi"]),
                        (gamma[0:64, :], t["gamma"]), (gamma[64:128, :], t["gamma"]),
                        (beta[0:64, :], t["beta"]), (beta[64:128, :], t["beta"]),
                        (b_out[:], t["b_out"])):
                    sp.dma_start(dst, src).then_inc(setup_in, 16)
                    n += 16
                assert n == 15 * 16
                for c in range(CT):
                    sp.dma_start(xr[:, c, :], x_dram[0:1, :, c, :].rearrange("b p f -> (b p) f")).then_inc(x_in, 16)

            @block.vector
            def _(dve):
                dve.wait_ge(setup_in, 15 * 16)
                for q in range(PAIRS):
                    nc.vector.tensor_tensor(
                        relbd[:, q, :].rearrange("p (k n) -> p k n", n=HEADS),
                        head_mask[:, q, :].rearrange("p (k n) -> p k n", n=HEADS),
                        reld[:].unsqueeze(2).to_broadcast([128, 2 * REL, HEADS]), ALU.mult).then_inc(relbd_ready, 1)
                dve.wait_ge(g_ready, 3)
                nc.vector.tensor_copy(g_n[:], CX[0:NS, 0:CHANNELS]).then_inc(g_copied, 1)
                nc.vector.tensor_copy(g_t[:, 0, :], MS[:, 0:NS]).then_inc(g_copied, 1)
                nc.vector.tensor_copy(g_t[:, 1, :], ST[:, 0, 0:NS]).then_inc(g_copied, 1)
                dve.wait_ge(g_copied, 3)

            @block.tensor
            def _(pe):
                pe.wait_ge(setup_in, 15 * 16)
                pe.wait_ge(relbd_ready, PAIRS)
                for dst, lhs, rhs in ((CX[0:NS, 0:CHANNELS], lambda q: relbd[:, q, :], lambda q: wq[:, q, :]),
                                      (MS[:, 0:NS], lambda q: wq[:, q, 0:128], lambda q: relbd[:, q, :]),
                                      (ST[:, 0, 0:NS], lambda q: wq[:, q, 128:256], lambda q: relbd[:, q, :])):
                    for q in range(PAIRS):
                        last = nc.tensor.matmul(dst, lhs(q), rhs(q), start=(q == 0), stop=(q == PAIRS - 1))
                    last.then_inc(g_ready, 1)

        setup.close()
        pass1(nc, t, locals())
        front.close()
        histogram_and_pass2(nc, t, locals())


def pass1(nc, t, e):
    fp32, bf16 = mybir.dt.float32, mybir.dt.bfloat16
    ALU, ACT, AX = mybir.AluOpType, mybir.ActivationFunctionType, mybir.AxisListType
    ds = bass.ds
    sb, sem = e["sb"], e["sem"]
    PJ, GN, ST, CX, MS = e["PJ"], e["GN"], e["ST"], e["CX"], e["MS"]
    wq, wout, g_t, affine, ustat = (e[k] for k in ("wq", "wout", "g_t", "affine", "ustat"))
    group_mean, swap_half, both_halves = e["group_mean"], e["swap_half"], e["both_halves"]
    s_dram, sp_dram, tp_dram, bad_dram, a_dram, p_dram, keys_dram = (
        e[k] for k in ("s_dram", "sp_dram", "tp_dram", "bad_dram", "a_dram", "p_dram", "keys_dram"))
    pc_dram, x_dram, cand_dram = e["pc_dram"], e["x_dram"], e["cand_dram"]
    VY = e["VY"]
    HY = YL // 2
    NST = 8
    SLOTS = 4

    with ExitStack() as own:
        xr = e["xr"]
        xn = sb(own, "xn", [128, CT, PIX])
        kv = sb(own, "kv", [128, YL, 256])
        band = [sb(own, "band0", [128, HY, 2, 2, SIDE]), sb(own, "band1", [128, HY, 2, 2, SIDE])]
        ptile = sb(own, "ptile", [128, SLOTS, 512])
        srow = sb(own, "srow", [GENK, 2, 2, YL, SIDE], bf16)
        wkv = sb(own, "wkv", [128, CT, PAIRS, 256])
        strip = sb(own, "strip", [GENK, 2, STRIP], bf16)
        bad_mask = sb(own, "bad_mask", [NS, EDGE])
        good_mask = sb(own, "good_mask", [NS, EDGE])
        tt = sb(own, "tt", [128, TAPS, 4, SIDE])
        sbad = sb(own, "sbad", [NS, SIDE, EDGE])
        bnst = sb(own, "bnst", [128, CT, 8, 6])
        ybn = sb(own, "ybn", [128, 16, 6])
        mvy = sb(own, "mvy", [128, 2])
        mv = sb(own, "mv", [128, CT, 2])
        tmp2 = sb(own, "tmp2", [128, CT])
        tmp3 = sb(own, "tmp3", [128, CT])
        mxq = sb(own, "mxq", [128, 4, 128])
        mx = sb(own, "mx", [128, 128])
        mxx = sb(own, "mxx", [128, 128])
        rz = sb(own, "rz", [128, 128])
        ctxbd = sb(own, "ctxbd", [128, 128])
        fmat = sb(own, "fmat", [128, CHANNELS])
        amat = sb(own, "amat", [128, CT * CHANNELS])
        pc = sb(own, "pc", [PROWS, CHUNK, 4])
        ptb = sb(own, "pt", [128, 6, CHUNK])
        pt = ptb[0:PROWS]
        top24 = sb(own, "top24", [PROWS, TOP])

        flat = xr[:].rearrange("p c f -> p (c f)")
        QW = 4 * SIDE
        stile = flat[0:NS, 0:PIX].rearrange("p (a l x) -> p a l x", a=2, x=SIDE)
        sy = flat[:, 2 * PIX - 2 * REL * QW:].rearrange("p (k l x) -> p k l x", l=4, x=SIDE)
        RS = PARTS * REL * QW // 2
        s_parts = flat[:, 0:RS].bitcast(bf16).rearrange("p (a f) -> p a f", a=PARTS)
        s_rest = flat[:, RS:RS + REL * QW]
        TW = TAPS * QW // 2
        t_at = [2 * PIX - 2 * REL * QW, 2 * PIX - 2 * REL * QW + TW, RS]
        t_parts = [flat[:, o:o + TW].bitcast(bf16) for o in t_at]
        t_view = lambda a, h: t_parts[a].rearrange("p (k l x) -> p k l x", l=4, x=SIDE)[:, :, 2 * h:2 * h + 2, :]
        prod = [ptb[:].rearrange("p k c -> p (k c)")[:, 0:REL * QW // 2].rearrange("p (k l x) -> p k l x", l=2, x=SIDE),
                ptile[:].rearrange("p k c -> p (k c)")[:, 0:REL * QW // 2].rearrange("p (k l x) -> p k l x", l=2, x=SIDE)]

        counted = ("bn_done mvp_ready gstat_mm var_ready std_ready xn_ready s_mm s_act s_dve s_out bad_out "
                   "s_cast s_sub t_sum_dve t_sum_pool t_cast0 t_cast1 sp_out tp_out s_back0 s_back1 t_back0 t_back1 pj_mm kv_evac gen_mm gen_act "
                   "y_mm y_stat p_mm p_head0 p_head1 p_out0 p_out1 p_out2 p_out3 "
                   "max_ready swap_mm shift_ready sub_done exp_done zsum_ready zsum_mm rz_ready norm_done ctx_mm ctx_copied "
                   "f_mm f_copied a_mm a_copied a_out pts_in key_ready key_out top_ready top_out unit_read dve_step pool_step").split()
        S = {n: sem(n) for n in counted + ["w_in", "sy_in", "zeroed", "strip_ready", "apart", "pool_apart", "credited"]}
        starts_at_one = [S[n] for n in counted]
        S["x_in"] = e["x_in"]
        G = type("Sems", (), S)
        p_out = [G.p_out0, G.p_out1, G.p_out2, G.p_out3]
        s_back, t_back = [G.s_back0, G.s_back1], [G.t_back0, G.t_back1]

        def per(img, each, n):
            return img * each + n + 1

        with nc.Block() as block:
            @block.sync
            def _(sp):
                for s in starts_at_one:
                    sp.sem_inc(s, 1)
                sp.sem_inc(G.credited, 1)
                sp.wait_ge(G.credited, 1)

        ORDER = {False: ("y0", "y1+t0", "p0+t1", "p1"), True: ("y0+s1", "y1", "t0", "p0+t1", "p1")}
        JOB = ("s0", "s1", "t0", "t1")
        STR = [ST[:, 0, :], ST[:, 1, :], PJ[:, 0, :], PJ[:, 1, :]]
        EARLY = {False: [(k,) for k in range(16)],
                 True: [()] * 12 + [(2 * k, 2 * k + 1) for k in range(4)]}
        MAX_CUT = (0, 12, 22, 30, 32)
        CAST_AT = (1, 4, 6)
        T_AT = {13: (0, 0), 14: (0, 1), 15: (1, 0)}
        SUM_AT = (0, 2, 4, 6)
        ZSUM_AT = 8
        BOTH_AT = (0, 2, 4, 6, 8, 9)
        DVE_STEPS = 197

        def free_band(eng, img, q, job):
            if job[0] == "s":
                eng.wait_ge(G.p_mm, per(img, 64, 16 * q))
            else:
                eng.wait_ge(G.y_mm, per(img, 64, 16 * q + 8 * int(job[1]) + 8))

        with nc.Block() as block:
            @block.sync
            def _(sp):
                sp.dma_start(wkv[:], t["w_kv_t"].rearrange("(t p) q f -> p t q f", p=128)).then_inc(G.w_in, 16)
                sp.dma_start(band[0][0:GENK].rearrange("p l n a x -> p (l n a x)")[:, 0:2 * STRIP], t["strip"]).then_inc(G.w_in, 16)
                sp.dma_start(bad_mask[:], t["bad_mask"]).then_inc(G.w_in, 16)
                sp.dma_start(good_mask[:], t["good_mask"]).then_inc(G.w_in, 16)
                sp.wait_ge(G.zeroed, 3)

                def load_image(img):
                    for c in range(CT):
                        sp.dma_start(xr[:, c, :], x_dram[ds(img, 1), :, c, :].rearrange("b p f -> (b p) f")).then_inc(G.x_in, 16)

                def load_rows(img, q, kind, half):
                    dram, rows, row0 = ((sp_dram, PARTS * REL, 0), (tp_dram, PARTS * TAPS, SROWS))[kind]
                    for y2 in range(2):
                        at = y2 * (PIX // 2) + half * (PIX // 4)
                        src = dram[ds(img, 1), :, :, 2 * q:2 * q + 2, at:at + PIX // 4].rearrange("b a k n f -> (b a k) n f")
                        sp.dma_start(srow[row0 + rows * y2:row0 + rows * (y2 + 1), :, y2, HY * half:HY * (half + 1), :]
                                     .rearrange("p n l x -> p n (l x)"), src).then_inc((s_back, t_back)[kind][half], 16)

                def s_out(img):
                    for h in range(2):
                        sp.wait_ge(G.s_act, per(img, NST, 4 * h + 4))
                        sp.wait_ge(G.s_dve, per(img, NST, 4 * h + 4))
                        sp.dma_start(s_dram[ds(img, 1), :, :].rearrange("b s (a l f) -> (b s) a l f", a=2, l=2)[:, :, h, :],
                                     stile[:, :, HY * h:HY * (h + 1), :].rearrange("p a l x -> p a (l x)")).then_inc(G.s_out, 16)
                    sp.dma_start(bad_dram[ds(img, 1), :, :].rearrange("b s f -> (b s) f"),
                                 sbad[:].rearrange("p y x -> p (y x)")).then_inc(G.bad_out, 16)

                def keys_out(img, c):
                    sp.wait_ge(G.key_ready, per(img, PAIRS, c + 1))
                    sp.dma_start(keys_dram[:, ds((img * PAIRS + c) * CHUNK + BLOCKS * SET, CHUNK)],
                                 pt[:, 5, :]).then_inc(G.key_out, 16)
                    sp.wait_ge(G.top_ready, per(img, PAIRS, c + 1))
                    sp.dma_start(cand_dram[:, ds((img * PAIRS + c) * TOP, TOP)], top24[:]).then_inc(G.top_out, 16)

                def points_in(img, c):
                    sp.wait_ge(G.unit_read, per(img, PAIRS, c))
                    sp.dma_start(pc[:].rearrange("p k c -> p (k c)"),
                                 pc_dram[:, ds((img * PAIRS + c) * (4 * CHUNK), 4 * CHUNK)]).then_inc(G.pts_in, 16)

                def image(img, last):
                    for a in range(PARTS):
                        sp.wait_ge(G.s_cast, per(img, PARTS, a + 1))
                        sp.dma_start(sp_dram[ds(img, 1), a, :, :, :].rearrange("b k n (c f) -> (b n c) k f", c=16),
                                     s_parts[:, a, :].rearrange("p (k f) -> p k f", k=REL)).then_inc(G.sp_out, 16)
                    sp.wait_ge(G.sp_out, per(img, 48, 48))
                    sp.wait_ge(G.gen_mm, per(img, 128, 0))
                    for h in range(2):
                        load_rows(img, 0, 0, h)
                    for a in range(PARTS):
                        sp.wait_ge(G.t_cast0, per(img, PARTS, a + 1))
                        sp.wait_ge(G.t_cast1, per(img, PARTS, a + 1))
                        sp.dma_start(tp_dram[ds(img, 1), a, :, :, :].rearrange("b k n (c f) -> (b n c) k f", c=16),
                                     t_parts[a].rearrange("p (k f) -> p k f", k=TAPS)).then_inc(G.tp_out, 16)
                    sp.wait_ge(G.tp_out, per(img, 48, 48))
                    for h in range(2):
                        load_rows(img, 0, 1, h)
                    if not last:
                        load_image(img + 1)
                    for q in range(PAIRS):
                        if q == 0:
                            points_in(img, 0)
                        if q == 2:
                            points_in(img, 3)
                            keys_out(img, 2)
                        if q + 1 < PAIRS:
                            sp.wait_ge(G.gen_mm, per(img, 128, 32 * q + 24))
                            load_rows(img, q + 1, 0, 0)
                            load_rows(img, q + 1, 1, 0)
                        if q == PAIRS - 1 and not last:
                            s_out(img + 1)
                        for k in range(8):
                            m = 8 * q + k
                            if k == 3 and q + 1 < PAIRS:
                                sp.wait_ge(G.gen_mm, per(img, 128, 32 * q + 32))
                                load_rows(img, q + 1, 0, 1)
                                load_rows(img, q + 1, 1, 1)
                            sp.wait_ge(G.p_head0, per(img, 64, 2 * m + 2))
                            sp.wait_ge(G.p_head1, per(img, 64, 2 * m + 2))
                            sp.dma_start(p_dram[ds(img, 1), q, :, 512 * k:512 * (k + 1)].rearrange("b p f -> (b p) f"),
                                         ptile[:, m % SLOTS, :]).then_inc(p_out[m % SLOTS], 16)
                        if q < 2:
                            points_in(img, q + 1)
                        if q < 3:
                            keys_out(img, (0, 1, 3)[q])
                    sp.wait_ge(G.a_copied, per(img, PAIRS, PAIRS))
                    sp.dma_start(a_dram[ds(img, 1), :, :].rearrange("b p f -> (b p) f"), amat[:]).then_inc(G.a_out, 16)

                s_out(0)
                with sp.Fori(0, IMAGES - 1) as img:
                    image(img, False)
                image(IMAGES - 1, True)
                for done, each in ((G.a_out, 16), (G.bad_out, 16), (G.key_out, 16 * PAIRS), (G.top_out, 16 * PAIRS),
                                   *((p, 8 * 16) for p in p_out)):
                    sp.wait_ge(done, per(IMAGES, each, 0))

            @block.gpsimd
            def _(pool):
                steps = [0]
                TSTEPS = 12

                def link(ins, img):
                    steps[0] += 1
                    ins.then_inc(G.pool_step, 1)
                    pool.wait_ge(G.pool_step, per(img, TSTEPS, steps[0]))

                nc.gpsimd.memset(srow[:, 0, :, :, :], 0.0).then_inc(G.zeroed, 1)
                nc.gpsimd.memset(srow[:, 1, :, :, :], 0.0).then_inc(G.zeroed, 1)
                nc.gpsimd.memset(ctxbd[:], 0.0).then_inc(G.zeroed, 1)

                def s_back_in(idx):
                    pool.wait_ge(G.s_out, per(idx, 32, 32))
                    for kind in range(2):
                        src = s_dram[ds(idx, 1), kind * REL * HEADS:(kind + 1) * REL * HEADS, :]
                        pool.dma_start(sy[:, REL * kind:REL * (kind + 1), :, :].rearrange("p k l x -> p k (l x)"),
                                       src.rearrange("b (k n) (c f) -> (b n c) k f", n=HEADS, c=16)).then_inc(G.sy_in, 16)

                def image(img, last):
                    steps[0] = 0
                    own_tt = tt[:, :, 2:4, :]
                    pool.wait_ge(G.sy_in, img * 32 + 32)
                    pool.wait_ge(G.tp_out, per(img, 48, 0))
                    pool.wait_ge(G.p_out0, per(img, 128, 0))
                    pool.wait_ge(G.p_out1, per(img, 128, 0))
                    pool.sem_inc(G.pool_apart, 1)
                    nc.gpsimd.memset(own_tt[:, REL:], 0.0)
                    link(nc.gpsimd.tensor_tensor(own_tt[:, 0:REL], sy[:, 0:REL, 2:4, :],
                                                 sy[:, REL, 2:4, :].unsqueeze(1).to_broadcast([128, REL, 2, SIDE]), ALU.mult), img)
                    for r2 in range(1, REL):
                        w = SIDE - r2
                        link(nc.gpsimd.tensor_tensor(prod[1][:, :, :, 0:w], sy[:, 0:REL, 2:4, r2:],
                                                     sy[:, REL + r2, 2:4, 0:w].unsqueeze(1).to_broadcast([128, REL, 2, w]), ALU.mult), img)
                        add = nc.gpsimd.tensor_tensor(own_tt[:, r2:r2 + REL, :, 0:w], own_tt[:, r2:r2 + REL, :, 0:w],
                                                      prod[1][:, :, :, 0:w], ALU.add)
                        if r2 < REL - 1:
                            link(add, img)
                        else:
                            add.then_inc(G.t_sum_pool, 1)
                    assert steps[0] == TSTEPS
                    for a in range(2):
                        pool.wait_ge(G.t_sum_pool, per(img, 3, a + 1))
                        pool.wait_ge(G.t_cast1, per(img, PARTS, a + 1))
                        nc.gpsimd.tensor_tensor(own_tt, own_tt, t_view(a, 1),
                                                ALU.subtract).then_inc(G.t_sum_pool, 1)
                    for q in range(PAIRS):
                        pool.wait_ge(G.shift_ready, per(img, PAIRS, q + 1))
                        for b in range(4):
                            k4 = kv[:, 8 * b:8 * b + 8, 0:128]
                            nc.gpsimd.tensor_tensor(k4, k4, mxx[:].unsqueeze(1).to_broadcast([128, 8, 128]),
                                                    ALU.subtract).then_inc(G.sub_done, 1)
                        if q == PAIRS - 1 and not last:
                            s_back_in(img + 1)
                        pool.wait_ge(G.rz_ready, per(img, PAIRS, q + 1))
                        for b in range(4):
                            k4 = kv[:, 8 * b:8 * b + 8, 0:128]
                            nc.gpsimd.tensor_tensor(k4, k4, rz[:].unsqueeze(1).to_broadcast([128, 8, 128]),
                                                    ALU.mult).then_inc(G.norm_done, 1)

                s_back_in(0)
                with pool.Fori(0, IMAGES - 1) as img:
                    image(img, False)
                image(IMAGES - 1, True)

            @block.scalar
            def _(act):
                act.wait_ge(G.w_in, 64)
                nc.scalar.activation(strip[:].rearrange("p k x -> p (k x)"),
                                     band[0][0:GENK].rearrange("p l n a x -> p (l n a x)")[:, 0:2 * STRIP], ACT.Copy).then_inc(G.strip_ready, 1)

                def root(idx):
                    act.wait_ge(G.var_ready, per(idx, 1, 1))
                    nc.scalar.activation(tmp3[:], tmp2[:], ACT.Sqrt).then_inc(G.std_ready, 1)

                def normalise(idx):
                    act.wait_ge(G.bn_done, per(idx, 1, 1))
                    nc.scalar.activation(xn[:, 1, :].rearrange("p (y x) -> p y x", x=SIDE),
                                         xr[:, 1, :].rearrange("p (x y) -> p y x", y=SIDE), ACT.Identity,
                                         bias=mv[:, 1, 1:2], scale=mv[:, 1, 0:1]).then_inc(G.xn_ready, 1)

                def gen_tile(img, q, g):
                    job, k = JOB[g // 8], g % 8
                    if k == 0:
                        free_band(act, img, q, job)
                    act.wait_ge(G.gen_mm, per(img, 128, 32 * q + g + 1))
                    nc.scalar.activation(
                        band[int(job[1])][:, :, :, :, 8 * k:8 * k + 8].rearrange("p l n a x -> p (n a) l x"),
                        GN[:, g % 2, :].rearrange("p (x m l) -> p m l x", x=8, l=HY), ACT.Copy).then_inc(G.gen_act, 1)

                def s_part(img, a):
                    if a == 0:
                        act.wait_ge(G.sy_in, img * 32 + 32)
                        src = sy[:, 0:REL, :, :].rearrange("p k l x -> p (k l x)")
                    else:
                        act.wait_ge(G.s_sub, per(img, 2, a))
                        src = s_rest
                    nc.scalar.activation(s_parts[:, a, :], src, ACT.Copy).then_inc(G.s_cast, 1)

                def t_part(img, a, h):
                    act.wait_ge([G.t_sum_dve, G.t_sum_pool][h], per(img, 3, a + 1))
                    if a == 0:
                        act.wait_ge([G.t_sum_dve, G.t_sum_pool][1 - h], per(img, 3, 1))
                    nc.scalar.activation(t_view(a, h), tt[:, :, 2 * h:2 * h + 2, :], ACT.Copy).then_inc([G.t_cast0, G.t_cast1][h], 1)

                def exps(img, q, bs):
                    for b in bs:
                        act.wait_ge(G.sub_done, per(img, 16, 4 * q + b + 1))
                        nc.scalar.activation(kv[:, 8 * b:8 * b + 8, 0:128], kv[:, 8 * b:8 * b + 8, 0:128],
                                             ACT.Exp).then_inc(G.exp_done, 1)

                def s_tiles(img):
                    for k in range(NST):
                        act.wait_ge(G.s_mm, per(img, NST, k + 1))
                        nc.scalar.activation(stile[:, :, 4 * k:4 * k + 4, :].rearrange("p a l x -> p l a x"),
                                             ST[0:NS, k % 2, :].rearrange("p (l a x) -> p l a x", l=4, a=2),
                                             ACT.Copy).then_inc(G.s_act, 1)

                def image(img, last):
                    for q in range(PAIRS):
                        act.wait_ge(G.ctx_mm, per(img, PAIRS, q))
                        for k in range(16):
                            act.wait_ge(G.pj_mm, per(img, 64, 16 * q + k + 1))
                            nc.scalar.activation(kv[:, 2 * k:2 * k + 2, :].rearrange("p l f -> p (l f)"),
                                                 PJ[:, k % 2, :], ACT.Copy).then_inc(G.kv_evac, 1)
                            for g in EARLY[q == 0][k]:
                                gen_tile(img, q, g)
                            if q == 0 and k in CAST_AT:
                                s_part(img, CAST_AT.index(k))
                            if q == 0 and k in T_AT:
                                t_part(img, *T_AT[k])
                            if q == PAIRS - 1 and k == 14 and not last:
                                root(img + 1)
                        if q == 0:
                            t_part(img, 1, 1)
                        if q == PAIRS - 1 and not last:
                            act.wait_ge(G.pj_mm, per(img, 64, 64))
                            normalise(img + 1)
                        for work in ORDER[q == 0]:
                            half = int(work[1])
                            if work[0] == "y":
                                if work == "y1+t0":
                                    for k in range(8):
                                        gen_tile(img, q, 16 + k)
                                        if k in (2, 4, 6):
                                            exps(img, q, (k // 2 - 1,))
                                elif work == "y0+s1":
                                    for k in range(8):
                                        gen_tile(img, q, 8 + k)
                                        if k == 2:
                                            t_part(img, 2, 0)
                                        if k == 5:
                                            t_part(img, 2, 1)
                                elif q == 0:
                                    exps(img, q, range(4))
                                if q == PAIRS - 1 and half == 1 and not last:
                                    s_tiles(img + 1)
                            elif work == "t0":
                                for k in range(8):
                                    gen_tile(img, q, 16 + k)
                            else:
                                for k in range(8):
                                    n = 8 * half + k
                                    m = 8 * q + n // 2
                                    if half == 0:
                                        gen_tile(img, q, 24 + k)
                                    act.wait_ge(G.p_mm, per(img, 64, 16 * q + n + 1))
                                    if n in BOTH_AT and n > 0:
                                        act.wait_ge(G.p_head1, per(img, 64, 16 * q + n))
                                    act.wait_ge(p_out[m % SLOTS], per(img, 128, 16 * (m // SLOTS)))
                                    nc.scalar.activation(ptile[0:64, m % SLOTS, 256 * (n % 2):256 * (n % 2) + 256],
                                                         STR[n % 4][0:64, 0:256], ACT.Copy).then_inc(G.p_head0, 1)
                                    if n in BOTH_AT:
                                        nc.scalar.activation(ptile[64:128, m % SLOTS, 256 * (n % 2):256 * (n % 2) + 256],
                                                             STR[n % 4][64:128, 256:512], ACT.Copy).then_inc(G.p_head1, 1)
                                    if n == 0 and q > 0:
                                        exps(img, q, (3,))

                root(0)
                normalise(0)
                s_tiles(0)
                with act.Fori(0, IMAGES - 1) as img:
                    image(img, False)
                image(IMAGES - 1, True)

            @block.tensor
            def _(pe):
                pe.wait_ge(G.w_in, 64)
                pe.wait_ge(G.strip_ready, 1)
                pe.wait_ge(G.zeroed, 3)

                def moments(idx):
                    pe.wait_ge(G.mvp_ready, per(idx, 1, 1))
                    nc.tensor.matmul(MS[:, 0:2 * CT], group_mean[:], mv[:].rearrange("p t k -> p (t k)"),
                                     start=True, stop=True).then_inc(G.gstat_mm, 1)

                def gen_tile(img, q, g):
                    job, k = JOB[g // 8], g % 8
                    half, kind = int(job[1]), 0 if job[0] == "s" else 1
                    K = SROWS if kind == 0 else GENK
                    if k == 0:
                        pe.wait_ge(s_back[half], per(img, 32 * PAIRS, 32 * (q + 1)))
                        if kind == 1:
                            pe.wait_ge(t_back[half], per(img, 32 * PAIRS, 32 * (q + 1)))
                    pe.wait_ge(G.gen_act, per(img, 128, 32 * q + (g - 1 if g >= 2 else 0)))
                    for j in range(8):
                        x = 8 * k + j
                        last = nc.tensor.matmul(
                            GN[:, g % 2, 64 * j:64 * j + 64],
                            strip[0:K, kind, SIDE - 1 - x:3 * SIDE - 1 - x],
                            srow[0:K, :, :, HY * half:HY * (half + 1), x].rearrange("p n a l -> p (n a) l"), start=True, stop=True)
                    last.then_inc(G.gen_mm, 1)

                def band_stands(img, q, job):
                    pe.wait_ge(G.gen_act, per(img, 128, 32 * q + 8 * JOB.index(job) + 8))

                def stage(n, half, k):
                    for j in range(2):
                        yl = 2 * k + j
                        last = nc.tensor.matmul(
                            STR[n % 4].rearrange("p (n l f) -> p l n f", n=2, l=2)[:, j],
                            kv[:, HY * half + yl, 128:256],
                            band[half][:, yl, :, :, :].rearrange("p n a x -> p (n a x)"), start=True, stop=True)
                    return last

                def flush_f(img, q):
                    pe.wait_ge(G.ctx_copied, per(img, 2 * PAIRS, 2 * q + 2))
                    nc.tensor.matmul(MS[:, 256:512], ctxbd[:], wout[:, q, :], start=True, stop=True).then_inc(G.f_mm, 1)

                def flush_a(img, q):
                    pe.wait_ge(G.f_copied, per(img, PAIRS, q + 1))
                    for c in range(CT):
                        last = nc.tensor.matmul(CX[:, 256 * c:256 * c + 256], wq[:, q, 128 * c:128 * c + 128],
                                                fmat[:], start=True, stop=True)
                    last.then_inc(G.a_mm, 1)

                def s_tiles(idx):
                    pe.wait_ge(G.xn_ready, per(idx, CT, CT))
                    for k in range(NST):
                        if k >= 2:
                            pe.wait_ge(G.s_act, per(idx, NST, k - 1))
                        for c in range(CT):
                            last = nc.tensor.matmul(ST[0:NS, k % 2, :], g_t[:, c, :], xn[:, c, 512 * k:512 * k + 512],
                                                    start=(c == 0), stop=(c == CT - 1))
                        last.then_inc(G.s_mm, 1)

                def image(img, last_image):
                    for q in range(PAIRS):
                        for k in range(16):
                            if k == 0:
                                for left in (G.p_head0, G.p_head1):
                                    pe.wait_ge(left, per(img, 64, 16 * q))
                            elif k >= 2:
                                pe.wait_ge(G.kv_evac, per(img, 64, 16 * q + k - 1))
                            for j in range(2):
                                yl = 2 * k + j
                                for c in range(CT):
                                    last = nc.tensor.matmul(PJ[:, k % 2, 256 * j:256 * j + 256],
                                                            xn[:, c, 128 * yl:128 * yl + 128], wkv[:, c, q, :],
                                                            start=(c == 0), stop=(c == CT - 1))
                            last.then_inc(G.pj_mm, 1)
                            for g in EARLY[q == 0][k]:
                                gen_tile(img, q, g)
                            if q > 0 and k == 3:
                                flush_f(img, q - 1)
                            if q > 0 and k == 7:
                                flush_a(img, q - 1)
                            if q == PAIRS - 1 and k == 12 and not last_image:
                                moments(img + 1)
                        for work in ORDER[q == 0]:
                            half = int(work[1])
                            if work == "t0":
                                for k in range(8):
                                    gen_tile(img, q, 16 + k)
                            elif work[0] == "y":
                                band_stands(img, q, "s%d" % half)
                                pe.wait_ge(G.kv_evac, per(img, 64, 16 * q + 8 * (half + 1)))
                                for k in range(8):
                                    n = 8 * half + k
                                    if n >= 4:
                                        pe.wait_ge(G.y_stat, per(img, 64, 16 * q + n - 3))
                                    elif n == 2:
                                        pe.wait_ge(G.kv_evac, per(img, 64, 16 * q + 16))
                                    elif q == 0:
                                        pe.wait_ge(G.s_act, per(img, NST, NST))
                                    if work == "y1+t0":
                                        gen_tile(img, q, 16 + k)
                                    if work == "y0+s1":
                                        gen_tile(img, q, 8 + k)
                                    stage(n, half, k).then_inc(G.y_mm, 1)
                                    if n == 1:
                                        pe.wait_ge(G.max_ready, per(img, PAIRS, q + 1))
                                        nc.tensor.matmul(MS[:, 0:128], swap_half[:], mx[:], start=True, stop=True).then_inc(G.swap_mm, 1)
                                if q == PAIRS - 1 and half == 1 and not last_image:
                                    pe.wait_ge(G.y_stat, per(img, 64, 64))
                                    s_tiles(img + 1)
                            else:
                                band_stands(img, q, "t%d" % half)
                                for k in range(8):
                                    n = 8 * half + k
                                    if n >= 4:
                                        pe.wait_ge(G.p_head0, per(img, 64, 16 * q + n - 3))
                                        pe.wait_ge(G.p_head1, per(img, 64, 16 * q + n - 3))
                                    else:
                                        pe.wait_ge(G.y_stat, per(img, 64, 16 * q + 13 + n))
                                        if q == PAIRS - 1 and n == 0 and not last_image:
                                            pe.wait_ge(G.s_act, per(img + 1, NST, NST))
                                    if half == 0:
                                        gen_tile(img, q, 24 + k)
                                    stage(n, half, k).then_inc(G.p_mm, 1)
                                    if n == ZSUM_AT:
                                        pe.wait_ge(G.zsum_ready, per(img, PAIRS, q + 1))
                                        nc.tensor.matmul(MS[:, 128:256], both_halves[:], mx[:], start=True, stop=True).then_inc(G.zsum_mm, 1)
                        for yl in range(YL):
                            if yl % 8 == 0:
                                pe.wait_ge(G.norm_done, per(img, 16, 4 * q + yl // 8 + 1))
                                if yl == 0:
                                    pe.wait_ge(G.a_copied, per(img, PAIRS, q))
                            last = nc.tensor.matmul(CX[:, 0:128], kv[:, yl, 128:256], kv[:, yl, 0:128],
                                                    start=(yl == 0), stop=(yl == YL - 1))
                        last.then_inc(G.ctx_mm, 1)
                    flush_f(img, PAIRS - 1)
                    flush_a(img, PAIRS - 1)

                moments(0)
                s_tiles(0)
                with pe.Fori(0, IMAGES - 1) as img:
                    image(img, False)
                image(IMAGES - 1, True)

            @block.vector
            def _(dve):
                steps = [0]
                now = [0]
                first = [0]

                def link(ins):
                    steps[0] += 1
                    ins.then_inc(G.dve_step, 1)
                    dve.wait_ge(G.dve_step, per(now[0], DVE_STEPS, first[0] + steps[0]))

                def apart():
                    dve.sem_inc(G.apart, 1)

                def stats(idx):
                    dve.wait_ge(G.x_in, idx * 32 + 32)
                    for c in range(CT):
                        for k in range(8):
                            apart()
                            last = nc.vector.bn_stats(bnst[:, c, k, :], xr[:, c, 512 * k:512 * k + 512])
                    link(last)
                    apart()
                    nc.vector.bn_aggr(mv[:, 0, :], bnst[:, 0, :, :].rearrange("p k s -> p (k s)"))
                    link(nc.vector.bn_aggr(mv[:, 1, :], bnst[:, 1, :, :].rearrange("p k s -> p (k s)")))
                    link(nc.vector.tensor_tensor(tmp2[:], mv[:, :, 0], mv[:, :, 0], ALU.mult))
                    link(nc.vector.tensor_tensor(mv[:, :, 1], mv[:, :, 1], tmp2[:], ALU.add))
                    nc.vector.sem_inc(G.mvp_ready, 1)

                def variance(idx):
                    dve.wait_ge(G.gstat_mm, per(idx, 1, 1))
                    link(nc.vector.tensor_copy(mv[:].rearrange("p t k -> p (t k)"), MS[:, 0:2 * CT]))
                    link(nc.vector.tensor_tensor(tmp2[:], mv[:, :, 0], mv[:, :, 0], ALU.mult))
                    link(nc.vector.tensor_tensor(tmp2[:], mv[:, :, 1], tmp2[:], ALU.subtract))
                    link(nc.vector.tensor_scalar(tmp2[:], tmp2[:], 0.0, GN_EPS, ALU.max, ALU.add))
                    nc.vector.sem_inc(G.var_ready, 1)

                def scale_bias(idx):
                    dve.wait_ge(G.std_ready, per(idx, 1, 1))
                    link(nc.vector.reciprocal(tmp3[:], tmp3[:]))
                    link(nc.vector.tensor_tensor(tmp2[:], mv[:, :, 0], tmp3[:], ALU.mult))
                    nc.vector.tensor_scalar(mv[:, :, 1], tmp2[:], -1.0, None, ALU.mult)
                    link(nc.vector.tensor_copy(mv[:, :, 0], tmp3[:]))
                    link(nc.vector.tensor_copy(affine[:, ds(idx, 1), :, :].rearrange("p b t k -> p (b t k)"),
                                               mv[:].rearrange("p t k -> p (t k)")))
                    nc.vector.sem_inc(G.bn_done, 1)

                def normalise():
                    nc.vector.tensor_scalar(xn[:, 0, :].rearrange("p (y x) -> p y x", x=SIDE),
                                            xr[:, 0, :].rearrange("p (x y) -> p y x", y=SIDE),
                                            mv[:, 0, 0:1], mv[:, 0, 1:2], ALU.mult, ALU.add).then_inc(G.xn_ready, 1)

                def s_edges(img):
                    dve.wait_ge(G.bad_out, per(img, 16, 0))
                    for k in range(NST):
                        dve.wait_ge(G.s_act, per(img, NST, k + 1))
                        edge = stile[:, :, 4 * k:4 * k + 4, SIDE - EDGE:].rearrange("p a l x -> p l a x")
                        link(nc.vector.tensor_tensor(
                            sbad[:, 8 * k:8 * k + 8, :].rearrange("p (l a) x -> p l a x", a=2), edge,
                            bad_mask[:].unsqueeze(1).unsqueeze(1).to_broadcast([NS, 4, 2, EDGE]), ALU.mult))
                        nc.vector.tensor_tensor(
                            edge, edge,
                            good_mask[:].unsqueeze(1).unsqueeze(1).to_broadcast([NS, 4, 2, EDGE]), ALU.mult).then_inc(G.s_dve, 1)

                def t_product(r2):
                    w = SIDE - r2
                    if r2 == 0:
                        nc.vector.memset(tt[:, REL:, 0:2, :], 0.0)
                        link(nc.vector.tensor_tensor(tt[:, 0:REL, 0:2, :], sy[:, 0:REL, 0:2, :],
                                                     sy[:, REL, 0:2, :].unsqueeze(1).to_broadcast([128, REL, 2, SIDE]), ALU.mult))
                        return
                    link(nc.vector.tensor_tensor(prod[0][:, :, :, 0:w], sy[:, 0:REL, 0:2, r2:],
                                                 sy[:, REL + r2, 0:2, 0:w].unsqueeze(1).to_broadcast([128, REL, 2, w]), ALU.mult))
                    sum_ = tt[:, r2:r2 + REL, 0:2, 0:w]
                    link(nc.vector.tensor_tensor(sum_, sum_, prod[0][:, :, :, 0:w], ALU.add))

                def t_rest(img, a):
                    dve.wait_ge(G.t_cast0, per(img, PARTS, a + 1))
                    nc.vector.tensor_tensor(tt[:, :, 0:2, :], tt[:, :, 0:2, :], t_view(a, 0),
                                            ALU.subtract).then_inc(G.t_sum_dve, 1)

                def s_minus(img, a):
                    dve.wait_ge(G.s_cast, per(img, PARTS, a + 1))
                    if a == 1:
                        dve.wait_ge(G.s_sub, per(img, 2, 1))
                    src = sy[:, 0:REL, :, :].rearrange("p k l x -> p (k l x)") if a == 0 else s_rest
                    nc.vector.tensor_tensor(s_rest, src, s_parts[:, a, :], ALU.subtract).then_inc(G.s_sub, 1)

                def maxima(img, q, b):
                    dve.wait_ge(G.kv_evac, per(img, 64, 16 * q + MAX_CUT[b + 1] // 2))
                    return nc.vector.tensor_reduce(mxq[:, b, :], kv[:, MAX_CUT[b]:MAX_CUT[b + 1], 0:128].rearrange("p l c -> p c l"),
                                                   AX.X, ALU.max)

                def take_f(img, q):
                    dve.wait_ge(G.f_mm, per(img, PAIRS, q + 1))
                    nc.vector.tensor_copy(fmat[:], MS[:, 256:512]).then_inc(G.f_copied, 1)

                def take_a(img, q):
                    dve.wait_ge(G.a_mm, per(img, PAIRS, q + 1))
                    if q == 0:
                        dve.wait_ge(G.a_out, per(img, 16, 0))
                        nc.vector.tensor_copy(amat[:], CX[:]).then_inc(G.a_copied, 1)
                    else:
                        dve.wait_ge(G.a_copied, per(img, PAIRS, q))
                        nc.vector.tensor_tensor(amat[:], amat[:], CX[:], ALU.add).then_inc(G.a_copied, 1)

                def points_x(img, q):
                    dve.wait_ge(G.pts_in, per(img, 16 * PAIRS, 16 * (q + 1)))
                    dve.wait_ge(G.key_out, per(img, 16 * PAIRS, 16 * q))
                    link(nc.vector.tensor_scalar(pt[:, 0, :], pc[:, :, 0], -25.6, 5.0, ALU.subtract, ALU.mult))
                    link(nc.vector.tensor_scalar(pt[:, 1, :], pt[:, 0, :], MAGIC, MAGIC, ALU.add, ALU.subtract))
                    link(nc.vector.tensor_tensor(pt[:, 2, :], pt[:, 1, :], pt[:, 0, :], ALU.is_gt))
                    link(nc.vector.tensor_tensor(pt[:, 1, :], pt[:, 1, :], pt[:, 2, :], ALU.subtract))
                    link(nc.vector.tensor_scalar(pt[:, 5, :], pt[:, 1, :], float(2 * BLOCK), 1.0, ALU.mult, ALU.add))

                def points_axis(img, q, axis, low, high, inv, size, vox, cells):
                    vh = float(np.round(float(vox) * 2 ** 14) / 2 ** 14)
                    vl = float(np.float32(float(vox) - vh - float(vox) * 2.0 ** -24 * 0.75))
                    v = pc[:, :, axis]
                    nc.vector.tensor_scalar(pt[:, 1, :], v, low, None, ALU.subtract)
                    link(nc.vector.tensor_scalar(pt[:, 0, :], v, low, inv, ALU.subtract, ALU.mult))
                    link(nc.vector.tensor_scalar(pt[:, 2, :], pt[:, 0, :], MAGIC, MAGIC, ALU.add, ALU.subtract))
                    link(nc.vector.scalar_tensor_tensor(pt[:, 0, :], pt[:, 2, :], -vh, pt[:, 1, :], ALU.mult, ALU.add))
                    link(nc.vector.scalar_tensor_tensor(pt[:, 1, :], pt[:, 2, :], vl, pt[:, 0, :], ALU.mult, ALU.is_gt))
                    link(nc.vector.tensor_tensor(pt[:, 2, :], pt[:, 2, :], pt[:, 1, :], ALU.subtract))
                    link(nc.vector.tensor_scalar(pt[:, 2, :], pt[:, 2, :], float(size - 1), float(cells), ALU.min, ALU.mult))
                    link(nc.vector.tensor_tensor(pt[:, 5, :], pt[:, 5, :], pt[:, 2, :], ALU.add))
                    link(nc.vector.scalar_tensor_tensor(pt[:, 3, :], v, low, pt[:, 4, :], ALU.is_ge, ALU.mult))
                    link(nc.vector.scalar_tensor_tensor(pt[:, 4, :], v, high, pt[:, 3, :], ALU.is_lt, ALU.mult))

                def points_label(img, q):
                    link(nc.vector.tensor_scalar(pt[:, 0, :], pc[:, :, 3], 0.0, float(NL - 1), ALU.max, ALU.min))
                    link(nc.vector.tensor_scalar(pt[:, 1, :], pt[:, 0, :], MAGIC, MAGIC, ALU.add, ALU.subtract))
                    link(nc.vector.tensor_tensor(pt[:, 2, :], pt[:, 1, :], pt[:, 0, :], ALU.is_gt))
                    link(nc.vector.tensor_tensor(pt[:, 1, :], pt[:, 1, :], pt[:, 2, :], ALU.subtract))
                    link(nc.vector.tensor_tensor(pt[:, 5, :], pt[:, 5, :], pt[:, 1, :], ALU.add))
                    link(nc.vector.memset(pt[:, 4, :], 1.0))

                def points_top(img, q):
                    nc.vector.sem_inc(G.unit_read, 1)
                    link(nc.vector.tensor_tensor(pt[:, 5, :], pt[:, 5, :], pt[:, 4, :], ALU.mult))
                    link(nc.vector.scalar_tensor_tensor(pt[:, 0, :], pt[:, 5, :], float(NX * 2 * BLOCK), pt[:, 5, :],
                                                        ALU.is_le, ALU.mult))
                    link(nc.vector.tensor_scalar(pt[:, 5, :], pt[:, 0, :], 0.0, None, ALU.max))
                    nc.vector.sem_inc(G.key_ready, 1)
                    src = pt[:, 5, :]
                    dve.wait_ge(G.top_out, per(img, 16 * PAIRS, 16 * q))
                    for k in range(3):
                        apart()
                        link(nc.vector.max(top24[:, 8 * k:8 * k + 8], src))
                        if k < 2:
                            apart()
                            link(nc.vector.match_replace(pt[:, k, :], top24[:, 8 * k:8 * k + 8], src, 0.0))
                            src = pt[:, k, :]
                    nc.vector.sem_inc(G.top_ready, 1)

                def points_xl(img, c):
                    points_x(img, c)
                    points_label(img, c)

                def points_y(img, c):
                    points_axis(img, c, 1, -25.6, 25.6, 5.0, NY, VY, ZL)

                def points_z(img, c):
                    points_axis(img, c, 2, -2.0, float(np.float32(1.2)), 10.0, NZ, np.float32(0.1), NL)

                def image(img, last):
                    now[0] = img
                    steps[0] = 0
                    for q in range(PAIRS):
                        if q == 0:
                            dve.wait_ge(G.sy_in, img * 32 + 32)
                            dve.wait_ge(G.tp_out, per(img, 48, 0))
                            apart()
                            t_product(0)
                            s_minus(img, 0)
                            t_product(1)
                            t_product(2)
                            s_minus(img, 1)
                            for r2 in range(3, REL):
                                t_product(r2)
                            nc.vector.sem_inc(G.t_sum_dve, 1)
                        for b in range(4):
                            last_max = maxima(img, q, b)
                            if q == 0 and b == 2:
                                t_rest(img, 0)
                            if q == PAIRS - 1 and not last:
                                if b == 0:
                                    variance(img + 1)
                                if b == 2:
                                    scale_bias(img + 1)
                        link(last_max)
                        nc.vector.tensor_reduce(mx[:], mxq[:].rearrange("p b c -> p c b"), AX.X, ALU.max).then_inc(G.max_ready, 1)
                        if q == 0:
                            t_rest(img, 1)
                        if q == PAIRS - 1 and not last:
                            dve.wait_ge(G.pj_mm, per(img, 64, 64))
                            normalise()
                        for job in ("y0", "y1", "p0", "p1"):
                            if job[0] == "y":
                                for k in range(8):
                                    n = 8 * int(job[1]) + k
                                    dve.wait_ge(G.y_mm, per(img, 64, 16 * q + n + 1))
                                    for h in range(2):
                                        apart()
                                        st = nc.vector.bn_stats(ybn[64 * h:64 * h + 64, n, :],
                                                                STR[n % 4][64 * h:64 * h + 64, 256 * h:256 * h + 256])
                                    st.then_inc(G.y_stat, 1)
                                    if n == 1:
                                        dve.wait_ge(G.swap_mm, per(img, PAIRS, q + 1))
                                        nc.vector.tensor_tensor(mxx[:], mx[:], MS[:, 0:128], ALU.max).then_inc(G.shift_ready, 1)
                                if q == PAIRS - 1 and job == "y1" and not last:
                                    s_edges(img + 1)
                            else:
                                for k in range(8):
                                    n = 8 * int(job[1]) + k
                                    m = 8 * q + n // 2
                                    if n not in BOTH_AT:
                                        dve.wait_ge(G.p_mm, per(img, 64, 16 * q + n + 1))
                                        dve.wait_ge(p_out[m % SLOTS], per(img, 128, 16 * (m // SLOTS)))
                                        dve.wait_ge(G.p_head1, per(img, 64, 16 * q + n))
                                        nc.vector.tensor_copy(ptile[64:128, m % SLOTS, 256 * (n % 2):256 * (n % 2) + 256],
                                                              STR[n % 4][64:128, 256:512]).then_inc(G.p_head1, 1)
                                    if n in SUM_AT:
                                        b = SUM_AT.index(n)
                                        dve.wait_ge(G.exp_done, per(img, 16, 4 * q + b + 1))
                                        part = nc.vector.tensor_reduce(
                                            mxq[:, b, :], kv[:, 8 * b:8 * b + 8, 0:128].rearrange("p l c -> p c l"), AX.X, ALU.add)
                                        if b == 3:
                                            link(part)
                                            nc.vector.tensor_reduce(mx[:], mxq[:].rearrange("p b c -> p c b"), AX.X, ALU.add)\
                                                .then_inc(G.zsum_ready, 1)
                                    if n == ZSUM_AT + 1:
                                        dve.wait_ge(G.zsum_mm, per(img, PAIRS, q + 1))
                                        nc.vector.reciprocal(rz[:], MS[:, 128:256]).then_inc(G.rz_ready, 1)
                        dve.wait_ge(G.y_stat, per(img, 64, 16 * q + 16))
                        apart()
                        link(nc.vector.bn_aggr(mvy[:], ybn[:].rearrange("p k s -> p (k s)")))
                        link(nc.vector.tensor_copy(ustat[:, ds(img * PAIRS + q, 1), :].rearrange("p u k -> p (u k)"), mvy[:]))
                        if q == 0:
                            points_xl(img, 0)
                            points_y(img, 0)
                            take_ctx(img, q)
                            points_z(img, 0)
                            points_top(img, 0)
                            take_f(img, q)
                            points_xl(img, 1)
                            take_a(img, q)
                            points_y(img, 1)
                        elif q == 1:
                            points_z(img, 1)
                            points_top(img, 1)
                            take_ctx(img, q)
                            points_xl(img, 2)
                            points_y(img, 2)
                            take_f(img, q)
                            points_z(img, 2)
                            take_a(img, q)
                            points_top(img, 2)
                        elif q == 2:
                            points_xl(img, 3)
                            points_y(img, 3)
                            take_ctx(img, q)
                            points_z(img, 3)
                            points_top(img, 3)
                            take_f(img, q)
                            if not last:
                                stats(img + 1)
                            take_a(img, q)
                        else:
                            take_ctx(img, q)
                            take_f(img, q)
                            take_a(img, q)

                def take_ctx(img, q):
                    dve.wait_ge(G.ctx_mm, per(img, PAIRS, q + 1))
                    for h in range(2):
                        nc.vector.tensor_copy(ctxbd[64 * h:64 * h + 64, 64 * h:64 * h + 64],
                                              CX[64 * h:64 * h + 64, 64 * h:64 * h + 64]).then_inc(G.ctx_copied, 1)

                stats(0)
                dve.wait_ge(G.w_in, 64)
                dve.wait_ge(G.zeroed, 3)
                variance(0)
                scale_bias(0)
                normalise()
                s_edges(0)
                first[0] = steps[0]
                with dve.Fori(0, IMAGES - 1) as img:
                    image(img, False)
                    assert steps[0] == DVE_STEPS
                image(IMAGES - 1, True)


def histogram_and_pass2(nc, t, e):
    fp32, bf16, fp16, i32 = mybir.dt.float32, mybir.dt.bfloat16, mybir.dt.float16, mybir.dt.int32
    ALU, ACT, AX = mybir.AluOpType, mybir.ActivationFunctionType, mybir.AxisListType
    ds = bass.ds
    sb, sem = e["sb"], e["sem"]
    PJ, GN, ST, CX, MS = e["PJ"], e["GN"], e["ST"], e["CX"], e["MS"]
    block_lo, block_hi, cand_dram, keys_dram = e["block_lo"], e["block_hi"], e["cand_dram"], e["keys_dram"]
    SLOTS = NX + 2
    with ExitStack() as own:
        hist = sb(own, "hist", [128, SLOTS * 2 * HROW])
        x_even = sb(own, "x_even", [128, CT, PIX])
        x_even_in = sem("out_x_in0")

        with ExitStack() as tmp:
            cand = sb(tmp, "cand", [PROWS, NCHUNK, TOP])
            work = sb(tmp, "work", [PROWS, 2, 2, NCHUNK * TOP])
            best = sb(tmp, "best", [PROWS, 2, SET])
            gbest = sb(tmp, "gbest", [PROWS, 2, GTOP])
            kept = sb(tmp, "kept", [PROWS, GROUPS, GTOP])
            sets = sb(tmp, "sets", [PROWS, BLOCKS, SET])
            over = sb(tmp, "over", [PROWS, 6])
            overb = sb(tmp, "overb", [PROWS, BLOCKS])
            ones = sb(tmp, "ones", [PROWS, 1])
            full = sb(tmp, "full", [1, 1])
            control = sb(tmp, "control", [1, 4], i32)
            kset = sb(tmp, "kset", [PROWS, 2, SET])
            rel = sb(tmp, "rel", [PROWS, SET])
            tq = sb(tmp, "tq", [PROWS, SET])
            yrow = sb(tmp, "yrow", [PROWS, 2, SET])
            zlab = sb(tmp, "zlab", [PROWS, 2, SET])
            index = sb(tmp, "index", [PROWS, ZL])
            index16 = sb(tmp, "index16", [PROWS, ZL], fp16)
            NG = SET // OHG
            ydist = sb(tmp, "ydist", [PROWS, OHG, 128])
            hoty = sb(tmp, "hoty", [PROWS, NG, OHG, 128], bf16)
            hotz = sb(tmp, "hotz", [PROWS, NG, OHG, ZL], bf16)
            names = ("idx_in apart sort_step flags_ready over_mm control_ready sets_ready sets_out set_in0 set_in1 set_read "
                     "hotz_ready hoty_pool hoty_act hoty_abs hot_used hist_mm hist_added hist_zero decode_step pool_apart sp_apart").split()
            G = type("Sems", (), {n: sem("hist_" + n) for n in names})
            SORT = 1 + 2 * (SET // 8)
            GSORT = 1 + 2 * (GTOP // 8)
            SORTED = GROUPS * GSORT + BLOCKS * SORT
            INDEX_STEP = SORTED + 8
            DEC = 4

            OWNER = ("PAPA", "PAAA")

            def made(pair, j, g):
                who = OWNER[j][g]
                return pair * (OWNER[0] + OWNER[1]).count(who) + (OWNER[0] + OWNER[1])[:j * NG + g + 1].count(who)

            def group_free(eng, it, g):
                if g < NG - 1:
                    eng.wait_ge(G.hot_used, it * (NG - 1) + g + 1)
                else:
                    eng.wait_ge(G.hist_mm, it + 1)

            PSUM = [PJ[:].rearrange("p b f -> p (b f)")[:, 0:ZL], GN[:].rearrange("p b f -> p (b f)")[:, 0:ZL]]

            with nc.Block() as block:
                @block.sync
                def _(sp):
                    sp.dma_start(cand[:].rearrange("p n k -> p (n k)"), cand_dram).then_inc(G.idx_in, 16)
                    sp.dma_start(index[:], t["index"][0:PROWS, :]).then_inc(G.idx_in, 16)
                    for c in range(CT):
                        sp.dma_start(x_even[:, c, :], e["x_dram"][0:1, :, c, :].rearrange("b p f -> (b p) f")).then_inc(x_even_in, 16)
                    sp.wait_ge(G.sets_ready, 1)
                    sp.dma_start(keys_dram[:, 0:BLOCKS * SET], sets[:].rearrange("p b k -> p (b k)")).then_inc(G.sets_out, 16)
                    sp.wait_ge(G.sets_out, 16)
                    sp.wait_ge(G.control_ready, 1)
                    rounds = sp.value_load(control[0:1, 0:1], min_val=1, max_val=PCOLS // SET)
                    stride = sp.value_load(control[0:1, 1:2], min_val=0, max_val=SET)
                    base = sp.value_load(control[0:1, 2:3], min_val=0, max_val=BLOCKS * SET)
                    with sp.Fori(0, rounds) as r:
                        with sp.Fori(0, BLOCKS // 2) as half:
                            for j in range(2):
                                sp.wait_ge(G.set_read, r * BLOCKS + half * 2 + j + 1)
                                sp.dma_start(kset[:, j, :], keys_dram[:, ds(base + r * SET + (half * 2 + j) * stride, SET)])\
                                  .then_inc([G.set_in0, G.set_in1][j], 16)
                    sp.wait_ge(G.set_read, rounds * BLOCKS + 2)
                    sp.sem_inc(G.sp_apart, 1)
                    for j in range(2):
                        sp.dma_start(kset[:, j, :], keys_dram[:, ds(base, SET)]).then_inc([G.set_in0, G.set_in1][j], 16)

                @block.gpsimd
                def _(pool):
                    nc.gpsimd.memset(hist[:], 0.0).then_inc(G.hist_zero, 1)
                    pool.wait_ge(G.control_ready, 1)
                    pool.wait_ge(G.sort_step, INDEX_STEP)
                    rounds = pool.value_load(control[0:1, 0:1], min_val=1, max_val=PCOLS // SET)
                    with pool.Fori(0, rounds) as r:
                        with pool.Fori(0, BLOCKS // 2) as half:
                            for j in range(2):
                                it = r * BLOCKS + half * 2 + j
                                pool.wait_ge(G.decode_step, it * DEC + 3)
                                for g in [g for g in range(NG) if OWNER[j][g] == "P"]:
                                    group_free(pool, it, g)
                                    pool.sem_inc(G.pool_apart, 1)
                                    for k in range(OHG):
                                        c = g * OHG + k
                                        hot = nc.gpsimd.tensor_scalar(hoty[:, g, k, :], index16[:, 0:128], yrow[:, j, c:c + 1], None,
                                                                      ALU.is_equal)
                                    hot.then_inc(G.hoty_pool, 1)

                @block.scalar
                def _(act):
                    act.sem_inc(G.hoty_act, 1)
                    act.wait_ge(G.control_ready, 1)
                    act.wait_ge(G.sort_step, INDEX_STEP)
                    rounds = act.value_load(control[0:1, 0:1], min_val=1, max_val=PCOLS // SET)
                    with act.Fori(0, rounds) as r:
                        with act.Fori(0, BLOCKS // 2) as half:
                            for j in range(2):
                                it = r * BLOCKS + half * 2 + j
                                act.wait_ge(G.decode_step, it * DEC + 3)
                                for g in [g for g in range(NG) if OWNER[j][g] == "A"]:
                                    n = made(r * (BLOCKS // 2) + half, j, g) - 1
                                    act.wait_ge(G.hoty_act, n + 1)
                                    for k in range(OHG):
                                        c = g * OHG + k
                                        dist = nc.scalar.activation(ydist[:, k, :], index[:, 0:128], ACT.Abs,
                                                                    bias=yrow[:, j, c:c + 1], scale=-1.0)
                                    dist.then_inc(G.hoty_abs, 1)
                                    act.wait_ge(G.hoty_abs, n + 1)
                                    group_free(act, it, g)
                                    nc.scalar.activation(hoty[:, g, :, :].rearrange("p k y -> p (k y)"),
                                                         ydist[:].rearrange("p k y -> p (k y)"), ACT.Relu,
                                                         bias=ones[:], scale=-1.0).then_inc(G.hoty_act, 1)

                @block.tensor
                def _(pe):
                    pe.sem_inc(G.hot_used, NG - 1)
                    pe.sem_inc(G.hist_mm, 1)
                    pe.wait_ge(G.flags_ready, 1)
                    nc.tensor.matmul(CX[0:1, 0:1], over[:, 3:4], ones[:], start=True, stop=True).then_inc(G.over_mm, 1)
                    pe.wait_ge(G.control_ready, 1)
                    rounds = pe.value_load(control[0:1, 0:1], min_val=1, max_val=PCOLS // SET)
                    with pe.Fori(0, rounds) as r:
                        with pe.Fori(0, BLOCKS // 2) as half:
                            for j in range(2):
                                pe.wait_ge(G.hist_added, r * BLOCKS + half * 2 + j + 1)
                                for g in range(NG):
                                    i = j * NG + g
                                    pe.wait_ge(G.hotz_ready, r * (BLOCKS * NG) + half * (2 * NG) + i + 1)
                                    n = made(r * (BLOCKS // 2) + half, j, g)
                                    if OWNER[j][g] == "A":
                                        pe.wait_ge(G.hoty_act, n + 1)
                                    else:
                                        pe.wait_ge(G.hoty_pool, n)
                                    for k in range(OHG):
                                        first, last = g == 0 and k == 0, g == NG - 1 and k == OHG - 1
                                        nc.tensor.matmul(PSUM[j][:, 0:512], hoty[:, g, k, :], hotz[:, g, k, 0:512],
                                                         start=first, stop=last)
                                        mm = nc.tensor.matmul(PSUM[j][:, 512:ZL], hoty[:, g, k, :], hotz[:, g, k, 512:ZL],
                                                              start=first, stop=last)
                                    if g < NG - 1:
                                        mm.then_inc(G.hot_used, 1)
                                    else:
                                        mm.then_inc(G.hist_mm, 1)

                @block.vector
                def _(dve):
                    steps = [0]

                    def link(ins, base):
                        steps[0] += 1
                        ins.then_inc(G.sort_step, 1)
                        dve.wait_ge(G.sort_step, base + steps[0])

                    dve.sem_inc(G.hist_added, 2)
                    dve.sem_inc(G.set_read, 2)
                    nc.vector.memset(ones[:], 1.0)
                    dve.wait_ge(G.idx_in, 32)
                    def turn(ins):
                        steps[0] += 1
                        ins.then_inc(G.sort_step, 1)

                    def own_last_done(base):
                        dve.wait_ge(G.sort_step, base + (steps[0] - 1))
                        dve.sem_inc(G.apart, 1)

                    W = NCHUNK // GROUPS * TOP
                    with dve.Fori(0, GROUPS // 2) as pair:
                        steps[0] = 0
                        base = pair * (2 * GSORT)
                        for j in range(2):
                            turn(nc.vector.tensor_copy(work[:, j, 0, 0:W].rearrange("p (n k) -> p n k", k=TOP),
                                                       cand[:, ds((pair * 2 + j) * (NCHUNK // GROUPS), NCHUNK // GROUPS), :]))
                        for k in range(GTOP // 8):
                            for j in range(2):
                                own_last_done(base)
                                turn(nc.vector.max(gbest[:, j, 8 * k:8 * k + 8], work[:, j, k % 2, 0:W]))
                            if k < GTOP // 8 - 1:
                                for j in range(2):
                                    own_last_done(base)
                                    turn(nc.vector.match_replace(work[:, j, 1 - k % 2, 0:W], gbest[:, j, 8 * k:8 * k + 8],
                                                                 work[:, j, k % 2, 0:W], 0.0))
                        for j in range(2):
                            own_last_done(base)
                            turn(nc.vector.tensor_copy(kept[:, ds(pair * 2 + j, 1), :].rearrange("p b k -> p (b k)"), gbest[:, j, :]))
                        assert steps[0] == 2 * GSORT
                    dve.wait_ge(G.sort_step, GROUPS * GSORT)
                    all_kept = kept[:].rearrange("p n k -> p (n k)")
                    W = GROUPS * GTOP
                    with dve.Fori(0, BLOCKS // 2) as pair:
                        steps[0] = 0
                        base = pair * (2 * SORT) + GROUPS * GSORT
                        for j in range(2):
                            turn(nc.vector.scalar_tensor_tensor(work[:, j, 0, 0:W], all_kept, block_hi[0:PROWS, ds(pair * 2 + j, 1)],
                                                                all_kept, ALU.is_lt, ALU.mult))
                        for k in range(SET // 8):
                            for j in range(2):
                                own_last_done(base)
                                turn(nc.vector.max(best[:, j, 8 * k:8 * k + 8], work[:, j, k % 2, 0:W]))
                            if k < SET // 8 - 1:
                                for j in range(2):
                                    own_last_done(base)
                                    turn(nc.vector.match_replace(work[:, j, 1 - k % 2, 0:W], best[:, j, 8 * k:8 * k + 8],
                                                                 work[:, j, k % 2, 0:W], 0.0))
                        for j in range(2):
                            own_last_done(base)
                            turn(nc.vector.tensor_copy(sets[:, ds(pair * 2 + j, 1), :].rearrange("p b k -> p (b k)"), best[:, j, :]))
                        assert steps[0] == 2 * SORT
                    dve.wait_ge(G.sort_step, SORTED)
                    nc.vector.sem_inc(G.sets_ready, 1)
                    steps[0] = 0
                    now = SORTED
                    link(nc.vector.tensor_reduce(over[:, 0:1], cand[:, :, TOP - 1], AX.X, ALU.max), now)
                    link(nc.vector.tensor_reduce(over[:, 4:5], kept[:, :, GTOP - 1], AX.X, ALU.max), now)
                    link(nc.vector.tensor_tensor(over[:, 5:6], over[:, 0:1], over[:, 4:5], ALU.max), now)
                    link(nc.vector.tensor_scalar(over[:, 1:2], over[:, 5:6], 0.0, None, ALU.is_gt), now)
                    link(nc.vector.tensor_tensor(overb[:], sets[:, :, SET - 1], block_lo[0:PROWS, 0:BLOCKS], ALU.is_ge), now)
                    link(nc.vector.tensor_reduce(over[:, 2:3], overb[:], AX.X, ALU.max), now)
                    nc.vector.tensor_tensor(over[:, 3:4], over[:, 1:2], over[:, 2:3], ALU.max).then_inc(G.flags_ready, 1)
                    dve.wait_ge(G.over_mm, 1)
                    link(nc.vector.tensor_scalar(full[:], CX[0:1, 0:1], 1.0, None, ALU.min), now)
                    nc.vector.tensor_scalar(control[:, 0:1], full[:], float(PCOLS // SET - 1), 1.0, ALU.mult, ALU.add)
                    nc.vector.tensor_scalar(control[:, 1:2], full[:], -float(SET), float(SET), ALU.mult, ALU.add)
                    nc.vector.tensor_scalar(control[:, 2:3], full[:], float(BLOCKS * SET), None, ALU.mult).then_inc(G.control_ready, 1)
                    link(nc.vector.tensor_copy(index16[:], index[:]), now)
                    dve.wait_ge(G.control_ready, 1)
                    dve.wait_ge(G.hist_zero, 1)
                    rounds = dve.value_load(control[0:1, 0:1], min_val=1, max_val=PCOLS // SET)
                    def decode(pair, b, j):
                        it = pair * 2 + j
                        dve.wait_ge([G.set_in0, G.set_in1][j], pair * 16 + 16)
                        nc.vector.tensor_scalar(rel[:], kset[:, j, :], block_lo[0:PROWS, ds(b, 1)], None,
                                                ALU.subtract).then_inc(G.decode_step, 1)
                        dve.wait_ge(G.decode_step, it * DEC + 1)
                        nc.vector.tensor_scalar(tq[:], rel[:], (ZL - 1) / 2, 1.0 / ZL, ALU.subtract, ALU.mult)\
                          .then_inc(G.decode_step, 1)
                        dve.wait_ge(G.decode_step, it * DEC + 2)
                        nc.vector.tensor_scalar(yrow[:, j, :], tq[:], MAGIC, MAGIC, ALU.add, ALU.subtract)\
                          .then_inc(G.decode_step, 1)
                        dve.wait_ge(G.decode_step, it * DEC + 3)
                        nc.vector.scalar_tensor_tensor(zlab[:, j, :], yrow[:, j, :], -float(ZL), rel[:], ALU.mult, ALU.add)\
                          .then_inc(G.decode_step, 1)
                        dve.wait_ge(G.decode_step, it * DEC + 4)
                        nc.vector.sem_inc(G.set_read, 1)

                    def one_hots(r, half, j, groups):
                        it = r * BLOCKS + half * 2 + j
                        for g in groups:
                            group_free(dve, it, g)
                            for k in range(OHG):
                                c = g * OHG + k
                                hot = nc.vector.tensor_scalar(hotz[:, g, k, :], index16[:], zlab[:, j, c:c + 1], None,
                                                              ALU.is_equal)
                            hot.then_inc(G.hotz_ready, 1)

                    def add(r, half, j):
                        it = r * BLOCKS + half * 2 + j
                        b = half * 2 + j
                        dve.wait_ge(G.hist_mm, it + 2)
                        row = hist[:, ds((b + 2) * HROW + NL, ZL)]
                        nc.vector.tensor_tensor(row, row, PSUM[j], ALU.add).then_inc(G.hist_added, 1)

                    for j in range(2):
                        decode(0, j, j)
                    with dve.Fori(0, rounds) as r:
                        with dve.Fori(0, BLOCKS // 2) as half:
                            one_hots(r, half, 0, range(NG))
                            one_hots(r, half, 1, range(NG // 2))
                            add(r, half, 0)
                            one_hots(r, half, 1, range(NG // 2, NG))
                            pair = r * (BLOCKS // 2) + half
                            dve.wait_ge(G.hoty_pool, made(pair, 1, 0))
                            dve.wait_ge(G.hoty_act, made(pair, 1, NG - 1) + 1)
                            dve.wait_ge(G.hotz_ready, pair * (2 * NG) + 2 * NG)
                            for j in range(2):
                                decode(pair + 1, half * 2 + (2 + j), j)
                            add(r, half, 1)

        pass2(nc, t, e, own, hist, x_even, x_even_in)


def pass2(nc, t, e, own, hist, x_even, x_even_in):
    fp32 = mybir.dt.float32
    ALU, ACT, AX = mybir.AluOpType, mybir.ActivationFunctionType, mybir.AxisListType
    ds = bass.ds
    sb, sem = e["sb"], e["sem"]
    PJ, GN, ST, CX, MS = e["PJ"], e["GN"], e["ST"], e["CX"], e["MS"]
    wout, g_t, g_n, affine, ustat, group_mean = (e[k] for k in ("wout", "g_t", "g_n", "affine", "ustat", "group_mean"))
    both_halves = e["both_halves"]
    gamma, beta, b_out = e["gamma"], e["beta"], e["b_out"]
    bad_dram, a_dram, p_dram, x_dram, out_dram, edge_dram = (
        e[k] for k in ("bad_dram", "a_dram", "p_dram", "x_dram", "out_dram", "edge_dram"))

    wouta = sb(own, "wouta", [128, PAIRS, CHANNELS])
    edge_u = sb(own, "edge_u", [NS, CHANNELS])
    edge_neg = sb(own, "edge_neg", [NS, CHANNELS])
    ug = sb(own, "ug", [128, CT * CHANNELS])
    taps = sb(own, "taps", [128, 9, 128])
    cross = sb(own, "cross", [9, 2, 128])

    with ExitStack() as tmp:
        mask_cols = sb(tmp, "mask_cols", [128, PAIRS, NS])
        ccols = sb(tmp, "ccols", [128, PAIRS, NS])
        shift = sb(tmp, "shift", [128, 3, 128])
        crossm = sb(tmp, "crossm", [9, 2, 128])
        wedge = sb(tmp, "wedge", [9, 2])
        filt = sb(tmp, "filt", [128, 27])
        fexp = sb(tmp, "fexp", [128, 27])
        mom = sb(tmp, "mom", [128, 2, NCHUNK])
        moms = sb(tmp, "moms", [128, 2])
        bn = sb(tmp, "bn", [128, 8])
        tacc = sb(tmp, "tacc", [128, 2, 128])
        names = "pre_in mom_ready mom_mm bn_var bn_std c_ready u_mm u_copied ug_mm ug_copied exp_out pre_step edge_out".split()
        G = type("Sems", (), {n: sem("pre_" + n) for n in names})
        with nc.Block() as block:
            @block.sync
            def _(sp):
                sp.dma_start(mask_cols[:].rearrange("p q s -> p (q s)"), t["head_mask_cols"]).then_inc(G.pre_in, 16)
                sp.dma_start(shift[:].rearrange("p b f -> p (b f)"), t["shift"]).then_inc(G.pre_in, 16)
                sp.dma_start(crossm[:].rearrange("p b f -> p (b f)"), t["cross"]).then_inc(G.pre_in, 16)
                sp.dma_start(filt[:], t["conv_w"].to_broadcast([128, 27])).then_inc(G.pre_in, 16)
                sp.dma_start(wedge[:], t["conv_edge"]).then_inc(G.pre_in, 16)
                slots = hist[:].rearrange("p (s h f) -> p s h f", h=2, f=HROW)
                for o, row in enumerate((0, 127)):
                    sp.dma_start(edge_dram[:, o, :].unsqueeze(0), slots[row:row + 1, :, 1 - o, :]).then_inc(G.edge_out, 16)
                sp.wait_ge(G.edge_out, 32)

            @block.scalar
            def _(act):
                act.wait_ge(G.pre_in, 80)
                nc.scalar.activation(fexp[:], filt[:], ACT.Exp, scale=-1.0).then_inc(G.exp_out, 1)
                nc.scalar.activation(wedge[:], wedge[:], ACT.Exp, scale=-1.0).then_inc(G.exp_out, 1)
                act.wait_ge(G.bn_var, 1)
                nc.scalar.activation(bn[:, 4:5], bn[:, 3:4], ACT.Sqrt).then_inc(G.bn_std, 1)

            @block.tensor
            def _(pe):
                pe.wait_ge(G.mom_ready, 1)
                nc.tensor.matmul(MS[:, 0:2], both_halves[:], moms[:], start=True, stop=True).then_inc(G.mom_mm, 1)
                pe.wait_ge(G.c_ready, 1)
                for q in range(PAIRS):
                    mm = nc.tensor.matmul(CX[0:NS, 0:CHANNELS], ccols[:, q, :], wout[:, q, :], start=(q == 0), stop=(q == PAIRS - 1))
                mm.then_inc(G.u_mm, 1)
                pe.wait_ge(G.u_copied, 2)
                for c in range(CT):
                    mm = nc.tensor.matmul(CX[:, 256 * c:256 * c + 256], g_n[:, 128 * c:128 * c + 128], edge_u[:], start=True, stop=True)
                mm.then_inc(G.ug_mm, 1)

            @block.vector
            def _(dve):
                steps = [0]

                def link(ins):
                    steps[0] += 1
                    ins.then_inc(G.pre_step, 1)
                    dve.wait_ge(G.pre_step, steps[0])

                def build_taps(a):
                    for c in range(3):
                        tap = lambda b: filt[:, 9 * a + 3 * b + c:9 * a + 3 * b + c + 1]
                        link(nc.vector.tensor_scalar(tacc[:, 0, :], shift[:, 0, :], tap(0), None, ALU.mult))
                        link(nc.vector.scalar_tensor_tensor(tacc[:, 1, :], shift[:, 1, :], tap(1), tacc[:, 0, :], ALU.mult, ALU.add))
                        link(nc.vector.scalar_tensor_tensor(taps[:, 3 * a + c, :], shift[:, 2, :], tap(2), tacc[:, 1, :], ALU.mult, ALU.add))

                link(nc.vector.tensor_tensor(mom[:, 1, :], ustat[:, :, 0], ustat[:, :, 0], ALU.mult))
                nc.vector.tensor_copy(mom[:, 0, :], ustat[:, :, 0])
                link(nc.vector.tensor_tensor(mom[:, 1, :], mom[:, 1, :], ustat[:, :, 1], ALU.add))
                nc.vector.tensor_reduce(moms[:], mom[:], AX.X, ALU.add).then_inc(G.mom_ready, 1)
                dve.wait_ge(G.exp_out, 2)
                link(nc.vector.tensor_scalar(wedge[:], wedge[:], 1.0, None, ALU.add))
                link(nc.vector.reciprocal(wedge[:], wedge[:]))
                for o in range(2):
                    nc.vector.tensor_scalar(cross[:, o, :], crossm[:, o, :], wedge[:, o:o + 1], None, ALU.mult)
                link(nc.vector.tensor_scalar(fexp[:], fexp[:], 1.0, None, ALU.add))
                link(nc.vector.reciprocal(filt[:], fexp[:]))
                link(nc.vector.memset(filt[:, 13:14], 1.0))
                build_taps(0)
                dve.wait_ge(G.mom_mm, 1)
                link(nc.vector.tensor_scalar(bn[:, 0:2], MS[:, 0:2], 1.0 / (2 * NCHUNK), None, ALU.mult))
                link(nc.vector.tensor_tensor(bn[:, 2:3], bn[:, 0:1], bn[:, 0:1], ALU.mult))
                link(nc.vector.tensor_tensor(bn[:, 2:3], bn[:, 1:2], bn[:, 2:3], ALU.subtract))
                nc.vector.tensor_scalar(bn[:, 3:4], bn[:, 2:3], 0.0, BN_EPS, ALU.max, ALU.add).then_inc(G.bn_var, 1)
                build_taps(1)
                dve.wait_ge(G.bn_std, 1)
                link(nc.vector.reciprocal(bn[:, 5:6], bn[:, 4:5]))
                link(nc.vector.tensor_tensor(bn[:, 5:6], bn[:, 5:6], gamma[:], ALU.mult))
                link(nc.vector.tensor_tensor(bn[:, 6:7], bn[:, 0:1], bn[:, 5:6], ALU.mult))
                link(nc.vector.tensor_tensor(bn[:, 6:7], beta[:], bn[:, 6:7], ALU.subtract))
                nc.vector.tensor_scalar(wouta[:], wout[:], bn[:, 5:6], None, ALU.mult)
                dve.wait_ge(G.pre_in, 80)
                nc.vector.tensor_scalar(ccols[:], mask_cols[:], bn[:, 6:7], None, ALU.mult).then_inc(G.c_ready, 1)
                build_taps(2)
                dve.wait_ge(G.u_mm, 1)
                nc.vector.tensor_copy(edge_u[:], CX[0:NS, 0:CHANNELS]).then_inc(G.u_copied, 1)
                nc.vector.tensor_scalar(edge_neg[:], CX[0:NS, 0:CHANNELS], -1.0, None, ALU.mult).then_inc(G.u_copied, 1)
                dve.wait_ge(G.ug_mm, 1)
                nc.vector.tensor_copy(ug[:], CX[:])
    xr = [x_even, sb(own, "x_odd", [128, CT, PIX])]
    xn = sb(own, "xn2", [128, CT, PIX])
    ptile = sb(own, "ptile2", [128, 2, PAIRS, 512])
    at = sb(own, "at", [128, 2, CT * CHANNELS])
    sbad = sb(own, "sbad2", [NS, 2, SIDE * EDGE])
    bnst = sb(own, "bnst2", [128, CT, 8, 6])
    mv = sb(own, "mv2", [128, CT, 2])
    aff = sb(own, "aff2", [128, CT, 2])
    tmp2 = sb(own, "tmp22", [128, CT])
    std = sb(own, "std2", [128, CT])
    hedge = sb(own, "hedge", [9, 2, (NZ + 1) * NL])
    names = ("x_in1 a_in0 a_in1 p_in0 p_in1 at_ready xn_ready o_mm o_evac p_used stat_ready stat_mm var_ready std_ready aff_ready apart "
             "scaled conv_mm conv_added stored0 stored1 step stat_read edge_in credited").split()
    G = type("Sems", (), {"x_in0": x_even_in, **{n: sem("out_" + n) for n in names}})
    STEPS = 20
    OPS = [PJ[:, 0, :], PJ[:, 1, :], GN[:, 0, :], GN[:, 1, :]]
    CPS = [ST[:, 0, :], ST[:, 1, :], CX[:], MS[:]]
    ZCUT = [(0, ZA), (ZA, NZ + 1 - ZA)]

    def past(n):
        return n + 1

    with nc.Block() as block:
        @block.sync
        def _(sp):
            for s in (G.o_evac, G.conv_added, G.p_used, G.stored0, G.stored1, G.stat_read, G.credited):
                sp.sem_inc(s, 1)
            sp.wait_ge(G.credited, 1)

    with nc.Block() as block:
        @block.sync
        def _(sp):
            def fetch(pair_of_images, j, x_too=True):
                i = pair_of_images
                sp.wait_ge([G.stored0, G.stored1][j], past(i * 32))
                for c in range(CT if x_too else 0):
                    sp.dma_start(xr[j][:, c, :], x_dram[ds(i * 2 + j, 1), :, c, :].rearrange("b p f -> (b p) f"))\
                      .then_inc([G.x_in0, G.x_in1][j], 16)
                sp.dma_start(at[:, j, :], a_dram[ds(i * 2 + j, 1), :, :].rearrange("b p f -> (b p) f"))\
                  .then_inc([G.a_in0, G.a_in1][j], 16)
                sp.dma_start(sbad[:, j, :], bad_dram[ds(i * 2 + j, 1), :, :].rearrange("b s f -> (b s) f"))\
                  .then_inc([G.a_in0, G.a_in1][j], 16)

            def store(i, j):
                sp.wait_ge(G.conv_added, past(i * 8 + 4 * j + 4))
                for c in range(CT):
                    sp.dma_start(out_dram[ds(i * 2 + j, 1), :, c, :].rearrange("b p f -> (b p) f"), xr[j][:, c, :])\
                      .then_inc([G.stored0, G.stored1][j], 16)

            def edges(i, j):
                for c in range(3):
                    sp.dma_start(hedge[3 * c:3 * c + 3, :, :], edge_dram[ds(i * 2 + j, 3), :, c * NL:(c + NZ + 1) * NL])\
                      .then_inc(G.edge_in, 16)

            fetch(0, 0, x_too=False)
            edges(0, 0)
            with sp.Fori(0, IMAGES // 2 - 1) as i:
                fetch(i, 1)
                store(i, 0)
                edges(i, 1)
                fetch(i + 1, 0)
                store(i, 1)
                edges(i + 1, 0)
            fetch(IMAGES // 2 - 1, 1)
            store(IMAGES // 2 - 1, 0)
            edges(IMAGES // 2 - 1, 1)
            store(IMAGES // 2 - 1, 1)
            sp.wait_ge(G.stored0, past(16 * IMAGES))
            sp.wait_ge(G.stored1, past(16 * IMAGES))

        @block.gpsimd
        def _(pool):
            with pool.Fori(0, IMAGES) as img:
                for k in range(8):
                    if k < 2:
                        pool.wait_ge(G.p_used, past(img * 8))
                    else:
                        pool.wait_ge(G.p_used, past(img * 8 + k - 1))
                    pool.dma_start(ptile[:, k % 2, :, :],
                                   p_dram[ds(img, 1), :, :, 512 * k:512 * k + 512].rearrange("b q p f -> (b p) q f"))\
                        .then_inc([G.p_in0, G.p_in1][k % 2], 16)

        @block.scalar
        def _(act):
            def normalise(i, j):
                act.wait_ge([G.x_in0, G.x_in1][j], i * 32 + 32)
                sc = affine[:, ds(i * 2 + j, 1), 1, 0:1].rearrange("p b k -> p (b k)")
                bi = affine[:, ds(i * 2 + j, 1), 1, 1:2].rearrange("p b k -> p (b k)")
                nc.scalar.activation(xn[:, 1, :].rearrange("p (y x) -> p y x", x=SIDE),
                                     xr[j][:, 1, :].rearrange("p (x y) -> p y x", y=SIDE), ACT.Identity,
                                     bias=bi, scale=sc).then_inc(G.xn_ready, 1)

            def pair(i, last):
                for j in range(2):
                    if not (last and j == 1):
                        act.wait_ge(G.o_mm, i * 32 + 16 * j + 16)
                        normalise(i + j, 1 - j)
                    act.wait_ge(G.var_ready, i * 2 + j + 1)
                    nc.scalar.activation(std[:], tmp2[:], ACT.Sqrt).then_inc(G.std_ready, 1)
                    act.wait_ge(G.aff_ready, i * 2 + j + 1)
                    nc.scalar.activation(xr[j][:, 1, :], xr[j][:, 1, :], ACT.Identity,
                                         bias=aff[:, 1, 1:2], scale=aff[:, 1, 0:1]).then_inc(G.scaled, 1)

            normalise(0, 0)
            with act.Fori(0, IMAGES // 2 - 1) as i:
                pair(i, False)
            pair(IMAGES // 2 - 1, True)

        @block.tensor
        def _(pe):
            with pe.Fori(0, IMAGES // 2) as i:
                for j in range(2):
                    pe.wait_ge(G.xn_ready, i * 4 + 2 * j + 2)
                    pe.wait_ge(G.at_ready, i * 2 + j + 1)
                    pe.wait_ge(G.stat_read, past(i * 2 + j))
                    for k in range(8):
                        pe.wait_ge([G.p_in0, G.p_in1][k % 2], i * 128 + 64 * j + 16 * (k // 2) + 16)
                        for o in range(CT):
                            n = 2 * k + o
                            ps = OPS[n % 4]
                            if n < 4:
                                pe.wait_ge(G.o_evac, past(i * 32 + 16 * j))
                            else:
                                pe.wait_ge(G.o_evac, past(i * 32 + 16 * j + n - 3))
                            for c in range(CT):
                                nc.tensor.matmul(ps, at[:, j, 256 * c + 128 * o:256 * c + 128 * o + 128],
                                                 xn[:, c, 512 * k:512 * k + 512], start=(c == 0), stop=False)
                            for q in range(PAIRS):
                                nc.tensor.matmul(ps, wouta[:, q, 128 * o:128 * o + 128], ptile[:, k % 2, q, :],
                                                 start=False, stop=False)
                            mm = nc.tensor.matmul(ps.rearrange("p (y x) -> p y x", x=SIDE)[:, :, SIDE - EDGE:],
                                                  edge_neg[:, 128 * o:128 * o + 128],
                                                  sbad[:, j, 8 * EDGE * k:8 * EDGE * (k + 1)].rearrange("p (y x) -> p y x", x=EDGE),
                                                  start=False, stop=True)
                            mm.then_inc(G.o_mm, 1)
                        pe.wait_ge(G.o_mm, i * 32 + 16 * j + 2 * k + 2)
                        pe.sem_inc(G.p_used, 1)
                    for o in range(CT):
                        for z, (z0, zn) in enumerate(ZCUT):
                            n = 2 * o + z
                            pe.wait_ge(G.conv_added, past(i * 8 + 4 * j))
                            for a in range(3):
                                for c in range(3):
                                    nc.tensor.matmul(CPS[n][:, 0:zn * NL], taps[:, 3 * a + c, :],
                                                     hist[:, ds((i * 2 + j + a) * (2 * HROW) + o * HROW + (z0 + c) * NL, zn * NL)],
                                                     start=(a == 0 and c == 0), stop=False)
                            pe.wait_ge(G.edge_in, i * 96 + 48 * j + 48)
                            nc.tensor.matmul(CPS[n][:, 0:zn * NL], cross[:, o, :], hedge[:, o, z0 * NL:(z0 + zn) * NL],
                                             start=False, stop=True).then_inc(G.conv_mm, 1)
                            if n == 2:
                                pe.wait_ge(G.stat_ready, i * 2 + j + 1)
                                pe.wait_ge(G.o_evac, past(i * 32 + 16 * j + 16))
                                nc.tensor.matmul(PJ[:, 0, 0:2 * CT], group_mean[:], mv[:].rearrange("p t k -> p (t k)"),
                                                 start=True, stop=True).then_inc(G.stat_mm, 1)

        @block.vector
        def _(dve):
            steps = [0]

            def normalise(i, j):
                dve.wait_ge([G.a_in0, G.a_in1][j], i * 32 + 32)
                nc.vector.tensor_tensor(at[:, j, :], at[:, j, :], ug[:], ALU.add).then_inc(G.at_ready, 1)
                dve.wait_ge([G.x_in0, G.x_in1][j], i * 32 + 32)
                sc = affine[:, ds(i * 2 + j, 1), 0, 0:1].rearrange("p b k -> p (b k)")
                bi = affine[:, ds(i * 2 + j, 1), 0, 1:2].rearrange("p b k -> p (b k)")
                nc.vector.tensor_scalar(xn[:, 0, :].rearrange("p (y x) -> p y x", x=SIDE),
                                        xr[j][:, 0, :].rearrange("p (x y) -> p y x", y=SIDE),
                                        sc, bi, ALU.mult, ALU.add).then_inc(G.xn_ready, 1)

            def pair(i, last):
                steps[0] = 0

                def link(ins):
                    steps[0] += 1
                    ins.then_inc(G.step, 1)
                    dve.wait_ge(G.step, i * STEPS + steps[0])

                for j in range(2):
                    dve.wait_ge(G.xn_ready, i * 4 + 2 * j + 2)
                    for k in range(8):
                        for o in range(CT):
                            n = 2 * k + o
                            dve.wait_ge(G.o_mm, i * 32 + 16 * j + n + 1)
                            xv = xr[j][:, o, :].rearrange("p (x y) -> p y x", y=SIDE)[:, 8 * k:8 * k + 8, :]
                            nc.vector.scalar_tensor_tensor(xv, OPS[n % 4].rearrange("p (y x) -> p y x", x=SIDE), b_out[:, o:o + 1],
                                                           xv, ALU.add, ALU.add).then_inc(G.o_evac, 1)
                    if not (last and j == 1):
                        dve.wait_ge(G.o_mm, i * 32 + 16 * j + 16)
                        normalise(i + j, 1 - j)
                    dve.wait_ge(G.o_evac, past(i * 32 + 16 * j + 16))
                    for c in range(CT):
                        for k in range(8):
                            ins = nc.vector.bn_stats(bnst[:, c, k, :], xr[j][:, c, 512 * k:512 * k + 512])
                    link(ins)
                    dve.sem_inc(G.apart, 1)
                    nc.vector.bn_aggr(mv[:, 0, :], bnst[:, 0, :, :].rearrange("p k s -> p (k s)"))
                    link(nc.vector.bn_aggr(mv[:, 1, :], bnst[:, 1, :, :].rearrange("p k s -> p (k s)")))
                    link(nc.vector.tensor_tensor(tmp2[:], mv[:, :, 0], mv[:, :, 0], ALU.mult))
                    nc.vector.tensor_tensor(mv[:, :, 1], mv[:, :, 1], tmp2[:], ALU.add).then_inc(G.stat_ready, 1)
                    dve.wait_ge(G.stat_mm, i * 2 + j + 1)
                    link(nc.vector.tensor_copy(mv[:].rearrange("p t k -> p (t k)"), PJ[:, 0, 0:2 * CT]))
                    nc.vector.sem_inc(G.stat_read, 1)
                    link(nc.vector.tensor_tensor(tmp2[:], mv[:, :, 0], mv[:, :, 0], ALU.mult))
                    link(nc.vector.tensor_tensor(tmp2[:], mv[:, :, 1], tmp2[:], ALU.subtract))
                    nc.vector.tensor_scalar(tmp2[:], tmp2[:], 0.0, GN_EPS, ALU.max, ALU.add).then_inc(G.var_ready, 1)
                    dve.wait_ge(G.std_ready, i * 2 + j + 1)
                    link(nc.vector.reciprocal(std[:], std[:]))
                    link(nc.vector.tensor_tensor(tmp2[:], mv[:, :, 0], std[:], ALU.mult))
                    nc.vector.tensor_scalar(aff[:, :, 0], std[:], 1.0, None, ALU.add)
                    link(nc.vector.tensor_scalar(aff[:, :, 1], tmp2[:], -1.0, None, ALU.mult))
                    nc.vector.sem_inc(G.aff_ready, 1)
                    link(nc.vector.tensor_scalar(xr[j][:, 0, :], xr[j][:, 0, :], aff[:, 0, 0:1], aff[:, 0, 1:2], ALU.mult, ALU.add))
                    for o in range(CT):
                        if o == 1:
                            dve.wait_ge(G.scaled, i * 2 + j + 1)
                        for z, (z0, zn) in enumerate(ZCUT):
                            n = 2 * o + z
                            dve.wait_ge(G.conv_mm, i * 8 + 4 * j + n + 1)
                            xv = xr[j][:, o, :].rearrange("p (z l) -> p z l", l=SIDE)[:, z0:z0 + zn, 0:NL]
                            nc.vector.tensor_tensor(xv, xv, CPS[n][:, 0:zn * NL].rearrange("p (z l) -> p z l", l=NL), ALU.add)\
                                .then_inc(G.conv_added, 1)
                assert steps[0] == STEPS

            normalise(0, 0)
            with dve.Fori(0, IMAGES // 2 - 1) as i:
                pair(i, False)
            pair(IMAGES // 2 - 1, True)


def kernel(**inputs):
    import concourse.bacc as bacc
    from concourse.bass_utils import run_bass_kernel_spmd

    def lay(name, *shape):
        return np.ascontiguousarray(np.asarray(inputs[name]).reshape(*shape))

    w_qkv = np.asarray(inputs["L0_conv_w_qkv"])
    kt = w_qkv[HEADS * DK:2 * HEADS * DK].T.reshape(CHANNELS, PAIRS, 128)
    vt = w_qkv[2 * HEADS * DK:].T.reshape(CHANNELS, PAIRS, 128)
    arrays = {
        "x": np.asarray(inputs["x"]),
        "points": np.asarray(inputs["L1_conv_point_cloud"]),
        "conv_w": lay("L1_conv_weights", 1, 27),
        "conv_edge": np.ascontiguousarray(np.asarray(inputs["L1_conv_weights"]).reshape(3, 3, 3)[:, [2, 0], :].transpose(2, 0, 1).reshape(9, 2)),
        "w_q": np.ascontiguousarray(w_qkv[:HEADS * DK]),
        "w_kv_t": np.ascontiguousarray(np.concatenate([kt, vt], axis=2)),
        "w_out_t": np.ascontiguousarray(np.asarray(inputs["L0_conv_w_out"]).T),
        "b_out": np.ascontiguousarray(np.asarray(inputs["L0_conv_b_out"]).reshape(CT, 128).T),
        "rel_t": np.ascontiguousarray(np.concatenate([np.asarray(inputs["L0_conv_rel_rows"]).T,
                                                      np.asarray(inputs["L0_conv_rel_columns"]).T], axis=1)),
        "gamma": lay("L0_conv_bn_gamma", DK, 1),
        "beta": lay("L0_conv_bn_beta", DK, 1),
        **constants(),
    }
    nc = bacc.Bacc("TRN2", target_bir_lowering=False, num_devices=1)
    t = {k: nc.dram_tensor("in_" + k, a.shape, mybir.dt.from_np(a.dtype), kind="ExternalInput").ap() for k, a in arrays.items()}
    out = nc.dram_tensor("out", [IMAGES, CHANNELS, SIDE, SIDE], mybir.dt.float32, kind="ExternalOutput").ap()
    build(nc, t, out)
    r = run_bass_kernel_spmd(nc, [{"in_" + k: a for k, a in arrays.items()}], core_ids=[0])
    return r.results[0]["out"]
```
